# Optimizing a Trainium2 kernel written in Bass

```python
import numpy as np
import jax
import jax.numpy as jnp

def _softmax(x, axis=-1):
    return jax.nn.softmax(x, axis=axis)

def _gelu(x):
    return jax.nn.gelu(x, approximate=True)

def _silu(x):
    return jax.nn.silu(x)

def _sigmoid(x):
    return jax.nn.sigmoid(x)

def _layernorm(x, axis=-1, eps=1e-05):
    m = jnp.mean(x, axis=axis, keepdims=True)
    v = jnp.var(x, axis=axis, keepdims=True)
    return (x - m) / jnp.sqrt(v + eps)

def _scatter_add(tgt, idx, src, axis=0):
    return tgt.at[idx].add(src)

def _segment_sum(src, seg, n):
    return jax.ops.segment_sum(src, seg, n)
kernel_name = 'mk_lm_tower_d1_tok_ids768_r4_3c4454'

def setup_inputs(seed: int=0):
    np.random.seed(seed)
    _w = jnp.asarray

    def _rec_inputs():
        import jax
        import jax.numpy as jnp
        _rk = jax.random.key(seed)
        x = jax.random.randint(jax.random.fold_in(_rk, 1), (2, 2048), 0, 70, jnp.int32)
        return x
    x = _rec_inputs()

    def _L0_tok_setup():
        import jax, jax.numpy as jnp
        import numpy as np
        import math
        D_MODEL = 192
        BASE = D_MODEL // 3

        def positional_encoding(seq_length, d_model, dtype=jnp.float32):
            pos = jnp.arange(seq_length, dtype=dtype)[:, None]
            i_even = jnp.arange(0, d_model, 2, dtype=dtype)
            inv = jnp.exp(-(i_even / d_model) * math.log(10000.0))
            ang = pos * inv
            pe = jnp.stack([jnp.sin(ang), jnp.cos(ang)], axis=-1)
            return pe.reshape(seq_length, d_model)
        key = jax.random.key(seed)
        k_tok, k_c, k_s, k_q, k_sp = jax.random.split(key, 5)
        tokens = jax.random.randint(k_tok, (64, 512), 0, 70, dtype=jnp.int64)
        scale = 1.0
        color_W = jax.random.normal(k_c, (4, BASE), dtype=jnp.float32) * scale
        shape_W = jax.random.normal(k_s, (4, BASE), dtype=jnp.float32) * scale
        quantity_W = jax.random.normal(k_q, (4, BASE), dtype=jnp.float32) * scale
        special_W = jax.random.normal(k_sp, (6, D_MODEL), dtype=jnp.float32) * scale
        return {'tokens': tokens, 'color_W': color_W, 'shape_W': shape_W, 'quantity_W': quantity_W, 'special_W': special_W}
    _L0_tok_all = _L0_tok_setup()
    _L0_tok_in = {k: v for k, v in _L0_tok_all.items() if k in ('color_W', 'shape_W', 'quantity_W', 'special_W')}
    del _L0_tok_all

    def _L0_attn_setup():
        import jax, jax.numpy as jnp
        import numpy as np
        D_MODEL = 192
        D_INNER = 384
        N_HEADS = 24
        HEADDIM = D_INNER // N_HEADS
        D_STATE = 64
        D_MLP = 768
        K_CONV = 4
        CONV_DIM = D_INNER + 2 * D_STATE
        EPS = 1e-06

        def _rmsnorm(x, w):
            return x * jax.lax.rsqrt(jnp.mean(x * x, axis=-1, keepdims=True) + EPS) * w

        def _mixer(u, in_proj_w, conv_w, conv_b, dt_bias, A_log, D, out_proj_w):
            B, L, _ = u.shape
            zxbcdt = u @ in_proj_w
            z = zxbcdt[..., :D_INNER]
            xBC = zxbcdt[..., D_INNER:D_INNER + CONV_DIM]
            dt = jax.nn.softplus(zxbcdt[..., -N_HEADS:] + dt_bias)
            xc = jnp.transpose(xBC, (0, 2, 1))
            xc = jax.lax.conv_general_dilated(xc, conv_w[:, None, :], (1,), [(K_CONV - 1, 0)], feature_group_count=CONV_DIM, dimension_numbers=('NCL', 'OIL', 'NCL'))
            xBC = jax.nn.silu(jnp.transpose(xc, (0, 2, 1)) + conv_b)
            xh = xBC[..., :D_INNER].reshape(B, L, N_HEADS, HEADDIM)
            Bm = xBC[..., D_INNER:D_INNER + D_STATE]
            Cm = xBC[..., D_INNER + D_STATE:]
            A = -jnp.exp(A_log)
            decay = jnp.exp(dt * A)

            def step(h, t):
                dec, dtt, xt, bt, ct = t
                h = dec[..., None, None] * h + (dtt[..., None] * xt)[..., None] * bt[:, None, None, :]
                y = jnp.einsum('bhpn,bn->bhp', h, ct)
                return (h, y)
            h0 = jnp.zeros((B, N_HEADS, HEADDIM, D_STATE), u.dtype)
            xs = (jnp.moveaxis(decay, 1, 0), jnp.moveaxis(dt, 1, 0), jnp.moveaxis(xh, 1, 0), jnp.moveaxis(Bm, 1, 0), jnp.moveaxis(Cm, 1, 0))
            _, ys = jax.lax.scan(step, h0, xs)
            y = jnp.moveaxis(ys, 0, 1) + D[None, None, :, None] * xh
            y = y.reshape(B, L, D_INNER) * jax.nn.silu(z)
            return y @ out_proj_w
        key = jax.random.key(seed)
        ks = jax.random.split(key, 10)
        B, L = (2, 256)
        s = 0.02
        return {'x': jax.random.normal(ks[0], (B, L, D_MODEL), jnp.float32), 'norm1_w': jnp.ones((D_MODEL,), jnp.float32), 'in_proj_w': jax.random.normal(ks[1], (D_MODEL, 2 * D_INNER + 2 * D_STATE + N_HEADS), jnp.float32) * s, 'conv_w': jax.random.normal(ks[2], (CONV_DIM, K_CONV), jnp.float32) * s, 'conv_b': jnp.zeros((CONV_DIM,), jnp.float32), 'dt_bias': jax.random.normal(ks[3], (N_HEADS,), jnp.float32) * s, 'A_log': jnp.log(jax.random.uniform(ks[4], (N_HEADS,), jnp.float32, 1.0, 16.0)), 'D': jnp.ones((N_HEADS,), jnp.float32), 'out_proj_w': jax.random.normal(ks[5], (D_INNER, D_MODEL), jnp.float32) * s, 'norm2_w': jnp.ones((D_MODEL,), jnp.float32), 'w_gate': jax.random.normal(ks[6], (D_MODEL, D_MLP), jnp.float32) * s, 'w_up': jax.random.normal(ks[7], (D_MODEL, D_MLP), jnp.float32) * s, 'w_down': jax.random.normal(ks[8], (D_MLP, D_MODEL), jnp.float32) * s}
    _L0_attn_all = _L0_attn_setup()
    _L0_attn_in = {k: v for k, v in _L0_attn_all.items() if k in ('norm1_w', 'in_proj_w', 'conv_w', 'conv_b', 'dt_bias', 'A_log', 'D', 'out_proj_w', 'norm2_w', 'w_gate', 'w_up', 'w_down')}
    del _L0_attn_all

    def _L0_ffn_setup():
        import jax, jax.numpy as jnp
        import numpy as np
        from jax import lax
        DIM = 192
        INTER = 128
        E = 8
        G = 4
        TOPK_G = 2
        TOPK = 2
        ROUTE_SCALE = 1.0

        def _gate(x2, gate_weight, gate_bias):
            T = x2.shape[0]
            scores = jax.nn.sigmoid(x2 @ gate_weight.T)
            s = scores + gate_bias
            sv = s.reshape(T, G, E // G)
            top2, _ = lax.top_k(sv, 2)
            group_scores = top2.sum(-1)
            _, gidx = lax.top_k(group_scores, TOPK_G)
            gmask = jnp.zeros((T, G), bool).at[jnp.arange(T)[:, None], gidx].set(True)
            masked = jnp.where(gmask[:, :, None], sv, -jnp.inf).reshape(T, E)
            _, idx = lax.top_k(masked, TOPK)
            w = jnp.take_along_axis(scores, idx, axis=1)
            w = w / (w.sum(-1, keepdims=True) + 1e-06) * ROUTE_SCALE
            return (w, idx)
        key = jax.random.key(seed)
        ks = jax.random.split(key, 9)
        s = 1.0 / np.sqrt(DIM)
        si = 1.0 / np.sqrt(INTER)
        return {'x': jax.random.normal(ks[0], (4, 1024, DIM), jnp.float32), 'gate_weight': jax.random.uniform(ks[1], (E, DIM), jnp.float32, -s, s), 'gate_bias': jnp.zeros((E,), jnp.float32), 'w1': jax.random.uniform(ks[2], (E, INTER, DIM), jnp.float32, -s, s), 'w2': jax.random.uniform(ks[3], (E, DIM, INTER), jnp.float32, -si, si), 'w3': jax.random.uniform(ks[4], (E, INTER, DIM), jnp.float32, -s, s), 'sw1': jax.random.uniform(ks[5], (INTER, DIM), jnp.float32, -s, s), 'sw2': jax.random.uniform(ks[6], (DIM, INTER), jnp.float32, -si, si), 'sw3': jax.random.uniform(ks[7], (INTER, DIM), jnp.float32, -s, s)}
    _L0_ffn_all = _L0_ffn_setup()
    _L0_ffn_in = {k: v for k, v in _L0_ffn_all.items() if k in ('gate_weight', 'gate_bias', 'w1', 'w2', 'w3', 'sw1', 'sw2', 'sw3')}
    del _L0_ffn_all
    return {'x': x, 'L0_tok_color_W': _L0_tok_in['color_W'], 'L0_tok_shape_W': _L0_tok_in['shape_W'], 'L0_tok_quantity_W': _L0_tok_in['quantity_W'], 'L0_tok_special_W': _L0_tok_in['special_W'], 'L0_attn_norm1_w': _L0_attn_in['norm1_w'], 'L0_attn_in_proj_w': _L0_attn_in['in_proj_w'], 'L0_attn_conv_w': _L0_attn_in['conv_w'], 'L0_attn_conv_b': _L0_attn_in['conv_b'], 'L0_attn_dt_bias': _L0_attn_in['dt_bias'], 'L0_attn_A_log': _L0_attn_in['A_log'], 'L0_attn_D': _L0_attn_in['D'], 'L0_attn_out_proj_w': _L0_attn_in['out_proj_w'], 'L0_attn_norm2_w': _L0_attn_in['norm2_w'], 'L0_attn_w_gate': _L0_attn_in['w_gate'], 'L0_attn_w_up': _L0_attn_in['w_up'], 'L0_attn_w_down': _L0_attn_in['w_down'], 'L0_ffn_gate_weight': _L0_ffn_in['gate_weight'], 'L0_ffn_gate_bias': _L0_ffn_in['gate_bias'], 'L0_ffn_w1': _L0_ffn_in['w1'], 'L0_ffn_w2': _L0_ffn_in['w2'], 'L0_ffn_w3': _L0_ffn_in['w3'], 'L0_ffn_sw1': _L0_ffn_in['sw1'], 'L0_ffn_sw2': _L0_ffn_in['sw2'], 'L0_ffn_sw3': _L0_ffn_in['sw3']}

def reference(x, L0_tok_color_W, L0_tok_shape_W, L0_tok_quantity_W, L0_tok_special_W, L0_attn_norm1_w, L0_attn_in_proj_w, L0_attn_conv_w, L0_attn_conv_b, L0_attn_dt_bias, L0_attn_A_log, L0_attn_D, L0_attn_out_proj_w, L0_attn_norm2_w, L0_attn_w_gate, L0_attn_w_up, L0_attn_w_down, L0_ffn_gate_weight, L0_ffn_gate_bias, L0_ffn_w1, L0_ffn_w2, L0_ffn_w3, L0_ffn_sw1, L0_ffn_sw2, L0_ffn_sw3):
    import jax
    import jax.numpy as jnp

    def _L0_tok_ref(tokens, color_W, shape_W, quantity_W, special_W):
        import jax, jax.numpy as jnp
        import numpy as np
        import math
        D_MODEL = 192
        BASE = D_MODEL // 3

        def positional_encoding(seq_length, d_model, dtype=jnp.float32):
            pos = jnp.arange(seq_length, dtype=dtype)[:, None]
            i_even = jnp.arange(0, d_model, 2, dtype=dtype)
            inv = jnp.exp(-(i_even / d_model) * math.log(10000.0))
            ang = pos * inv
            pe = jnp.stack([jnp.sin(ang), jnp.cos(ang)], axis=-1)
            return pe.reshape(seq_length, d_model)
        B, S = tokens.shape
        d_model = special_W.shape[1]
        t = jnp.minimum(tokens, 63)
        color = t // 16
        shape = t % 16 // 4
        quantity = t % 4
        feat_emb = jnp.concatenate([color_W[color], shape_W[shape], quantity_W[quantity]], axis=-1)
        sp_idx = jnp.clip(tokens - 64, 0, special_W.shape[0] - 1)
        spec_emb = special_W[sp_idx]
        emb = jnp.where((tokens < 64)[..., None], feat_emb, spec_emb)
        pe = positional_encoding(S, d_model, dtype=emb.dtype)
        out = emb * jnp.asarray(math.sqrt(d_model), emb.dtype) + pe[None, :, :]
        return out

    def _L0_attn_ref(x, norm1_w, in_proj_w, conv_w, conv_b, dt_bias, A_log, D, out_proj_w, norm2_w, w_gate, w_up, w_down):
        import jax, jax.numpy as jnp
        import numpy as np
        D_MODEL = 192
        D_INNER = 384
        N_HEADS = 24
        HEADDIM = D_INNER // N_HEADS
        D_STATE = 64
        D_MLP = 768
        K_CONV = 4
        CONV_DIM = D_INNER + 2 * D_STATE
        EPS = 1e-06

        def _rmsnorm(x, w):
            return x * jax.lax.rsqrt(jnp.mean(x * x, axis=-1, keepdims=True) + EPS) * w

        def _mixer(u, in_proj_w, conv_w, conv_b, dt_bias, A_log, D, out_proj_w):
            B, L, _ = u.shape
            zxbcdt = u @ in_proj_w
            z = zxbcdt[..., :D_INNER]
            xBC = zxbcdt[..., D_INNER:D_INNER + CONV_DIM]
            dt = jax.nn.softplus(zxbcdt[..., -N_HEADS:] + dt_bias)
            xc = jnp.transpose(xBC, (0, 2, 1))
            xc = jax.lax.conv_general_dilated(xc, conv_w[:, None, :], (1,), [(K_CONV - 1, 0)], feature_group_count=CONV_DIM, dimension_numbers=('NCL', 'OIL', 'NCL'))
            xBC = jax.nn.silu(jnp.transpose(xc, (0, 2, 1)) + conv_b)
            xh = xBC[..., :D_INNER].reshape(B, L, N_HEADS, HEADDIM)
            Bm = xBC[..., D_INNER:D_INNER + D_STATE]
            Cm = xBC[..., D_INNER + D_STATE:]
            A = -jnp.exp(A_log)
            decay = jnp.exp(dt * A)

            def step(h, t):
                dec, dtt, xt, bt, ct = t
                h = dec[..., None, None] * h + (dtt[..., None] * xt)[..., None] * bt[:, None, None, :]
                y = jnp.einsum('bhpn,bn->bhp', h, ct)
                return (h, y)
            h0 = jnp.zeros((B, N_HEADS, HEADDIM, D_STATE), u.dtype)
            xs = (jnp.moveaxis(decay, 1, 0), jnp.moveaxis(dt, 1, 0), jnp.moveaxis(xh, 1, 0), jnp.moveaxis(Bm, 1, 0), jnp.moveaxis(Cm, 1, 0))
            _, ys = jax.lax.scan(step, h0, xs)
            y = jnp.moveaxis(ys, 0, 1) + D[None, None, :, None] * xh
            y = y.reshape(B, L, D_INNER) * jax.nn.silu(z)
            return y @ out_proj_w
        h = _mixer(_rmsnorm(x, norm1_w), in_proj_w, conv_w, conv_b, dt_bias, A_log, D, out_proj_w)
        v = _rmsnorm(h, norm2_w)
        m = jax.nn.silu(v @ w_gate) * (v @ w_up) @ w_down
        return h + m

    def _L0_ffn_ref(x, gate_weight, gate_bias, w1, w2, w3, sw1, sw2, sw3):
        import jax, jax.numpy as jnp
        import numpy as np
        from jax import lax
        DIM = 192
        INTER = 128
        E = 8
        G = 4
        TOPK_G = 2
        TOPK = 2
        ROUTE_SCALE = 1.0

        def _gate(x2, gate_weight, gate_bias):
            T = x2.shape[0]
            scores = jax.nn.sigmoid(x2 @ gate_weight.T)
            s = scores + gate_bias
            sv = s.reshape(T, G, E // G)
            top2, _ = lax.top_k(sv, 2)
            group_scores = top2.sum(-1)
            _, gidx = lax.top_k(group_scores, TOPK_G)
            gmask = jnp.zeros((T, G), bool).at[jnp.arange(T)[:, None], gidx].set(True)
            masked = jnp.where(gmask[:, :, None], sv, -jnp.inf).reshape(T, E)
            _, idx = lax.top_k(masked, TOPK)
            w = jnp.take_along_axis(scores, idx, axis=1)
            w = w / (w.sum(-1, keepdims=True) + 1e-06) * ROUTE_SCALE
            return (w, idx)
        B, S, D = x.shape
        x2 = x.reshape(-1, D)
        T = x2.shape[0]
        weights, indices = _gate(x2, gate_weight, gate_bias)
        cw = jnp.zeros((T, E), x.dtype).at[jnp.arange(T)[:, None], indices].add(weights)
        h1 = jnp.einsum('td,eid->tei', x2, w1)
        h3 = jnp.einsum('td,eid->tei', x2, w3)
        h = jax.nn.silu(h1) * h3
        y = jnp.einsum('tei,edi,te->td', h, w2, cw)
        z = jax.nn.silu(x2 @ sw1.T) * (x2 @ sw3.T) @ sw2.T
        return (y + z).reshape(B, S, D)
    h = _L0_tok_ref(x, L0_tok_color_W, L0_tok_shape_W, L0_tok_quantity_W, L0_tok_special_W)
    h = h + _L0_attn_ref(_layernorm(h, axis=-1), L0_attn_norm1_w, L0_attn_in_proj_w, L0_attn_conv_w, L0_attn_conv_b, L0_attn_dt_bias, L0_attn_A_log, L0_attn_D, L0_attn_out_proj_w, L0_attn_norm2_w, L0_attn_w_gate, L0_attn_w_up, L0_attn_w_down)
    h = h + _L0_ffn_ref(_layernorm(h, axis=-1), L0_ffn_gate_weight, L0_ffn_gate_bias, L0_ffn_w1, L0_ffn_w2, L0_ffn_w3, L0_ffn_sw1, L0_ffn_sw2, L0_ffn_sw3)
    return h

_drawn_inputs = setup_inputs


def setup_inputs(seed=0):
    import zlib

    import numpy as np

    out = dict(_drawn_inputs(seed))
    spreads = {'L0_attn_norm1_w': (1.0, 0.6),
     'L0_attn_conv_b': (0.0, 0.8),
     'L0_attn_D': (1.0, 0.6),
     'L0_attn_norm2_w': (1.0, 0.6),
     'L0_ffn_gate_bias': (0.0, 0.8)}
    factors = {'L0_attn_in_proj_w': 8.0,
     'L0_attn_conv_w': 8.0,
     'L0_attn_dt_bias': 8.0,
     'L0_attn_A_log': 8.0,
     'L0_attn_out_proj_w': 8.0,
     'L0_attn_w_gate': 8.0,
     'L0_attn_w_up': 8.0,
     'L0_attn_w_down': 8.0,
     'L0_ffn_gate_weight': 8.0,
     'L0_ffn_w1': 8.0,
     'L0_ffn_w2': 8.0,
     'L0_ffn_w3': 8.0,
     'L0_ffn_sw1': 7.561,
     'L0_ffn_sw2': 7.14,
     'L0_ffn_sw3': 7.232}
    for name, (base, spread) in spreads.items():
        noise = np.random.default_rng([zlib.crc32(name.encode()), seed]).standard_normal(out[name].shape)
        drawn = base * np.exp(spread * noise) if base else spread * noise
        out[name] = jnp.asarray(drawn.astype(out[name].dtype))
    for name, factor in factors.items():
        out[name] = (out[name] * factor).astype(out[name].dtype)
    return out
```

```python
from contextlib import ExitStack

import concourse.bass as bass
from concourse import mybir

ALU = mybir.AluOpType
ACT = mybir.ActivationFunctionType
AX_X = mybir.AxisListType.X
F32 = mybir.dt.float32
F16 = mybir.dt.float16
BF16 = mybir.dt.bfloat16
I32 = mybir.dt.int32

NB = 2
L = 2048
Q = 128
NC = L // Q
D = 192
DH, DT = 128, D - 128
V = 70
DI = 384
NH, HD = 24, 16
NS = 64
KC = 4
NM = (DI + 2 * NS) // 128
DM = 768
NF = DM // 128
NE, NI = 8, 128
NG, GE = 4, 2
HG = 4
NQ = NH // HG
ZD = DI + NH
COL_X = ZD
COL_G = COL_X + NM * 128
COL_U = COL_G + DM
COL_E = COL_U + DM
COL_R = COL_E + (NE + 1) * 2 * NI
COLS = COL_R + NE
HF = NH // 2
STEP = 1.0 / 16
ROUND = 1.5 * 2.0 ** 23 * STEP
DEAD = 88.0
FAR = -12000.0
EMB_SCALE = float(D) ** 0.5

PRE_V, FRONT_V, BACK_V = 3, 23, 23
PRE_P, FRONT_P, BACK_P = 1, 1, 2


def later(c):
    return not (isinstance(c, int) and c == 0)


class Steps:

    def __init__(self, per):
        self.per, self.n = per, 0

    def start(self):
        self.n = 0

    def next(self, c):
        self.n += 1
        return c * self.per + self.n


def program(nc, tokens, position, vocab_ids, table, weights, norm1, norm2, conv_w, conv_b, dt_bias, a_log,
            d_skip, w_out, w_down, w2, gate_bias, identity, lower_ones, head_rows, mask_rows, pair_rows, order8, order4, out):
    with ExitStack() as ctx:
        def sb(name, shape, dt=F32):
            return ctx.enter_context(nc.sbuf_tensor(name, shape, dt))

        def sem(name):
            return ctx.enter_context(nc.semaphore(name))

        ids = sb("ids", [V, 1])
        tab = sb("tab", [V, D])
        tab_rest = sb("tab_rest", [V, 2, D])
        tab3 = sb("tab3", [V, 3, D], BF16)
        w_raw = sb("w_raw", [128, COLS])
        wt_raw = sb("wt_raw", [128, COLS])
        w_hi = sb("w_hi", [128, COLS], F16)
        w_lo = sb("w_lo", [128, COLS], F16)
        wt_hi = sb("wt_hi", [128, COLS], F16)
        wt_lo = sb("wt_lo", [DT, COLS], F16)
        nrm = sb("nrm", [128, 4])
        cw_ = sb("cw_", [128, NM, KC])
        cb_ = sb("cb_", [128, NM])
        dtb = sb("dtb", [128, NH])
        alog = sb("alog", [128, NH])
        aexp = sb("aexp", [128, NH])
        dsk = sb("dsk", [128, NH])
        wo = sb("wo", [128, DI // 128, D])
        wd = sb("wd", [128, NF, D])
        w2t = sb("w2t", [128, NE + 1, D])
        gbias = sb("gbias", [128, NE])
        idf = sb("idf", [128, 128])
        upper = sb("upper", [128, 128])
        upper16 = sb("upper16", [128, 128], F16)
        ones16 = sb("ones16", [128, 64], F16)
        hrows = sb("hrows", [NS, HF])
        mrows = sb("mrows", [128, Q])
        prows = sb("prows", [128, Q])
        before8 = sb("before8", [128, NE, NE])
        before4 = sb("before4", [128, NG, NG])
        mhalf = sb("mhalf", [128, 2])

        tok = sb("tok", [V, NB, Q], I32)
        pos = sb("pos", [128, D])
        onehot = sb("onehot", [V, NB, Q], BF16)
        h0_next = sb("h0_next", [128, NB, D])
        stat = sb("stat", [128, NB, 6])
        mv = sb("mv", [128, NB, 2])
        var0 = sb("var0", [128, NB])
        r0 = sb("r0", [128, NB])
        un = sb("un", [128, NB, D])
        u_h = sb("u_h", [128, 2, NB * Q], F16)
        u_l = sb("u_l", [128, NB * Q], F16)

        h0 = sb("h0", [128, NB, D])
        xr = sb("xr", [128, NM, NB, KC - 1 + Q])
        xa = sb("xa", [128, NM, NB, Q])
        xs = sb("xs", [128, NM - 1, NB, Q])
        bc = sb("bc", [NS, NB, Q])
        cc = sb("cc", [NS, NB, Q])
        zs = sb("zs", [128, NB, DI])
        dx = sb("dx", [128, NB, NH])
        dn = sb("dn", [128, NB, NH])
        de = sb("de", [128, NB, NH])
        dl = sb("dl", [128, NB, NH])
        dt_ = sb("dt_", [128, NB, NH])
        ap_ = sb("ap_", [128, NB, NH])
        ag_ = sb("ag_", [128, NB, NH])
        ar_ = sb("ar_", [128, NB, NH])
        pa = sb("pa", [128, NB, 2, 32], F16)
        pb = sb("pb", [128, NB, 2, 32], F16)
        ecum = sb("ecum", [128, 2, NB, NH])
        lj = sb("lj", [128, NB, 2, 128], F16)
        ri = sb("ri", [128, NB, 2, HF, Q], F16)
        gm = sb("gm", [128, NB, Q])
        bt = sb("bt", [128, NB, NS])
        xd = sb("xd", [128, NB, DI])
        xk = sb("xk", [128, NB, DI])
        xw = sb("xw", [128, NB, DI])
        NER = 3
        er = sb("er", [128, NER, HG, Q])
        mr = sb("mr", [128, NER, HG, Q])
        t1 = sb("t1", [128, NB, DI])
        state = sb("state", [NS, NB, DI])
        y = sb("y", [128, NB, DI])

        yt = sb("yt", [128, NB, DI // 128, Q])
        hm = sb("hm", [128, NB, D])
        junk = sb("junk", [128, NB, D])
        ss = sb("ss", [128, NB])
        vv = sb("vv", [128, NB])
        rm = sb("rm", [128, NB])
        vn = sb("vn", [128, NB, D])
        v_h = sb("v_h", [128, 2, NB * Q], F16)
        v_l = sb("v_l", [128, NB * Q], F16)
        sg = sb("sg", [128, 2, NB * Q])
        gt = sb("gt", [128, NF, NB * Q])
        h1 = sb("h1", [128, NB, D])
        stat2 = sb("stat2", [128, NB, 6])
        mv2 = sb("mv2", [128, NB, 2])
        var2 = sb("var2", [128, NB])
        r2 = sb("r2", [128, NB])
        xn = sb("xn", [128, NB, D])
        x_h = sb("x_h", [128, 2, NB * Q], F16)
        x_l = sb("x_l", [128, NB * Q], F16)
        th = sb("th", [128, NB, NE])
        sc = sb("sc", [128, NB, NE])
        sv = sb("sv", [128, NB, NE])
        gs = sb("gs", [128, NB, NG])
        g_gt = sb("g_gt", [128, NB, NG, NG])
        g_ge = sb("g_ge", [128, NB, NG, NG])
        g_rank = sb("g_rank", [128, NB, NG])
        g_on = sb("g_on", [128, NB, NG, GE])
        e_gt = sb("e_gt", [128, NB, NE, NE])
        e_ge = sb("e_ge", [128, NB, NE, NE])
        e_rank = sb("e_rank", [128, NB, NE])
        e_on = sb("e_on", [128, NB, NE])
        e_w = sb("e_w", [128, NB, NE])
        e_sum = sb("e_sum", [128, NB])
        e_sum1 = sb("e_sum1", [128, NB])
        e_inv = sb("e_inv", [128, NB])
        cw = sb("cw", [128, NB, NE])
        NHH = 3
        hh = sb("hh", [128, NHH, NB * Q])
        acc = sb("acc", [128, NB, D])

        sums = nc.dram_tensor("sums", (NB, 2, 64, Q), F16, kind="Internal").ap()
        bank = [ctx.enter_context(nc.psum_tensor(f"bank{i}", [128, 512], F32)) for i in range(8)]
        p_pair = bank[0:2]
        p_out = bank[2:4]
        p_misc, p_d0, p_d1, p_y = bank[4:8]
        p_d = (p_d0, p_d1)

        in_small, in_w, in_late = sem("in_small"), sem("in_w"), sem("in_late")
        setup_v, setup_a, setup_p = sem("setup_v"), sem("setup_a"), sem("setup_p")
        w_in_hi, w_in_lo, w_rest_hi, w_rest_lo = sem("w_in_hi"), sem("w_in_lo"), sem("w_rest_hi"), sem("w_rest_lo")
        passed = sem("passed")
        tokens_in, position_in = sem("tokens_in"), sem("position_in")
        onehot_ready, emb_done, h0_ready, stat_ready, r0_ready = (sem(n) for n in (
            "onehot_ready", "emb_done", "h0_ready", "stat_ready", "r0_ready"))
        un_ready, ut_done, u_hi_ready, u_hi_tail, u_lo_ready, u_lo_tail = (sem(n) for n in (
            "un_ready", "ut_done", "u_hi_ready", "u_hi_tail", "u_lo_ready", "u_lo_tail"))
        pre_v, front_v, back_v, pre_p, front_p, back_p, back_a = (sem(n) for n in (
            "pre_v", "front_v", "back_v", "pre_p", "front_p", "back_p", "back_a"))
        h0_copied = sem("h0_copied")
        x_done = [sem(f"x_done{i}") for i in range(2)]
        z_done = [sem(f"z_done{b}") for b in range(NB)]
        xr_ready = [sem(f"xr_ready{i}") for i in range(2)]
        z_ready = [sem(f"z_ready{b}") for b in range(NB)]
        dx_ready, dn_ready, de_ready, dl_ready, pab_ready = (sem(n) for n in (
            "dx_ready", "dn_ready", "de_ready", "dl_ready", "pab_ready"))
        xa_ready, halo_kept, xs_ready, b_ready, c_ready = (sem(n) for n in (
            "xa_ready", "halo_kept", "xs_ready", "b_ready", "c_ready"))
        cum_done, ecum_ready = sem("cum_done"), sem("ecum_ready")
        g_done, gm_ready, bt_ready = sem("g_done"), sem("gm_ready"), sem("bt_ready")
        xt_done = [sem(f"xt_done{b}") for b in range(NB)]
        lj_high, lj_ready = sem("lj_high"), sem("lj_ready")
        xd_ready = [sem(f"xd_ready{b}") for b in range(NB)]
        xk_ready = [sem(f"xk_ready{b}") for b in range(NB)]
        ri_in, sums_out = sem("ri_in"), sem("sums_out")
        NR = NB * NQ
        d_done = sem("d_done")
        e_ready = sem("e_ready")
        m_ready = sem("m_ready")
        yq_done = sem("yq_done")
        xw_ready = sem("xw_ready")
        yi_done = [sem(f"yi_done{b}") for b in range(NB)]
        t1_ready = [sem(f"t1_ready{b}") for b in range(NB)]
        t1_sum = [sem(f"t1_sum{b}") for b in range(NB)]
        sn_done = [sem(f"sn_done{b}") for b in range(NB)]
        s_decayed = [sem(f"s_decayed{b}") for b in range(NB)]
        s_ready = [sem(f"s_ready{b}") for b in range(NB)]
        y_sum = [sem(f"y_sum{b}") for b in range(NB)]
        y_ready = [sem(f"y_ready{b}") for b in range(NB)]
        yt_done = [sem(f"yt_done{b}") for b in range(NB)]
        yt_ready = [sem(f"yt_ready{b}") for b in range(NB)]
        m_out, hm_ready, rm_ready, vn_ready, vt_done = (sem(n) for n in (
            "m_out", "hm_ready", "rm_ready", "vn_ready", "vt_done"))
        v_hi_ready, v_hi_tail, v_lo_ready, v_lo_tail = (sem(n) for n in (
            "v_hi_ready", "v_hi_tail", "v_lo_ready", "v_lo_tail"))
        gu_done, sg_ready, gt_ready = sem("gu_done"), sem("sg_ready"), sem("gt_ready")
        mlp_done, h1_ready, stat2_ready, r2_ready, xn_ready, xnt_done = (sem(n) for n in (
            "mlp_done", "h1_ready", "stat2_ready", "r2_ready", "xn_ready", "xnt_done"))
        x_hi_ready, x_hi_tail, x_lo_ready, x_lo_tail = (sem(n) for n in (
            "x_hi_ready", "x_hi_tail", "x_lo_ready", "x_lo_tail"))
        router_done, th_ready, cw_ready = sem("router_done"), sem("th_ready"), sem("cw_ready")
        NX = NE + 1
        h13_done, sx_ready, hh_ready, ex_done, acc_done = (sem(n) for n in (
            "h13_done", "sx_ready", "hh_ready", "ex_done", "acc_done"))
        out_written = sem("out_written")

        def settle(eng):
            eng.sem_inc(passed, 1)

        block = ctx.enter_context(nc.Block())

        def run(eng, body):
            body(0, None, None)
            body(1, 0, None)
            body(2, 1, 0)
            with eng.Fori(1, NC - 2) as i:
                body(i + 2, i + 1, i)
            body(None, NC - 1, NC - 2)
            body(None, None, NC - 1)

        @block.sync
        def _(sp):
            small = [(ids[:], vocab_ids), (tab[:], table), (idf[:], identity), (upper[:], lower_ones),
                     (nrm[:, 0:1], norm1[0:DH, :]), (nrm[0:DT, 1:2], norm1[DH:D, :]), (nrm[DT:128, 1:2], norm1[DH:D, :]),
                     (nrm[:, 2:3], norm2[0:DH, :]), (nrm[0:DT, 3:4], norm2[DH:D, :]), (nrm[DT:128, 3:4], norm2[DH:D, :]),
                     (cw_[:], conv_w), (cb_[:], conv_b),
                     (dtb[:], dt_bias.partition_broadcast(128)), (alog[:], a_log.partition_broadcast(128)),
                     (dsk[:], d_skip.partition_broadcast(128)), (gbias[:], gate_bias.partition_broadcast(128)),
                     (hrows[:], head_rows), (mrows[64:128, :], mask_rows), (prows[64:128, :], pair_rows),
                     (before8[:], order8.partition_broadcast(128)),
                     (before4[:], order4.partition_broadcast(128))]
            assert len(small) == N_SMALL
            for dst, src in small:
                sp.dma_start(dst, src).then_inc(in_small, 16)
            for part in (slice(0, COL_G),):
                sp.dma_start(w_raw[:, part], weights[0:DH, part]).then_inc(in_w, 16)
                sp.dma_start(wt_raw[0:DT, part], weights[DH:D, part]).then_inc(in_w, 16)
                sp.dma_start(wt_raw[DT:128, part], weights[DH:D, part]).then_inc(in_w, 16)

            def load(c):
                if later(c):
                    sp.wait_ge(onehot_ready, c)
                settle(sp)
                sp.dma_start(tok[:], tokens[:, bass.ds(c * Q, Q)].partition_broadcast(V)).then_inc(tokens_in, 16)
                if later(c):
                    sp.wait_ge(h0_ready, c)
                settle(sp)
                sp.dma_start(pos[:], position[bass.ds(c * Q, Q), :]).then_inc(position_in, 16)

            def spread(c):
                sp.wait_ge(lj_ready, c + 1)
                settle(sp)
                sp.dma_start(sums.rearrange("b f r i -> r b f i"), lj[0:64]).then_inc(sums_out, 16)
                sp.wait_ge(sums_out, c * 16 + 16)
                settle(sp)
                if later(c):
                    sp.wait_ge(d_done, c * NR)
                settle(sp)
                for b in range(NB):
                    for f in range(2):
                        sp.dma_start(ri[HF:HF + 4, b, f, :, :],
                                     sums[b, f].rearrange("(g r) i -> g r i", g=4)[:, 0:HF, :]).then_inc(ri_in, 16)

            def store(c):
                sp.wait_ge(acc_done, c * NX + NX)
                settle(sp)
                sp.dma_start(out[:, bass.ds(c * Q, Q), :].rearrange("b t d -> t b d"), acc[:]).then_inc(out_written, 16)

            def body(p, f, b):
                if f is not None:
                    spread(f)
                if b is not None:
                    store(b)
                if p is not None and not isinstance(p, int):
                    load(p + 1)
                elif p is not None and p + 1 < NC:
                    load(p + 1)

            load(0)
            rest = slice(COL_G, COLS)
            sp.dma_start(w_raw[:, rest], weights[0:DH, rest]).then_inc(in_late, 16)
            sp.dma_start(wt_raw[0:DT, rest], weights[DH:D, rest]).then_inc(in_late, 16)
            sp.dma_start(wt_raw[DT:128, rest], weights[DH:D, rest]).then_inc(in_late, 16)
            sp.dma_start(wo[:], w_out).then_inc(in_late, 16)
            sp.dma_start(wd[:], w_down).then_inc(in_late, 16)
            sp.dma_start(w2t[:], w2).then_inc(in_late, 16)
            body(0, None, None)
            body(1, 0, None)
            body(2, 1, 0)
            with sp.Fori(1, NC - 3) as i:
                body(i + 2, i + 1, i)
            body(NC - 1, NC - 2, NC - 3)
            body(None, NC - 1, NC - 2)
            body(None, None, NC - 1)
            sp.wait_ge(out_written, 16 * NC)

        @block.gpsimd
        def _(pool):
            pool.memset(mhalf[:], -0.5).then_inc(setup_p, 1)
            pool.memset(state[:], 0.0).then_inc(setup_p, 1)
            pool.memset(xr[:, :, :, 0:KC - 1], 0.0).then_inc(setup_p, 1)
            pool.memset(ones16[:], 1.0).then_inc(setup_p, 1)
            pool.wait_ge(setup_p, 4)

            def rsqrt(c, ready, src, scale, bias, mid, dst, chain, steps, k, done):
                pool.wait_ge(ready, c + 1)
                settle(pool)
                pool.tensor_scalar(mid, src, scale, bias, ALU.mult, ALU.add).then_inc(chain, 1)
                pool.wait_ge(chain, c * steps + k)
                pool.tensor_tensor(dst, mid, mhalf[:], ALU.pow).then_inc(done, 1)

            def pre(c):
                rsqrt(c, stat_ready, mv[:, :, 1], 1.0 + 1e-6, 1e-11, var0[:], r0[:], pre_p, PRE_P, 1, r0_ready)

            def keep(c):
                if later(c):
                    pool.wait_ge(hm_ready, c)
                pool.wait_ge(h0_ready, c + 1)
                settle(pool)
                pool.tensor_copy(h0[:], h0_next[:]).then_inc(h0_copied, 1)

            def halo(c):
                pool.wait_ge(xa_ready, c + 1)
                settle(pool)
                pool.tensor_copy(xr[:, :, :, 0:KC - 1], xr[:, :, :, Q:Q + KC - 1]).then_inc(halo_kept, 1)

            def scan(c, b):
                pool.wait_ge(ecum_ready, c + 1)
                pool.wait_ge(yi_done[b], c + 1)
                if later(c):
                    pool.wait_ge(s_ready[b], c)
                sv_ = state[:, b, :].rearrange("n (h p) -> n h p", h=NH)
                pool.tensor_tensor(sv_, sv_, ecum[0:NS, 1, b, :].unsqueeze(2).to_broadcast([NS, NH, HD]), ALU.mult)\
                    .then_inc(s_decayed[b], 1)
                if later(c):
                    pool.wait_ge(sn_done[b], c)
                for q in range(NQ):
                    r = b * NQ + q
                    pool.wait_ge(e_ready, c * NR + r + 1)
                    if q == 0:
                        pool.wait_ge(xd_ready[b], c + 1)
                    o = slice(q * HG * HD, (q + 1) * HG * HD)
                    pool.tensor_tensor(xw[:, b, o].rearrange("p (h d) -> p h d", h=HG),
                                       xd[:, b, o].rearrange("p (h d) -> p h d", h=HG),
                                       er[:, r % NER, :, Q - 1:Q].to_broadcast([128, HG, HD]), ALU.mult)\
                        .then_inc(xw_ready, 1)
                pool.wait_ge(t1_ready[b], c + 1)
                pool.wait_ge(xk_ready[b], c + 1)
                pool.tensor_tensor(t1[:, b, :], t1[:, b, :], xk[:, b, :], ALU.add).then_inc(t1_sum[b], 1)

            def gate(c, b):
                pool.wait_ge(y_sum[b], c + 1)
                pool.wait_ge(z_ready[b], c + 1)
                pool.tensor_tensor(y[:, b, :], y[:, b, :], zs[:, b, :], ALU.mult).then_inc(y_ready[b], 1)

            def body(p, f, b):
                if b is not None:
                    pool.wait_ge(back_a, b * 2 + 2)
                    settle(pool)
                    pool.tensor_scalar(vv[:], ss[:], 1.0 / D, 1e-6, ALU.mult, ALU.add).then_inc(back_p, 1)
                    pool.wait_ge(back_p, b + 1)
                    pool.tensor_tensor(rm[:], vv[:], mhalf[:], ALU.pow).then_inc(rm_ready, 1)
                if f is not None:
                    keep(f)
                    halo(f)
                if b is not None:
                    rsqrt(b, stat2_ready, mv2[:, :, 1], 1.0, 1e-5, var2[:], r2[:], front_p, 1, 1, r2_ready)
                if f is not None:
                    scan(f, 0)
                    gate(f, 0)
                    scan(f, 1)
                    gate(f, 1)
                if p is not None:
                    pre(p)

            run(pool, body)

        @block.scalar
        def _(act):
            act.wait_ge(in_small, 16 * N_SMALL)
            act.activation(aexp[:], alog[:], ACT.Exp).then_inc(setup_a, 1)
            act.wait_ge(in_w, 48)
            act.activation(w_hi[:, 0:COL_G], w_raw[:, 0:COL_G], ACT.Copy, scale=nrm[:, 0:1]).then_inc(w_in_hi, 1)
            act.activation(wt_hi[:, 0:COL_G], wt_raw[:, 0:COL_G], ACT.Copy, scale=nrm[:, 1:2]).then_inc(w_in_hi, 1)

            def setup_rest():
                act.wait_ge(in_late, 96)
                act.activation(w_hi[:, COL_G:COL_E], w_raw[:, COL_G:COL_E], ACT.Copy, scale=nrm[:, 2:3])\
                    .then_inc(w_rest_hi, 1)
                act.activation(wt_hi[:, COL_G:COL_E], wt_raw[:, COL_G:COL_E], ACT.Copy, scale=nrm[:, 3:4])\
                    .then_inc(w_rest_hi, 1)
                act.copy(w_hi[:, COL_E:COLS], w_raw[:, COL_E:COLS]).then_inc(w_rest_hi, 1)
                act.copy(wt_hi[:, COL_E:COLS], wt_raw[:, COL_E:COLS]).then_inc(w_rest_hi, 1)

            def split(c, done, src, hi, taken, head, tail):
                act.wait_ge(done, c + 1)
                if later(c):
                    act.wait_ge(taken[0], c * taken[1])
                act.copy(hi[:, 0, :], src[:, 0:NB * Q]).then_inc(head, 1)
                act.copy(hi[0:DT, 1, :], src[0:DT, NB * Q:2 * NB * Q]).then_inc(tail, 1)

            def convolved_in(c):
                for i in range(2):
                    act.wait_ge(x_done[i], c + 1)
                    if later(c):
                        act.wait_ge(xa_ready, c)
                    if later(c):
                        act.wait_ge(halo_kept, c)
                    act.copy(xr[:, 2 * i:2 * i + 2, :, KC - 1:KC - 1 + Q],
                             p_d[i][:].rearrange("p (m b t) -> p m b t", m=2, b=NB)).then_inc(xr_ready[i], 1)

            def gates(c):
                for b, p in ((0, p_y), (1, p_misc)):
                    act.wait_ge(z_done[b], c + 1)
                    if later(c):
                        act.wait_ge(y_ready[b], c)
                    act.activation(zs[:, b, :], p[:, 0:DI], ACT.Silu).then_inc(z_ready[b], 1)

            def convolved_out(c):
                act.wait_ge(xa_ready, c + 1)
                if later(c):
                    act.wait_ge(xt_done[1], c)
                act.activation(xs[:], xa[:, 0:NM - 1], ACT.Silu).then_inc(xs_ready, 1)
                if later(c):
                    act.wait_ge(g_done, c)
                if later(c):
                    act.wait_ge(yi_done[1], c)
                act.activation(bc[:], xa[0:NS, NM - 1], ACT.Silu).then_inc(b_ready, 1)
                act.activation(cc[:], xa[NS:128, NM - 1], ACT.Silu).then_inc(c_ready, 1)

            def softplus(c):
                act.wait_ge(dn_ready, c + 1)
                if later(c):
                    act.wait_ge(dl_ready, c)
                act.activation(de[:], dn[:], ACT.Exp).then_inc(de_ready, 1)
                act.wait_ge(de_ready, c + 1)
                if later(c):
                    act.wait_ge(pab_ready, c)
                act.activation(dl[:], de[:], ACT.Ln, bias=1.0).then_inc(dl_ready, 1)

            def decays(c):
                act.wait_ge(cum_done, c + 1)
                if later(c):
                    act.wait_ge(s_decayed[1], c)
                if later(c):
                    act.wait_ge(t1_ready[1], c)
                act.activation(ecum[:], p_misc[:, 256:256 + 2 * NB * NH].rearrange("p (k b h) -> p k b h", k=2, b=NB),
                               ACT.Exp, scale=-1.0).then_inc(ecum_ready, 1)
                act.wait_ge(g_done, c + 1)
                if later(c):
                    act.wait_ge(sn_done[1], c)
                act.copy(bt[:], p_y[:, 256:256 + NB * NS].rearrange("p (b n) -> p b n", b=NB)).then_inc(bt_ready, 1)

            def scan(c, b):
                for q in range(NQ):
                    r = b * NQ + q
                    act.wait_ge(d_done, c * NR + r + 1)
                    if later(c) or r - NER + 1 > 0:
                        act.wait_ge(m_ready, c * NR + r - NER + 1)
                    if later(c) or r - NER + 1 > 0:
                        act.wait_ge(xw_ready, c * NR + r - NER + 1)
                    act.activation(er[:, r % NER], p_d[r % 2][:].rearrange("p (h i) -> p h i", h=HG), ACT.Exp)\
                        .then_inc(e_ready, 1)

            def mixed(c):
                for b in range(NB):
                    act.wait_ge(yt_done[b], c + 1)
                    if later(c):
                        act.wait_ge(m_out, c)
                    act.copy(yt[:, b], p_out[b][:, 0:DI].rearrange("p (k t) -> p k t", t=Q)).then_inc(yt_ready[b], 1)
                act.wait_ge(m_out, c + 1)
                if later(c):
                    act.wait_ge(rm_ready, c)
                for b in range(NB):
                    if later(c):
                        act.wait_ge(back_a, c * 2)
                    act.activation(junk[:, b, :], p_out[0][:, b * D:(b + 1) * D], ACT.Square, accum_out=ss[:, b:b + 1])\
                        .then_inc(back_a, 1)

            def swiglu(c):
                for f in range(NF):
                    act.wait_ge(gu_done, c * NF + f + 1)
                    if f >= 2:
                        act.wait_ge(gt_ready, c * NF + f - 1)
                    else:
                        if later(c):
                            act.wait_ge(hh_ready, c * NX)
                    act.activation(sg[:, f % 2, :], p_pair[f % 2][:, 0:NB * Q], ACT.Silu).then_inc(sg_ready, 1)

            def route(c):
                act.wait_ge(router_done, c + 1)
                if later(c):
                    act.wait_ge(cw_ready, c)
                act.activation(th[:], p_out[0][:, 0:NB * NE].rearrange("p (b e) -> p b e", b=NB), ACT.Tanh, scale=0.5)\
                    .then_inc(th_ready, 1)

            def pre_split(c):
                split(c, ut_done, p_misc, u_h, (z_done[1], 1), u_hi_ready, u_hi_tail)

            def experts(c, p):
                for e in range(NX):
                    act.wait_ge(h13_done, c * NX + e + 1)
                    if e >= 2:
                        act.wait_ge(hh_ready, c * NX + e - 1)
                    else:
                        act.wait_ge(gt_ready, c * NF + NF - 1 + e)
                    act.activation(sg[:, e % 2, :], p_pair[e % 2][:, 0:NB * Q], ACT.Silu).then_inc(sx_ready, 1)
                    if e == 1:
                        route(c)
                    if e == 6 and p is not None:
                        pre_split(p)

            def body(p, f, b):
                if b is not None:
                    mixed(b)
                if f is not None:
                    convolved_in(f)
                    gates(f)
                if b is not None:
                    split(b, vt_done, p_out[1], v_h, (gu_done, NF), v_hi_ready, v_hi_tail)
                if f is not None:
                    convolved_out(f)
                if b is not None:
                    swiglu(b)
                if not later(f):
                    setup_rest()
                if f is not None:
                    softplus(f)
                    decays(f)
                    scan(f, 0)
                if b is not None:
                    split(b, xnt_done, p_out[1], x_h, (h13_done, NX), x_hi_ready, x_hi_tail)
                if f is not None:
                    scan(f, 1)
                if b is not None:
                    experts(b, p)
                elif p is not None:
                    pre_split(p)

            run(act, body)

        @block.vector
        def _(ve):
            pre_steps, front_steps, back_steps = Steps(PRE_V), Steps(FRONT_V), Steps(BACK_V)

            def setup():
                ve.wait_ge(in_small, 16 * N_SMALL)
                setup_steps = Steps(0)
                ve.tensor_scalar(tab_rest[:, 0, :], tab[:], EMB_SCALE, None, ALU.mult).then_inc(setup_v, 1)
                ve.wait_ge(setup_v, setup_steps.next(0))
                ve.tensor_copy(tab3[:, 0, :], tab_rest[:, 0, :]).then_inc(setup_v, 1)
                ve.wait_ge(setup_v, setup_steps.next(0))
                ve.tensor_tensor(tab_rest[:, 1, :], tab_rest[:, 0, :], tab3[:, 0, :], ALU.subtract).then_inc(setup_v, 1)
                ve.wait_ge(setup_v, setup_steps.next(0))
                ve.tensor_copy(tab3[:, 1, :], tab_rest[:, 1, :]).then_inc(setup_v, 1)
                ve.wait_ge(setup_v, setup_steps.next(0))
                ve.tensor_tensor(tab3[:, 2, :], tab_rest[:, 1, :], tab3[:, 1, :], ALU.subtract).then_inc(setup_v, 1)
                ve.wait_ge(setup_v, setup_steps.next(0))
                ve.tensor_copy(upper16[:], upper[:]).then_inc(setup_v, 1)
                ve.wait_ge(setup_v, setup_steps.next(0))
                ve.memset(pa[:], 0.0).then_inc(setup_v, 1)
                ve.wait_ge(setup_v, setup_steps.next(0))
                ve.memset(pb[:], 0.0).then_inc(setup_v, 1)
                ve.wait_ge(setup_v, setup_steps.next(0))
                ve.memset(pa[0:1, :, :, HF:HF + 4], -1.0).then_inc(setup_v, 1)
                ve.wait_ge(setup_v, setup_steps.next(0))
                for b in range(NB):
                    for f in range(2):
                        ve.tensor_copy(ri[0:64, b, f], hrows[:].unsqueeze(2).to_broadcast([64, HF, Q])).then_inc(setup_v, 1)
                        ve.wait_ge(setup_v, setup_steps.next(0))
                        ve.tensor_copy(ri[64:128, b, f],
                                       mrows[64:128, :].unsqueeze(1).to_broadcast([64, HF, Q])).then_inc(setup_v, 1)
                        ve.wait_ge(setup_v, setup_steps.next(0))
                        ve.tensor_copy(lj[64:128, b, f], prows[64:128, :]).then_inc(setup_v, 1)
                        ve.wait_ge(setup_v, setup_steps.next(0))
                ve.wait_ge(in_w, 48)
                ve.wait_ge(w_in_hi, 2)
                ve.scalar_tensor_tensor(w_lo[:, 0:COL_G], w_raw[:, 0:COL_G], nrm[:, 0:1], w_hi[:, 0:COL_G],
                                        ALU.mult, ALU.subtract).then_inc(w_in_lo, 1)
                ve.scalar_tensor_tensor(wt_lo[:, 0:COL_G], wt_raw[0:DT, 0:COL_G], nrm[0:DT, 1:2], wt_hi[0:DT, 0:COL_G],
                                        ALU.mult, ALU.subtract).then_inc(w_in_lo, 1)

            def setup_rest():
                ve.wait_ge(in_late, 96)
                ve.wait_ge(w_rest_hi, 4)
                m, x = slice(COL_G, COL_E), slice(COL_E, COLS)
                ve.scalar_tensor_tensor(w_lo[:, m], w_raw[:, m], nrm[:, 2:3], w_hi[:, m],
                                        ALU.mult, ALU.subtract).then_inc(w_rest_lo, 1)
                ve.scalar_tensor_tensor(wt_lo[:, m], wt_raw[0:DT, m], nrm[0:DT, 3:4], wt_hi[0:DT, m],
                                        ALU.mult, ALU.subtract).then_inc(w_rest_lo, 1)
                ve.tensor_tensor(w_lo[:, x], w_raw[:, x], w_hi[:, x], ALU.subtract).then_inc(w_rest_lo, 1)
                ve.tensor_tensor(wt_lo[:, x], wt_raw[0:DT, x], wt_hi[0:DT, x], ALU.subtract).then_inc(w_rest_lo, 1)

            def split(c, head, tail, src, hi, lo, lo_ready, lo_tail):
                ve.wait_ge(head, c + 1)
                ve.wait_ge(tail, c + 1)
                ve.tensor_tensor(lo[:], src[:, 0:NB * Q], hi[:, 0, :], ALU.subtract).then_inc(lo_ready, 1)
                ve.tensor_tensor(hi[DT:128, 1, :], src[0:DT, NB * Q:2 * NB * Q], hi[0:DT, 1, :], ALU.subtract)\
                    .then_inc(lo_tail, 1)

            def pre_onehot(c):
                ve.wait_ge(tokens_in, c * 16 + 16)
                if later(c):
                    ve.wait_ge(emb_done, c)
                ve.tensor_scalar(onehot[:], tok[:], float(V - 1), ids[:, 0:1], ALU.min, ALU.is_equal)\
                    .then_inc(onehot_ready, 1)

            def pre_norm(c):
                ve.wait_ge(emb_done, c + 1)
                ve.wait_ge(position_in, c * 16 + 16)
                if later(c):
                    ve.wait_ge(h0_copied, c)
                ve.tensor_tensor(h0_next[:], p_misc[:, 0:NB * D].rearrange("p (b d) -> p b d", b=NB),
                                 pos[:].unsqueeze(1).to_broadcast([128, NB, D]), ALU.add).then_inc(h0_ready, 1)
                ve.wait_ge(h0_ready, c + 1)
                pre_steps.start()
                ve.bn_stats(stat[:, 0, :], h0_next[:, 0, :]).then_inc(pre_v, 1)
                ve.wait_ge(pre_v, pre_steps.next(c))
                ve.bn_stats(stat[:, 1, :], h0_next[:, 1, :]).then_inc(pre_v, 1)
                ve.wait_ge(pre_v, pre_steps.next(c))
                settle(ve)
                ve.bn_aggr(mv[:, 0, :], stat[:, 0, :]).then_inc(pre_v, 1)
                ve.wait_ge(pre_v, pre_steps.next(c))
                assert pre_steps.n == PRE_V
                settle(ve)
                ve.bn_aggr(mv[:, 1, :], stat[:, 1, :]).then_inc(stat_ready, 1)

            def pre_apply(c):
                ve.wait_ge(r0_ready, c + 1)
                if later(c):
                    ve.wait_ge(ut_done, c)
                ve.tensor_scalar(un[:, 0, :], h0_next[:, 0, :], mv[:, 0, 0:1], r0[:, 0:1], ALU.subtract, ALU.mult)
                ve.tensor_scalar(un[:, 1, :], h0_next[:, 1, :], mv[:, 1, 0:1], r0[:, 1:2], ALU.subtract, ALU.mult)\
                    .then_inc(un_ready, 1)

            def pre_split(c):
                split(c, u_hi_ready, u_hi_tail, p_misc, u_h, u_l, u_lo_ready, u_lo_tail)

            def convolve(c):
                front_steps.start()
                if later(c):
                    ve.wait_ge(xs_ready, c)
                if later(c):
                    ve.wait_ge(b_ready, c)
                if later(c):
                    ve.wait_ge(c_ready, c)
                for m in range(NM):
                    if m % 2 == 0:
                        ve.wait_ge(xr_ready[m // 2], c + 1)
                        if later(c):
                            ve.wait_ge(halo_kept, c)
                    ve.tensor_scalar(xa[:, m], xr[:, m, :, 0:Q], cw_[:, m, 0:1], cb_[:, m:m + 1],
                                     ALU.mult, ALU.add).then_inc(front_v, 1)
                    ve.wait_ge(front_v, front_steps.next(c))
                    for k in range(1, KC):
                        ins = ve.scalar_tensor_tensor(xa[:, m], xr[:, m, :, k:k + Q], cw_[:, m, k:k + 1], xa[:, m],
                                                      ALU.mult, ALU.add)
                        if k < KC - 1:
                            ins.then_inc(front_v, 1)
                            ve.wait_ge(front_v, front_steps.next(c))
                        elif m < NM - 1:
                            ins.then_inc(front_v, 1)
                            ve.wait_ge(front_v, front_steps.next(c))
                        else:
                            ins.then_inc(xa_ready, 1)

            def steps_dt(c):
                for b, p in ((0, p_y), (1, p_misc)):
                    ve.wait_ge(z_ready[b], c + 1)
                    ins = ve.tensor_tensor(dx[:, b, :], p[:, DI:ZD], dtb[:], ALU.add)
                    if b == 0:
                        ins.then_inc(front_v, 1)
                        ve.wait_ge(front_v, front_steps.next(c))
                    else:
                        ins.then_inc(dx_ready, 1)
                ve.wait_ge(dx_ready, c + 1)
                ve.scalar_tensor_tensor(dn[:], dx[:], -1.0, dx[:], ALU.mult, ALU.min).then_inc(dn_ready, 1)

            def halves(t):
                return t[:].rearrange("p b (f h) -> p b f h", f=2)

            def steps_decay(c):
                ve.wait_ge(dl_ready, c + 1)
                if later(c):
                    ve.wait_ge(cum_done, c)
                ve.scalar_tensor_tensor(dt_[:], dx[:], 0.0, dl[:], ALU.max, ALU.add).then_inc(front_v, 1)
                ve.wait_ge(front_v, front_steps.next(c))
                ve.tensor_tensor(ap_[:], dt_[:], aexp[:].unsqueeze(1).to_broadcast([128, NB, NH]), ALU.mult).then_inc(front_v, 1)
                ve.wait_ge(front_v, front_steps.next(c))
                ve.tensor_scalar(ag_[:], ap_[:], DEAD, ROUND, ALU.min, ALU.add).then_inc(front_v, 1)
                ve.wait_ge(front_v, front_steps.next(c))
                ve.tensor_scalar(pa[:, :, :, 0:HF], halves(ag_), ROUND, None, ALU.subtract).then_inc(front_v, 1)
                ve.wait_ge(front_v, front_steps.next(c))
                ve.tensor_scalar(ag_[:], ap_[:], DEAD, None, ALU.min).then_inc(front_v, 1)
                ve.wait_ge(front_v, front_steps.next(c))
                ve.tensor_tensor(halves(ar_), halves(ag_), pa[:, :, :, 0:HF], ALU.subtract).then_inc(front_v, 1)
                ve.wait_ge(front_v, front_steps.next(c))
                ve.tensor_copy(pa[:, :, :, 16:16 + HF], halves(ar_)).then_inc(front_v, 1)
                ve.wait_ge(front_v, front_steps.next(c))
                ve.tensor_tensor(pb[:, :, :, 16:16 + HF], halves(ar_), pa[:, :, :, 16:16 + HF], ALU.subtract).then_inc(pab_ready, 1)
                assert front_steps.n == FRONT_V, front_steps.n

            def masked_g(c):
                ve.wait_ge(bt_ready, c + 1)
                ve.tensor_tensor(gm[:], p_y[:, 0:NB * Q].rearrange("p (b i) -> p b i", b=NB),
                                 upper[:].unsqueeze(1).to_broadcast([128, NB, Q]), ALU.mult).then_inc(gm_ready, 1)

            def operands(c):
                ve.wait_ge(ecum_ready, c + 1)
                if later(c):
                    ve.wait_ge(d_done, c * NR)
                if later(c):
                    ve.wait_ge(sums_out, c * 16)
                part = [p_misc[32 * f:32 * (f + 1), 0:NB * Q].rearrange("p (b i) -> p b i", b=NB) for f in range(2)]
                ve.tensor_copy(lj[0:32, :, 0, :], part[0])
                ve.tensor_copy(lj[0:32, :, 1, :], part[1]).then_inc(lj_high, 1)
                ve.wait_ge(lj_high, c + 1)
                ve.tensor_tensor(lj[32:64, :, 0, :], part[0], lj[0:32, :, 0, :], ALU.subtract)
                ve.tensor_tensor(lj[32:64, :, 1, :], part[1], lj[0:32, :, 1, :], ALU.subtract).then_inc(lj_ready, 1)

            def scaled_x(c, b):
                ve.wait_ge(xt_done[b], c + 1)
                x3 = p_d[b][:, 0:DI].rearrange("p (h d) -> p h d", h=NH)
                if later(c) or (b + 1) * NQ - NR > 0:
                    ve.wait_ge(xw_ready, c * NR + (b + 1) * NQ - NR)
                ve.tensor_tensor(xd[:, b, :].rearrange("p (h d) -> p h d", h=NH), x3,
                                 dt_[:, b, :].unsqueeze(2).to_broadcast([128, NH, HD]), ALU.mult).then_inc(xd_ready[b], 1)
                if later(c):
                    ve.wait_ge(t1_sum[b], c)
                ve.tensor_tensor(xk[:, b, :].rearrange("p (h d) -> p h d", h=NH), x3,
                                 dsk[:].unsqueeze(2).to_broadcast([128, NH, HD]), ALU.mult).then_inc(xk_ready[b], 1)

            def scan(c, b):
                ve.wait_ge(yi_done[b], c + 1)
                ve.wait_ge(ecum_ready, c + 1)
                if later(c):
                    ve.wait_ge(y_sum[b], c)
                ve.tensor_tensor(t1[:, b, :].rearrange("p (h d) -> p h d", h=NH),
                                 p_misc[:, 0:DI].rearrange("p (h d) -> p h d", h=NH),
                                 ecum[:, 0, b, :].unsqueeze(2).to_broadcast([128, NH, HD]), ALU.mult).then_inc(t1_ready[b], 1)
                for q in range(NQ):
                    r = b * NQ + q
                    ve.wait_ge(e_ready, c * NR + r + 1)
                    if q == 0:
                        ve.wait_ge(gm_ready, c + 1)
                    if later(c) or r - NER + 1 > 0:
                        ve.wait_ge(yq_done, c * NR + r - NER + 1)
                    ve.scalar_tensor_tensor(mr[:, r % NER], er[:, r % NER], 1.0,
                                            gm[:, b, :].unsqueeze(1).to_broadcast([128, HG, Q]), ALU.min, ALU.mult)\
                        .then_inc(m_ready, 1)
                ve.wait_ge(sn_done[b], c + 1)
                ve.wait_ge(s_decayed[b], c + 1)
                ve.tensor_tensor(state[:, b, :], state[:, b, :], p_misc[0:NS, 0:DI], ALU.add).then_inc(s_ready[b], 1)
                ve.wait_ge(t1_sum[b], c + 1)
                ve.wait_ge(yq_done, c * NR + (b + 1) * NQ)
                if later(c):
                    ve.wait_ge(yt_done[b], c)
                ve.tensor_tensor(y[:, b, :], p_y[:, 0:DI], t1[:, b, :], ALU.add).then_inc(y_sum[b], 1)

            def mixed(c):
                ve.wait_ge(rm_ready, c + 1)
                if later(c):
                    ve.wait_ge(vt_done, c)
                for b in range(NB):
                    ins = ve.tensor_scalar(vn[:, b, :], p_out[0][:, b * D:(b + 1) * D], rm[:, b:b + 1], None, ALU.mult)
                ins.then_inc(vn_ready, 1)
                ve.wait_ge(h0_copied, c + 1)
                if later(c):
                    ve.wait_ge(h1_ready, c)
                ve.tensor_tensor(hm[:], p_out[0][:, 0:NB * D].rearrange("p (b d) -> p b d", b=NB), h0[:], ALU.add)\
                    .then_inc(hm_ready, 1)

            def swiglu(c):
                for f in range(NF):
                    ve.wait_ge(sg_ready, c * NF + f + 1)
                    if f == 0:
                        if later(c):
                            ve.wait_ge(mlp_done, c)
                    ve.tensor_tensor(gt[:, f, :], sg[:, f % 2, :], p_pair[f % 2][:, NB * Q:2 * NB * Q], ALU.mult)\
                        .then_inc(gt_ready, 1)

            def norm2(c):
                back_steps.start()
                ve.wait_ge(mlp_done, c + 1)
                if later(c):
                    ve.wait_ge(acc_done, c * NX)
                ve.tensor_tensor(h1[:], p_out[0][:, 0:NB * D].rearrange("p (b d) -> p b d", b=NB), hm[:], ALU.add)\
                    .then_inc(h1_ready, 1)
                ve.wait_ge(h1_ready, c + 1)
                ve.bn_stats(stat2[:, 0, :], h1[:, 0, :]).then_inc(back_v, 1)
                ve.wait_ge(back_v, back_steps.next(c))
                ve.bn_stats(stat2[:, 1, :], h1[:, 1, :]).then_inc(back_v, 1)
                ve.wait_ge(back_v, back_steps.next(c))
                settle(ve)
                ve.bn_aggr(mv2[:, 0, :], stat2[:, 0, :]).then_inc(back_v, 1)
                ve.wait_ge(back_v, back_steps.next(c))
                settle(ve)
                ve.bn_aggr(mv2[:, 1, :], stat2[:, 1, :]).then_inc(stat2_ready, 1)

            def norm2_apply(c):
                ve.wait_ge(r2_ready, c + 1)
                if later(c):
                    ve.wait_ge(xnt_done, c)
                for b in range(NB):
                    ins = ve.tensor_scalar(xn[:, b, :], h1[:, b, :], mv2[:, b, 0:1], r2[:, b:b + 1], ALU.subtract, ALU.mult)
                ins.then_inc(xn_ready, 1)

            def ranks(c, s, n, before, gt_, ge_, rank):
                other = s.unsqueeze(2).to_broadcast([128, NB, n, n])
                own = s.unsqueeze(3).to_broadcast([128, NB, n, n])
                prior = before[:].unsqueeze(1).to_broadcast([128, NB, n, n])
                ve.tensor_tensor(gt_[:], other, own, ALU.is_gt).then_inc(back_v, 1)
                ve.wait_ge(back_v, back_steps.next(c))
                ve.tensor_tensor(ge_[:], other, own, ALU.is_ge).then_inc(back_v, 1)
                ve.wait_ge(back_v, back_steps.next(c))
                ve.tensor_tensor(ge_[:], ge_[:], prior, ALU.mult).then_inc(back_v, 1)
                ve.wait_ge(back_v, back_steps.next(c))
                ve.tensor_tensor(gt_[:], gt_[:], ge_[:], ALU.max).then_inc(back_v, 1)
                ve.wait_ge(back_v, back_steps.next(c))
                if rank is not None:
                    ve.reduce_sum(rank[:], gt_[:], AX_X).then_inc(back_v, 1)
                    ve.wait_ge(back_v, back_steps.next(c))

            def route(c):
                ve.wait_ge(th_ready, c + 1)
                ve.tensor_scalar(sc[:], th[:], 0.5, 0.5, ALU.mult, ALU.add).then_inc(back_v, 1)
                ve.wait_ge(back_v, back_steps.next(c))
                ve.tensor_tensor(sv[:], sc[:], gbias[:].unsqueeze(1).to_broadcast([128, NB, NE]), ALU.add).then_inc(back_v, 1)
                ve.wait_ge(back_v, back_steps.next(c))
                pairs = sv[:].rearrange("p b (g j) -> p b g j", j=GE)
                ve.tensor_tensor(gs[:], pairs[:, :, :, 0], pairs[:, :, :, 1], ALU.add).then_inc(back_v, 1)
                ve.wait_ge(back_v, back_steps.next(c))
                ranks(c, gs[:], NG, before4, g_gt, g_ge, g_rank)
                ve.tensor_scalar(g_on[:], g_rank[:].unsqueeze(3).to_broadcast([128, NB, NG, GE]), 1.5, None,
                                 ALU.is_lt).then_inc(back_v, 1)
                ve.wait_ge(back_v, back_steps.next(c))
                on = g_on[:].rearrange("p b g j -> p b (g j)")
                ranks(c, sv[:], NE, before8, e_gt, e_ge, None)
                ve.tensor_tensor(e_gt[:], e_gt[:], on.unsqueeze(2).to_broadcast([128, NB, NE, NE]), ALU.mult).then_inc(back_v, 1)
                ve.wait_ge(back_v, back_steps.next(c))
                ve.reduce_sum(e_rank[:], e_gt[:], AX_X).then_inc(back_v, 1)
                ve.wait_ge(back_v, back_steps.next(c))
                ve.scalar_tensor_tensor(e_on[:].rearrange("p b e -> p (b e)"),
                                        e_rank[:].rearrange("p b e -> p (b e)"), 1.5,
                                        g_on[:].rearrange("p b g j -> p (b g j)"), ALU.is_lt, ALU.mult).then_inc(back_v, 1)
                ve.wait_ge(back_v, back_steps.next(c))
                ve.tensor_tensor(e_w[:], e_on[:], sc[:], ALU.mult).then_inc(back_v, 1)
                ve.wait_ge(back_v, back_steps.next(c))
                ve.reduce_sum(e_sum[:], e_w[:], AX_X).then_inc(back_v, 1)
                ve.wait_ge(back_v, back_steps.next(c))
                ve.tensor_scalar(e_sum1[:], e_sum[:], 1e-6, None, ALU.add).then_inc(back_v, 1)
                ve.wait_ge(back_v, back_steps.next(c))
                ve.reciprocal(e_inv[:], e_sum1[:]).then_inc(back_v, 1)
                ve.wait_ge(back_v, back_steps.next(c))
                ve.tensor_tensor(cw[:], e_w[:], e_inv[:].unsqueeze(2).to_broadcast([128, NB, NE]), ALU.mult)\
                    .then_inc(cw_ready, 1)
                assert back_steps.n == BACK_V, back_steps.n

            def weigh(c, e):
                ve.wait_ge(ex_done, c * NX + e + 1)
                p = p_out[(e + 1) % 2]
                if e == 0:
                    if later(c):
                        ve.wait_ge(out_written, c * 16)
                    ve.tensor_tensor(acc[:], p[:, 0:NB * D].rearrange("p (b d) -> p b d", b=NB), h1[:], ALU.add)\
                        .then_inc(acc_done, 1)
                    return
                if e == 1:
                    ve.wait_ge(cw_ready, c + 1)
                ve.wait_ge(acc_done, c * NX + e)
                for b in range(NB):
                    ins = ve.scalar_tensor_tensor(acc[:, b, :], p[:, b * D:(b + 1) * D], cw[:, b, e - 1:e], acc[:, b, :],
                                                  ALU.mult, ALU.add)
                ins.then_inc(acc_done, 1)

            def experts(c, p):
                for e in range(NX):
                    ve.wait_ge(sx_ready, c * NX + e + 1)
                    if e >= NHH:
                        ve.wait_ge(ex_done, c * NX + e - NHH + 1)
                    else:
                        if later(c):
                            ve.wait_ge(ex_done, c * NX)
                    ve.tensor_tensor(hh[:, e % NHH, :], sg[:, e % 2, :], p_pair[e % 2][:, NB * Q:2 * NB * Q], ALU.mult)\
                        .then_inc(hh_ready, 1)
                    if e == 1:
                        route(c)
                    if e >= 2:
                        weigh(c, e - 2)
                    if p is not None:
                        if e == 2:
                            pre_norm(p)
                        if e == 4:
                            pre_apply(p)
                        if e == 6:
                            pre_split(p)
                weigh(c, NX - 2)
                weigh(c, NX - 1)

            def body(p, f, b):
                if b is not None:
                    mixed(b)
                if f is not None:
                    convolve(f)
                    steps_dt(f)
                if b is not None:
                    split(b, v_hi_ready, v_hi_tail, p_out[1], v_h, v_l, v_lo_ready, v_lo_tail)
                    swiglu(b)
                if f is not None:
                    steps_decay(f)
                    masked_g(f)
                    operands(f)
                    for i in range(NB):
                        scaled_x(f, i)
                if not later(f):
                    setup_rest()
                if p is not None:
                    pre_onehot(p)
                if b is not None:
                    norm2(b)
                    norm2_apply(b)
                if f is not None:
                    scan(f, 0)
                if b is not None:
                    split(b, x_hi_ready, x_hi_tail, p_out[1], x_h, x_l, x_lo_ready, x_lo_tail)
                if f is not None:
                    scan(f, 1)
                if b is not None:
                    experts(b, p)
                elif p is not None:
                    pre_norm(p)
                    pre_apply(p)
                    pre_split(p)

            setup()
            run(ve, body)

        @block.tensor
        def _(pe):
            def split_products(out_, cols, hi, lo, toks, weights_first):
                parts = ((w_hi[:, cols], hi[:, 0, toks]), (wt_hi[:, cols], hi[:, 1, toks]), (w_hi[:, cols], lo[:, toks]),
                         (w_lo[:, cols], hi[:, 0, toks]), (wt_lo[:, cols], hi[0:DT, 1, toks]))
                for i, (w, x) in enumerate(parts):
                    a, b = (w, x) if weights_first else (x, w)
                    ins = pe.matmul(out_, a, b, start=(i == 0), stop=(i == len(parts) - 1))
                return ins

            def transpose_channels(dst, src, done):
                for b in range(NB):
                    pe.transpose(dst[:, b * Q:(b + 1) * Q], src[:, b, 0:DH], idf[:])
                for b in range(NB):
                    ins = pe.transpose(dst[0:DT, (NB + b) * Q:(NB + b + 1) * Q], src[:, b, DH:D], idf[:])
                ins.then_inc(done, 1)

            def pre_embed(c):
                if not later(c):
                    pe.wait_ge(setup_v, 9 + 6 * NB)
                pe.wait_ge(onehot_ready, c + 1)
                if later(c):
                    pe.wait_ge(s_ready[1], c)
                settle(pe)
                for b in range(NB):
                    for k in range(3):
                        ins = pe.matmul(p_misc[:, b * D:(b + 1) * D], onehot[:, b, :], tab3[:, k, :],
                                        start=(k == 0), stop=(k == 2))
                ins.then_inc(emb_done, 1)

            def pre_turn(c):
                pe.wait_ge(un_ready, c + 1)
                transpose_channels(p_misc, un, ut_done)

            def project_in(c):
                if not later(c):
                    pe.wait_ge(w_in_hi, 2)
                    pe.wait_ge(w_in_lo, 2)
                pe.wait_ge(u_hi_ready, c + 1)
                pe.wait_ge(u_hi_tail, c + 1)
                pe.wait_ge(u_lo_ready, c + 1)
                pe.wait_ge(u_lo_tail, c + 1)
                if later(c):
                    pe.wait_ge(e_ready, c * NR)
                if later(c):
                    pe.wait_ge(y_sum[1], c)
                settle(pe)
                for i in range(2):
                    for j in range(2):
                        col = COL_X + (2 * i + j) * 128
                        ins = split_products(p_d[i][:, j * NB * Q:(j + 1) * NB * Q], slice(col, col + 128),
                                             u_h, u_l, slice(0, NB * Q), True)
                    ins.then_inc(x_done[i], 1)
                for b, p in ((0, p_y), (1, p_misc)):
                    split_products(p[:, 0:ZD], slice(0, ZD), u_h, u_l, slice(b * Q, (b + 1) * Q), False)\
                        .then_inc(z_done[b], 1)

            def scan_operands(c):
                pe.wait_ge(xs_ready, c + 1)
                pe.wait_ge(b_ready, c + 1)
                pe.wait_ge(c_ready, c + 1)
                pe.wait_ge(z_ready[0], c + 1)
                pe.wait_ge(z_ready[1], c + 1)
                pe.wait_ge(dx_ready, c + 1)
                pe.wait_ge(xr_ready[0], c + 1)
                pe.wait_ge(xr_ready[1], c + 1)
                settle(pe)
                for b in range(NB):
                    for m in range(NM - 1):
                        ins = pe.transpose(p_d[b][:, m * 128:(m + 1) * 128], xs[:, m, b, :], idf[:])
                    ins.then_inc(xt_done[b], 1)
                for b in range(NB):
                    pe.matmul(p_y[:, b * Q:(b + 1) * Q], bc[:, b, :], cc[:, b, :], start=True, stop=True)
                for b in range(NB):
                    ins = pe.transpose(p_y[:, 256 + b * NS:256 + (b + 1) * NS], bc[:, b, :], idf[0:NS, 0:NS])
                ins.then_inc(g_done, 1)
                pe.wait_ge(pab_ready, c + 1)
                settle(pe)
                for b in range(NB):
                    for i, part in enumerate((pa, pb)):
                        pe.matmul(p_misc[0:64, b * Q:(b + 1) * Q], part[:, b].rearrange("p f r -> p (f r)"), upper16[:],
                                  start=(i == 0), stop=(i == 1))
                for k, left, n in ((0, upper16, 128), (1, ones16, 64)):
                    o = p_misc[0:n, 256 + k * NB * NH:256 + (k + 1) * NB * NH]
                    pe.matmul(o, left[:], pa[:, :, :, 0:HF], start=True, stop=False)
                    pe.matmul(o, left[:], pa[:, :, :, 16:16 + HF], start=False, stop=False)
                    ins = pe.matmul(o, left[:], pb[:, :, :, 16:16 + HF], start=False, stop=True)
                ins.then_inc(cum_done, 1)

            def exponents(c, r):
                b, q = divmod(r, NQ)
                f, g = divmod(q, NQ // 2)
                if r == 0:
                    pe.wait_ge(ri_in, c * 64 + 64)
                    pe.wait_ge(lj_ready, c + 1)
                    pe.wait_ge(xd_ready[0], c + 1)
                    pe.wait_ge(xk_ready[0], c + 1)
                    pe.wait_ge(xd_ready[1], c + 1)
                    pe.wait_ge(xk_ready[1], c + 1)
                if r >= 2:
                    pe.wait_ge(e_ready, c * NR + r - 1)
                pe.matmul(p_d[r % 2][:], lj[:, b, f, :], ri[:, b, f, g * HG:(g + 1) * HG, :].rearrange("p h i -> p (h i)"),
                          start=True, stop=True).then_inc(d_done, 1)

            def scan(c, b):
                if b == 0:
                    pe.wait_ge(lj_ready, c + 1)
                    pe.wait_ge(ecum_ready, c + 1)
                    pe.wait_ge(gm_ready, c + 1)
                    pe.wait_ge(bt_ready, c + 1)
                else:
                    pe.wait_ge(s_ready[0], c + 1)
                    pe.wait_ge(y_sum[0], c + 1)
                if later(c):
                    pe.wait_ge(s_ready[b], c)
                settle(pe)
                pe.matmul(p_misc[:, 0:DI], cc[:, b, :], state[:, b, :], start=True, stop=True).then_inc(yi_done[b], 1)
                if b == 0:
                    exponents(c, 0)
                    exponents(c, 1)
                for q in range(NQ):
                    r = b * NQ + q
                    pe.wait_ge(m_ready, c * NR + r + 1)
                    for h in range(HG):
                        o = slice((q * HG + h) * HD, (q * HG + h + 1) * HD)
                        ins = pe.matmul(p_y[:, o], mr[:, r % NER, h, :], xd[:, b, o], start=True, stop=True)
                    ins.then_inc(yq_done, 1)
                    if r + 2 < NR:
                        exponents(c, r + 2)
                pe.wait_ge(xw_ready, c * NR + (b + 1) * NQ)
                pe.wait_ge(t1_ready[b], c + 1)
                settle(pe)
                pe.matmul(p_misc[0:NS, 0:DI], bt[:, b, :], xw[:, b, :], start=True, stop=True).then_inc(sn_done[b], 1)

            def turn_y(c):
                for b in range(NB):
                    pe.wait_ge(y_ready[b], c + 1)
                    if later(c):
                        pe.wait_ge(acc_done, c * NX)
                    for k in range(DI // 128):
                        ins = pe.transpose(p_out[b][:, k * Q:(k + 1) * Q], y[:, b, k * 128:(k + 1) * 128], idf[:])
                    ins.then_inc(yt_done[b], 1)

            def project_out(c):
                if not later(c):
                    pe.wait_ge(in_late, 96)
                for b in range(NB):
                    pe.wait_ge(yt_ready[b], c + 1)
                for b in range(NB):
                    for k in range(DI // 128):
                        ins = pe.matmul(p_out[0][:, b * D:(b + 1) * D], yt[:, b, k, :], wo[:, k, :],
                                        start=(k == 0), stop=(k == DI // 128 - 1))
                ins.then_inc(m_out, 1)

            def swiglu(c):
                if not later(c):
                    pe.wait_ge(w_rest_hi, 4)
                    pe.wait_ge(w_rest_lo, 4)
                pe.wait_ge(vn_ready, c + 1)
                transpose_channels(p_out[1], vn, vt_done)
                pe.wait_ge(v_hi_ready, c + 1)
                pe.wait_ge(v_hi_tail, c + 1)
                pe.wait_ge(v_lo_ready, c + 1)
                pe.wait_ge(v_lo_tail, c + 1)
                pe.wait_ge(hm_ready, c + 1)

                def down(f):
                    pe.wait_ge(gt_ready, c * NF + f + 1)
                    for b in range(NB):
                        ins = pe.matmul(p_out[0][:, b * D:(b + 1) * D], gt[:, f, b * Q:(b + 1) * Q], wd[:, f, :],
                                        start=(f == 0 and b == 0), stop=(f == NF - 1), skip_group_check=True)
                    if f == NF - 1:
                        ins.then_inc(mlp_done, 1)

                for f in range(NF):
                    if f >= 2:
                        pe.wait_ge(gt_ready, c * NF + f - 1)
                    else:
                        if later(c):
                            pe.wait_ge(hh_ready, c * NX)
                    p = p_pair[f % 2]
                    split_products(p[:, 0:NB * Q], slice(COL_G + f * 128, COL_G + (f + 1) * 128), v_h, v_l,
                                   slice(0, NB * Q), True)
                    split_products(p[:, NB * Q:2 * NB * Q], slice(COL_U + f * 128, COL_U + (f + 1) * 128), v_h, v_l,
                                   slice(0, NB * Q), True).then_inc(gu_done, 1)
                    if f >= 2:
                        down(f - 2)
                down(NF - 2)
                down(NF - 1)

            def turn_x(c):
                pe.wait_ge(xn_ready, c + 1)
                transpose_channels(p_out[1], xn, xnt_done)

            def experts(c, p):
                pe.wait_ge(x_hi_ready, c + 1)
                pe.wait_ge(x_hi_tail, c + 1)
                pe.wait_ge(x_lo_ready, c + 1)
                pe.wait_ge(x_lo_tail, c + 1)
                pe.wait_ge(h1_ready, c + 1)
                settle(pe)
                for b in range(NB):
                    ins = split_products(p_out[0][:, b * NE:(b + 1) * NE], slice(COL_R, COLS), x_h, x_l,
                                         slice(b * Q, (b + 1) * Q), False)
                ins.then_inc(router_done, 1)

                def down(e):
                    pe.wait_ge(hh_ready, c * NX + e + 1)
                    if e == 1:
                        pe.wait_ge(th_ready, c + 1)
                    if e >= 2:
                        pe.wait_ge(acc_done, c * NX + e - 1)
                    for b in range(NB):
                        ins = pe.matmul(p_out[(e + 1) % 2][:, b * D:(b + 1) * D], hh[:, e % NHH, b * Q:(b + 1) * Q],
                                        w2t[:, e, :], start=True, stop=True)
                    ins.then_inc(ex_done, 1)

                for e in range(NX):
                    if e >= 2:
                        pe.wait_ge(hh_ready, c * NX + e - 1)
                    else:
                        pe.wait_ge(gt_ready, c * NF + NF - 1 + e)
                    o, col = p_pair[e % 2], COL_E + e * 2 * NI
                    split_products(o[:, 0:NB * Q], slice(col, col + NI), x_h, x_l, slice(0, NB * Q), True)
                    split_products(o[:, NB * Q:2 * NB * Q], slice(col + NI, col + 2 * NI), x_h, x_l,
                                   slice(0, NB * Q), True).then_inc(h13_done, 1)
                    if e == 5 and p is not None:
                        pre_turn(p)
                    if e >= 2:
                        down(e - 2)
                down(NX - 2)
                down(NX - 1)

            def body(p, f, b):
                if b is not None:
                    turn_y(b)
                    project_out(b)
                if f is not None:
                    project_in(f)
                if b is not None:
                    swiglu(b)
                if f is not None:
                    scan_operands(f)
                    scan(f, 0)
                if b is not None:
                    turn_x(b)
                if f is not None:
                    scan(f, 1)
                if p is not None:
                    pre_embed(p)
                if b is not None:
                    experts(b, p)
                elif p is not None:
                    pre_turn(p)

            pe.wait_ge(in_small, 16 * N_SMALL)
            pe.wait_ge(setup_p, 4)
            run(pe, body)


N_SMALL = 21


def kernel(x, L0_tok_color_W, L0_tok_shape_W, L0_tok_quantity_W, L0_tok_special_W, L0_attn_norm1_w,
           L0_attn_in_proj_w, L0_attn_conv_w, L0_attn_conv_b, L0_attn_dt_bias, L0_attn_A_log, L0_attn_D,
           L0_attn_out_proj_w, L0_attn_norm2_w, L0_attn_w_gate, L0_attn_w_up, L0_attn_w_down, L0_ffn_gate_weight,
           L0_ffn_gate_bias, L0_ffn_w1, L0_ffn_w2, L0_ffn_w3, L0_ffn_sw1, L0_ffn_sw2, L0_ffn_sw3):
    import numpy as np
    import concourse.bacc as bacc
    from concourse.bass_utils import run_bass_kernel_spmd

    f32 = np.float32
    rate = np.exp(-(np.arange(0, D, 2, dtype=f32) / f32(D)) * f32(np.log(10000.0)))
    angle = np.arange(L, dtype=f32)[:, None] * rate.astype(f32)
    position = np.stack([np.sin(angle), np.cos(angle)], axis=-1).reshape(L, D).astype(f32)
    head_rows = np.zeros((64, HF), f32)
    for g in range(4):
        for h in range(HF):
            head_rows[16 * g + h, h] = 1.0
    token, pair = np.arange(Q)[None, :], np.arange(Q // 2)[:, None]
    mask_rows = np.where(token < 2 * pair, f32(FAR), f32(0)).astype(f32)
    pair_rows = (token // 2 == pair).astype(f32)
    ids = np.arange(64)
    features = np.concatenate([L0_tok_color_W[ids // 16], L0_tok_shape_W[ids % 16 // 4], L0_tok_quantity_W[ids % 4]],
                              axis=1)
    z, xbc, dt = np.split(np.asarray(L0_attn_in_proj_w), [DI, 2 * DI + 2 * NS], axis=1)
    columns = [z, dt, xbc, L0_attn_w_gate, L0_attn_w_up, np.transpose(L0_ffn_sw1), np.transpose(L0_ffn_sw3)]
    for e in range(NE):
        columns += [np.transpose(L0_ffn_w1[e]), np.transpose(L0_ffn_w3[e])]
    columns.append(np.transpose(L0_ffn_gate_weight))
    w2 = np.concatenate([np.transpose(L0_ffn_sw2)[:, None, :], np.transpose(L0_ffn_w2, (2, 0, 1))], axis=1)
    arrays = {
        "tokens": x, "position": position, "vocab_ids": np.arange(V, dtype=f32)[:, None],
        "table": np.concatenate([features, L0_tok_special_W], axis=0),
        "weights": np.concatenate(columns, axis=1),
        "norm1": np.reshape(L0_attn_norm1_w, (D, 1)), "norm2": np.reshape(L0_attn_norm2_w, (D, 1)),
        "conv_w": np.transpose(np.reshape(L0_attn_conv_w, (NM, 128, KC)), (1, 0, 2)),
        "conv_b": np.transpose(np.reshape(L0_attn_conv_b, (NM, 128))),
        "dt_bias": L0_attn_dt_bias, "a_log": L0_attn_A_log, "d_skip": L0_attn_D,
        "w_out": np.transpose(np.reshape(L0_attn_out_proj_w, (DI // 128, 128, D)), (1, 0, 2)),
        "w_down": np.transpose(np.reshape(L0_attn_w_down, (NF, 128, D)), (1, 0, 2)),
        "w2": w2, "gate_bias": L0_ffn_gate_bias,
        "identity": np.eye(128, dtype=f32), "lower_ones": np.triu(np.ones((128, 128), f32)),
        "head_rows": head_rows, "mask_rows": mask_rows, "pair_rows": pair_rows,
        "order8": np.tril(np.ones((NE, NE), f32), -1), "order4": np.tril(np.ones((NG, NG), f32), -1),
    }
    nc = bacc.Bacc("TRN2", target_bir_lowering=False, num_devices=1)
    args = []
    for name, a in arrays.items():
        arrays[name] = a = np.ascontiguousarray(a)
        args.append(nc.dram_tensor(name, a.shape, mybir.dt.from_np(a.dtype), kind="ExternalInput").ap())
    args.append(nc.dram_tensor("out", (NB, L, D), F32, kind="ExternalOutput").ap())
    program(nc, *args)
    r = run_bass_kernel_spmd(nc, [arrays], core_ids=[0])
    return r.results[0]["out"]
```

```python
from contextlib import ExitStack

import concourse.bass as bass
from concourse import mybir

ALU = mybir.AluOpType
ACT = mybir.ActivationFunctionType
AX_X = mybir.AxisListType.X
F32 = mybir.dt.float32
F16 = mybir.dt.float16
BF16 = mybir.dt.bfloat16
I32 = mybir.dt.int32

NB = 2
L = 2048
Q = 128
NC = L // Q
D = 192
DH, DT = 128, D - 128
V = 70
DI = 384
NH, HD = 24, 16
NS = 64
KC = 4
NM = (DI + 2 * NS) // 128
DM = 768
NF = DM // 128
NE, NI = 8, 128
NG, GE = 4, 2
HG = 4
NQ = NH // HG
KT = DI // 128
ZD = DI + NH
COL_X = ZD
COL_G = COL_X + NM * 128
COL_U = COL_G + DM
COL_E = COL_U + DM
COL_R = COL_E + (NE + 1) * 2 * NI
COLS = COL_R + NE
HF = NH // 2
STEP = 1.0 / 16
ROUND = 1.5 * 2.0 ** 23 * STEP
DEAD = 88.0
FAR = -12000.0
EMB_SCALE = float(D) ** 0.5

PRE_V, FRONT_V, BACK_V = 3, 22, 23
PRE_P, FRONT_P, BACK_P = 1, 1, 2


def later(c):
    return not (isinstance(c, int) and c == 0)


class Steps:

    def __init__(self, per):
        self.per, self.n = per, 0

    def start(self):
        self.n = 0

    def next(self, c):
        self.n += 1
        return c * self.per + self.n

    def back(self, c, n):
        return c * self.per + self.n - n


def program(nc, tokens, position, vocab_ids, table, weights, norm1, norm2, conv_w, conv_b, dt_bias, a_log,
            d_skip, w_out, w_down, w2, gate_bias, identity, lower_ones, head_rows, mask_rows, pair_rows, spread_rows, order8, order4, out):
    with ExitStack() as ctx:
        def sb(name, shape, dt=F32):
            return ctx.enter_context(nc.sbuf_tensor(name, shape, dt))

        def sem(name):
            return ctx.enter_context(nc.semaphore(name))

        ids = sb("ids", [V, 1])
        tab = sb("tab", [V, D])
        tab_rest = sb("tab_rest", [V, 2, D])
        tab3 = sb("tab3", [V, 3, D], BF16)
        w_raw = sb("w_raw", [128, COLS])
        wt_raw = sb("wt_raw", [128, COLS])
        w_hi = sb("w_hi", [128, COLS], F16)
        w_lo = sb("w_lo", [128, COLS], F16)
        wt_hi = sb("wt_hi", [128, COLS], F16)
        wt_lo = sb("wt_lo", [DT, COLS], F16)
        nrm = sb("nrm", [128, 4])
        cw_ = sb("cw_", [128, NM, KC])
        cb_ = sb("cb_", [128, NM])
        dtb = sb("dtb", [128, NH])
        alog = sb("alog", [128, NH])
        aexp = sb("aexp", [128, NH])
        dsk = sb("dsk", [128, KT])
        spread = sb("spread", [64, KT, 2, 128])
        spread16 = sb("spread16", [64, KT, 2, 128], F16)
        wo = sb("wo", [128, DI // 128, D])
        wd = sb("wd", [128, NF, D])
        w2t = sb("w2t", [128, NE + 1, D])
        gbias = sb("gbias", [128, NE])
        idf = sb("idf", [128, 128])
        upper = sb("upper", [128, 128])
        upper16 = sb("upper16", [128, 128], F16)
        ones16 = sb("ones16", [128, 64], F16)
        hrows = sb("hrows", [NS, HF])
        mrows = sb("mrows", [128, Q])
        prows = sb("prows", [128, Q])
        before8 = sb("before8", [128, NE, NE])
        before4 = sb("before4", [128, NG, NG])
        mhalf = sb("mhalf", [128, 2])

        tok = sb("tok", [V, NB, Q], I32)
        pos = sb("pos", [128, D])
        onehot = sb("onehot", [V, NB, Q], BF16)
        h0_next = sb("h0_next", [128, NB, D])
        stat = sb("stat", [128, NB, 6])
        mv = sb("mv", [128, NB, 2])
        var0 = sb("var0", [128, NB])
        r0 = sb("r0", [128, NB])
        un = sb("un", [128, NB, D])
        u_h = sb("u_h", [128, 2, NB * Q], F16)
        u_l = sb("u_l", [128, NB * Q], F16)

        h0 = sb("h0", [128, NB, D])
        xr = sb("xr", [128, NM, NB, KC - 1 + Q])
        xa = sb("xa", [128, NM, NB, Q])
        xs = sb("xs", [128, NM - 1, NB, Q])
        bc = sb("bc", [NS, NB, Q])
        cc = sb("cc", [NS, NB, Q])
        zs = sb("zs", [128, KT, NB, Q])
        dx = sb("dx", [128, NB, NH])
        dn = sb("dn", [128, NB, NH])
        de = sb("de", [128, NB, NH])
        dl = sb("dl", [128, NB, NH])
        dt_ = sb("dt_", [128, NB, NH])
        ap_ = sb("ap_", [128, NB, NH])
        ag_ = sb("ag_", [128, NB, NH])
        ar_ = sb("ar_", [128, NB, NH])
        pa = sb("pa", [128, NB, 2, 32], F16)
        pb = sb("pb", [128, NB, 2, 32], F16)
        eend = sb("eend", [NS, NB, NH])
        ecx = sb("ecx", [128, KT, NB, Q])
        lj = sb("lj", [128, NB, 2, 128], F16)
        ri = sb("ri", [128, NB, 2, HF, Q], F16)
        gm = sb("gm", [128, NB, Q])
        bt = sb("bt", [128, NB, NS])
        xd = sb("xd", [128, NB, NH, 2 * HD])
        xk = sb("xk", [128, KT, NB, Q])
        xw = sb("xw", [128, NB, DI])
        NER = 4
        er = sb("er", [128, NER, HG, Q])
        mr = sb("mr", [128, NER, HG, Q])
        t1 = sb("t1", [128, NB, KT, Q])
        state = sb("state", [NS, NB, DI])
        y = sb("y", [128, NB, KT, Q])

        hm = sb("hm", [128, NB, D])
        junk = sb("junk", [128, NB, D])
        ss = sb("ss", [128, NB])
        vv = sb("vv", [128, NB])
        rm = sb("rm", [128, NB])
        vn = sb("vn", [128, NB, D])
        v_h = sb("v_h", [128, 2, NB * Q], F16)
        v_l = sb("v_l", [128, NB * Q], F16)
        sg = sb("sg", [128, 2, NB * Q])
        gt = sb("gt", [128, NF, NB * Q])
        h1 = sb("h1", [128, NB, D])
        stat2 = sb("stat2", [128, NB, 6])
        mv2 = sb("mv2", [128, NB, 2])
        var2 = sb("var2", [128, NB])
        r2 = sb("r2", [128, NB])
        xn = sb("xn", [128, NB, D])
        x_h = sb("x_h", [128, 2, NB * Q], F16)
        x_l = sb("x_l", [128, NB * Q], F16)
        th = sb("th", [128, NB, NE])
        sc = sb("sc", [128, NB, NE])
        sv = sb("sv", [128, NB, NE])
        gs = sb("gs", [128, NB, NG])
        g_gt = sb("g_gt", [128, NB, NG, NG])
        g_ge = sb("g_ge", [128, NB, NG, NG])
        g_rank = sb("g_rank", [128, NB, NG])
        g_on = sb("g_on", [128, NB, NG, GE])
        e_gt = sb("e_gt", [128, NB, NE, NE])
        e_ge = sb("e_ge", [128, NB, NE, NE])
        e_rank = sb("e_rank", [128, NB, NE])
        e_on = sb("e_on", [128, NB, NE])
        e_w = sb("e_w", [128, NB, NE])
        e_sum = sb("e_sum", [128, NB])
        e_sum1 = sb("e_sum1", [128, NB])
        e_inv = sb("e_inv", [128, NB])
        cw = sb("cw", [128, NB, NE])
        NHH = 3
        hh = sb("hh", [128, NHH, NB * Q])
        acc = sb("acc", [128, NB, D])

        sums = nc.dram_tensor("sums", (NB, 2, 64, Q), F16, kind="Internal").ap()
        bank = [ctx.enter_context(nc.psum_tensor(f"bank{i}", [128, 512], F32)) for i in range(8)]
        p_pair = bank[0:2]
        p_out = bank[2:4]
        p_misc, p_d0, p_d1, p_y = bank[4:8]
        p_d = (p_d0, p_d1)

        in_small, in_w, in_late = sem("in_small"), sem("in_w"), sem("in_late")
        setup_v, setup_a, setup_p = sem("setup_v"), sem("setup_a"), sem("setup_p")
        w_in_hi, w_in_lo, w_rest_hi, w_rest_lo = sem("w_in_hi"), sem("w_in_lo"), sem("w_rest_hi"), sem("w_rest_lo")
        passed = sem("passed")
        tokens_in, position_in = sem("tokens_in"), sem("position_in")
        onehot_ready, emb_done, h0_ready, stat_ready, r0_ready = (sem(n) for n in (
            "onehot_ready", "emb_done", "h0_ready", "stat_ready", "r0_ready"))
        un_ready, ut_done, u_hi_ready, u_hi_tail, u_lo_ready, u_lo_tail = (sem(n) for n in (
            "un_ready", "ut_done", "u_hi_ready", "u_hi_tail", "u_lo_ready", "u_lo_tail"))
        pre_v, front_v, back_v, pre_p, front_p, back_p, back_a = (sem(n) for n in (
            "pre_v", "front_v", "back_v", "pre_p", "front_p", "back_p", "back_a"))
        h0_copied = sem("h0_copied")
        x_done = [sem(f"x_done{i}") for i in range(2)]
        z_done = [sem(f"z_done{i}") for i in range(2)]
        xr_ready = [sem(f"xr_ready{i}") for i in range(2)]
        z_ready = [sem(f"z_ready{i}") for i in range(2)]
        dx_ready, dn_ready, de_ready, dl_ready, pab_ready = (sem(n) for n in (
            "dx_ready", "dn_ready", "de_ready", "dl_ready", "pab_ready"))
        xa_ready, halo_kept, xs_ready, b_ready, c_ready = (sem(n) for n in (
            "xa_ready", "halo_kept", "xs_ready", "b_ready", "c_ready"))
        cum_done, eend_ready = sem("cum_done"), sem("eend_ready")
        cumx_done = [sem(f"cumx_done{i}") for i in range(2)]
        ecx_ready = [sem(f"ecx_ready{i}") for i in range(2)]
        g_done, gm_ready, bt_ready = sem("g_done"), sem("gm_ready"), sem("bt_ready")
        xt_done = [sem(f"xt_done{b}") for b in range(NB)]
        lj_high, lj_ready = sem("lj_high"), sem("lj_ready")
        xd_ready = [sem(f"xd_ready{b}") for b in range(NB)]
        xk_ready = sem("xk_ready")
        ri_in, sums_out = sem("ri_in"), sem("sums_out")
        NR = NB * NQ
        d_done = sem("d_done")
        e_ready = sem("e_ready")
        m_ready = sem("m_ready")
        yq_done = sem("yq_done")
        xw_ready = sem("xw_ready")
        yi_done = [sem(f"yi_done{b}") for b in range(NB)]
        t1_ready = [sem(f"t1_ready{b}") for b in range(NB)]
        t1_sum = [sem(f"t1_sum{b}") for b in range(NB)]
        sn_done = [sem(f"sn_done{b}") for b in range(NB)]
        s_decayed = [sem(f"s_decayed{b}") for b in range(NB)]
        s_ready = [sem(f"s_ready{b}") for b in range(NB)]
        y_sum = [sem(f"y_sum{b}") for b in range(NB)]
        y_ready = [sem(f"y_ready{b}") for b in range(NB)]
        m_out, hm_ready, rm_ready, vn_ready, vt_done = (sem(n) for n in (
            "m_out", "hm_ready", "rm_ready", "vn_ready", "vt_done"))
        v_hi_ready, v_hi_tail, v_lo_ready, v_lo_tail = (sem(n) for n in (
            "v_hi_ready", "v_hi_tail", "v_lo_ready", "v_lo_tail"))
        gu_done, sg_ready, gt_ready = sem("gu_done"), sem("sg_ready"), sem("gt_ready")
        mlp_done, h1_ready, stat2_ready, r2_ready, xn_ready, xnt_done = (sem(n) for n in (
            "mlp_done", "h1_ready", "stat2_ready", "r2_ready", "xn_ready", "xnt_done"))
        x_hi_ready, x_hi_tail, x_lo_ready, x_lo_tail = (sem(n) for n in (
            "x_hi_ready", "x_hi_tail", "x_lo_ready", "x_lo_tail"))
        router_done, th_ready, cw_ready = sem("router_done"), sem("th_ready"), sem("cw_ready")
        NX = NE + 1
        h13_done, sx_ready, hh_ready, ex_done, acc_done = (sem(n) for n in (
            "h13_done", "sx_ready", "hh_ready", "ex_done", "acc_done"))
        out_written = sem("out_written")

        def settle(eng):
            eng.sem_inc(passed, 1)

        block = ctx.enter_context(nc.Block())

        def run(eng, body):
            body(0, None, None)
            body(1, 0, None)
            body(2, 1, 0)
            with eng.Fori(1, NC - 2) as i:
                body(i + 2, i + 1, i)
            body(None, NC - 1, NC - 2)
            body(None, None, NC - 1)

        @block.sync
        def _(sp):
            small = [(ids[:], vocab_ids), (tab[:], table), (idf[:], identity), (upper[:], lower_ones),
                     (nrm[:, 0:1], norm1[0:DH, :]), (nrm[0:DT, 1:2], norm1[DH:D, :]), (nrm[DT:128, 1:2], norm1[DH:D, :]),
                     (nrm[:, 2:3], norm2[0:DH, :]), (nrm[0:DT, 3:4], norm2[DH:D, :]), (nrm[DT:128, 3:4], norm2[DH:D, :]),
                     (cw_[:], conv_w), (cb_[:], conv_b),
                     (dtb[:], dt_bias.partition_broadcast(128)), (alog[:], a_log.partition_broadcast(128)),
                     (dsk[:], d_skip), (spread[:], spread_rows), (gbias[:], gate_bias.partition_broadcast(128)),
                     (hrows[:], head_rows), (mrows[64:128, :], mask_rows), (prows[64:128, :], pair_rows),
                     (before8[:], order8.partition_broadcast(128)),
                     (before4[:], order4.partition_broadcast(128))]
            assert len(small) == N_SMALL
            for dst, src in small:
                sp.dma_start(dst, src).then_inc(in_small, 16)
            for part in (slice(0, COL_G),):
                sp.dma_start(w_raw[:, part], weights[0:DH, part]).then_inc(in_w, 16)
                sp.dma_start(wt_raw[0:DT, part], weights[DH:D, part]).then_inc(in_w, 16)
                sp.dma_start(wt_raw[DT:128, part], weights[DH:D, part]).then_inc(in_w, 16)

            def load(c):
                if later(c):
                    sp.wait_ge(onehot_ready, c)
                settle(sp)
                sp.dma_start(tok[:], tokens[:, bass.ds(c * Q, Q)].partition_broadcast(V)).then_inc(tokens_in, 16)
                if later(c):
                    sp.wait_ge(h0_ready, c)
                settle(sp)
                sp.dma_start(pos[:], position[bass.ds(c * Q, Q), :]).then_inc(position_in, 16)

            def sums_in_rows(c):
                sp.wait_ge(lj_ready, c + 1)
                settle(sp)
                sp.dma_start(sums.rearrange("b f r i -> r b f i"), lj[0:64]).then_inc(sums_out, 16)
                sp.wait_ge(sums_out, c * 16 + 16)
                settle(sp)
                if later(c):
                    sp.wait_ge(d_done, c * NR)
                settle(sp)
                for b in range(NB):
                    for f in range(2):
                        sp.dma_start(ri[HF:HF + 4, b, f, :, :],
                                     sums[b, f].rearrange("(g r) i -> g r i", g=4)[:, 0:HF, :]).then_inc(ri_in, 16)

            def store(c):
                sp.wait_ge(acc_done, c * NX + NX)
                settle(sp)
                sp.dma_start(out[:, bass.ds(c * Q, Q), :].rearrange("b t d -> t b d"), acc[:]).then_inc(out_written, 16)

            def body(p, f, b):
                if later_chunk(p):
                    load(p)
                if p is not None:
                    sums_in_rows(p)
                if b is not None:
                    store(b)

            def later_chunk(p):
                return p is not None and later(p)

            load(0)
            rest = slice(COL_G, COLS)
            sp.dma_start(w_raw[:, rest], weights[0:DH, rest]).then_inc(in_late, 16)
            sp.dma_start(wt_raw[0:DT, rest], weights[DH:D, rest]).then_inc(in_late, 16)
            sp.dma_start(wt_raw[DT:128, rest], weights[DH:D, rest]).then_inc(in_late, 16)
            sp.dma_start(wo[:], w_out).then_inc(in_late, 16)
            sp.dma_start(wd[:], w_down).then_inc(in_late, 16)
            sp.dma_start(w2t[:], w2).then_inc(in_late, 16)
            run(sp, body)
            sp.wait_ge(out_written, 16 * NC)

        @block.gpsimd
        def _(pool):
            pool.memset(mhalf[:], -0.5).then_inc(setup_p, 1)
            pool.memset(state[:], 0.0).then_inc(setup_p, 1)
            pool.memset(xr[:, :, :, 0:KC - 1], 0.0).then_inc(setup_p, 1)
            pool.memset(ones16[:], 1.0).then_inc(setup_p, 1)
            pool.memset(xd[:], 0.0).then_inc(setup_p, 1)
            pool.wait_ge(setup_p, 5)

            def rsqrt(c, ready, src, scale, bias, mid, dst, chain, steps, k, done):
                pool.wait_ge(ready, c + 1)
                settle(pool)
                pool.tensor_scalar(mid, src, scale, bias, ALU.mult, ALU.add).then_inc(chain, 1)
                pool.wait_ge(chain, c * steps + k)
                pool.tensor_tensor(dst, mid, mhalf[:], ALU.pow).then_inc(done, 1)

            def pre(c):
                rsqrt(c, stat_ready, mv[:, :, 1], 1.0 + 1e-6, 1e-11, var0[:], r0[:], pre_p, PRE_P, 1, r0_ready)

            def keep(c):
                if later(c):
                    pool.wait_ge(hm_ready, c)
                pool.wait_ge(h0_ready, c + 1)
                settle(pool)
                pool.tensor_copy(h0[:], h0_next[:]).then_inc(h0_copied, 1)

            def halo(c):
                pool.wait_ge(xa_ready, c + 1)
                settle(pool)
                pool.tensor_copy(xr[:, :, :, 0:KC - 1], xr[:, :, :, Q:Q + KC - 1]).then_inc(halo_kept, 1)

            def scan(c, b):
                pool.wait_ge(eend_ready, c + 1)
                pool.wait_ge(yi_done[b], c + 1)
                if later(c):
                    pool.wait_ge(s_ready[b], c)
                sv_ = state[:, b, :].rearrange("n (h p) -> n h p", h=NH)
                pool.tensor_tensor(sv_, sv_, eend[:, b, :].unsqueeze(2).to_broadcast([NS, NH, HD]), ALU.mult)\
                    .then_inc(s_decayed[b], 1)
                pool.wait_ge(t1_ready[b], c + 1)
                pool.wait_ge(xk_ready, c + 1)
                pool.tensor_tensor(t1[:, b], t1[:, b], xk[:, :, b, :], ALU.add).then_inc(t1_sum[b], 1)
                if later(c):
                    pool.wait_ge(sn_done[b], c)
                for q in range(NQ):
                    r = b * NQ + q
                    pool.wait_ge(e_ready, c * NR + r + 1)
                    if q == 0:
                        pool.wait_ge(xd_ready[b], c + 1)
                    for odd in range(2):
                        h = slice(q * HG + odd, (q + 1) * HG, 2)
                        o = slice(q * HG * HD, (q + 1) * HG * HD)
                        ins = pool.tensor_tensor(
                            xw[:, b, o].rearrange("p (g o d) -> p g o d", o=2, d=HD)[:, :, odd, :],
                            xd[:, b, h, odd * HD:(odd + 1) * HD],
                            er[:, r % NER, odd:HG:2, Q - 1:Q].to_broadcast([128, HG // 2, HD]), ALU.mult)
                    ins.then_inc(xw_ready, 1)

            def gate(c, b):
                pool.wait_ge(y_sum[b], c + 1)
                pool.wait_ge(z_ready[0], c + 1)
                pool.wait_ge(z_ready[1], c + 1)
                pool.tensor_tensor(y[:, b], y[:, b], zs[:, :, b, :], ALU.mult).then_inc(y_ready[b], 1)

            def mixed(c):
                pool.wait_ge(back_a, c * 2 + 2)
                settle(pool)
                pool.tensor_scalar(vv[:], ss[:], 1.0 / D, 1e-6, ALU.mult, ALU.add).then_inc(back_p, 1)
                pool.wait_ge(back_p, c + 1)
                pool.tensor_tensor(rm[:], vv[:], mhalf[:], ALU.pow).then_inc(rm_ready, 1)

            def body(p, f, b):
                if b is not None:
                    mixed(b)
                if f is not None:
                    keep(f)
                    scan(f, 0)
                    gate(f, 0)
                if p is not None:
                    pre(p)
                if b is not None:
                    rsqrt(b, stat2_ready, mv2[:, :, 1], 1.0, 1e-5, var2[:], r2[:], front_p, 1, 1, r2_ready)
                if f is not None:
                    scan(f, 1)
                    gate(f, 1)
                if p is not None:
                    halo(p)

            run(pool, body)

        @block.scalar
        def _(act):
            act.wait_ge(in_small, 16 * N_SMALL)
            act.activation(aexp[:], alog[:], ACT.Exp).then_inc(setup_a, 1)
            act.wait_ge(in_w, 48)
            act.activation(w_hi[:, 0:COL_G], w_raw[:, 0:COL_G], ACT.Copy, scale=nrm[:, 0:1]).then_inc(w_in_hi, 1)
            act.activation(wt_hi[:, 0:COL_G], wt_raw[:, 0:COL_G], ACT.Copy, scale=nrm[:, 1:2]).then_inc(w_in_hi, 1)

            def setup_rest():
                act.wait_ge(in_late, 96)
                act.activation(w_hi[:, COL_G:COL_E], w_raw[:, COL_G:COL_E], ACT.Copy, scale=nrm[:, 2:3])\
                    .then_inc(w_rest_hi, 1)
                act.activation(wt_hi[:, COL_G:COL_E], wt_raw[:, COL_G:COL_E], ACT.Copy, scale=nrm[:, 3:4])\
                    .then_inc(w_rest_hi, 1)
                act.copy(w_hi[:, COL_E:COLS], w_raw[:, COL_E:COLS]).then_inc(w_rest_hi, 1)
                act.copy(wt_hi[:, COL_E:COLS], wt_raw[:, COL_E:COLS]).then_inc(w_rest_hi, 1)

            def split(c, done, src, hi, taken, head, tail):
                act.wait_ge(done, c + 1)
                if later(c):
                    act.wait_ge(taken[0], c * taken[1])
                act.copy(hi[:, 0, :], src[:, 0:NB * Q]).then_inc(head, 1)
                act.copy(hi[0:DT, 1, :], src[0:DT, NB * Q:2 * NB * Q]).then_inc(tail, 1)

            def convolved_in(c):
                for i in range(2):
                    act.wait_ge(x_done[i], c + 1)
                    if later(c):
                        act.wait_ge(xa_ready, c)
                    if later(c):
                        act.wait_ge(halo_kept, c)
                    act.copy(xr[:, 2 * i:2 * i + 2, :, KC - 1:KC - 1 + Q],
                             p_d[i][:].rearrange("p (m b t) -> p m b t", m=2, b=NB)).then_inc(xr_ready[i], 1)

            def gates(c):
                for i, t in ((0, slice(0, 2)), (1, slice(2, KT))):
                    act.wait_ge(z_done[i], c + 1)
                    if later(c):
                        act.wait_ge(y_ready[1], c)
                    act.activation(zs[:, t], (p_y, p_misc)[i][:, 0:(t.stop - t.start) * NB * Q]
                                   .rearrange("p (k b t) -> p k b t", b=NB, t=Q), ACT.Silu).then_inc(z_ready[i], 1)

            def convolved_out(c):
                act.wait_ge(xa_ready, c + 1)
                if later(c):
                    act.wait_ge(xt_done[1], c)
                    act.wait_ge(xk_ready, c)
                act.activation(xs[:], xa[:, 0:NM - 1], ACT.Silu).then_inc(xs_ready, 1)
                if later(c):
                    act.wait_ge(g_done, c)
                    act.wait_ge(yi_done[1], c)
                act.activation(bc[:], xa[0:NS, NM - 1], ACT.Silu).then_inc(b_ready, 1)
                act.activation(cc[:], xa[NS:128, NM - 1], ACT.Silu).then_inc(c_ready, 1)

            def softplus(c):
                act.wait_ge(dn_ready, c + 1)
                if later(c):
                    act.wait_ge(dl_ready, c)
                act.activation(de[:], dn[:], ACT.Exp).then_inc(de_ready, 1)
                act.wait_ge(de_ready, c + 1)
                if later(c):
                    act.wait_ge(pab_ready, c)
                act.activation(dl[:], de[:], ACT.Ln, bias=1.0).then_inc(dl_ready, 1)

            def b_on_tokens(c):
                act.wait_ge(g_done, c + 1)
                if later(c):
                    act.wait_ge(sn_done[1], c)
                act.copy(bt[:], p_y[:, 256:256 + NB * NS].rearrange("p (b n) -> p b n", b=NB)).then_inc(bt_ready, 1)

            def decays(c):
                act.wait_ge(lj_ready, c + 1)
                if later(c):
                    act.wait_ge(s_decayed[1], c)
                act.activation(eend[:], p_misc[0:NS, 256:256 + NB * NH].rearrange("p (b h) -> p b h", b=NB),
                               ACT.Exp, scale=-1.0).then_inc(eend_ready, 1)
                for i, t in ((0, slice(0, 2)), (1, slice(2, KT))):
                    act.wait_ge(cumx_done[i], c + 1)
                    if later(c):
                        act.wait_ge(t1_ready[1], c)
                    act.activation(ecx[:, t], p_d[i][:, 0:(t.stop - t.start) * NB * Q]
                                   .rearrange("p (k b t) -> p k b t", b=NB, t=Q), ACT.Exp, scale=-1.0)\
                        .then_inc(ecx_ready[i], 1)

            def scan(c, b, between=None):
                for q in range(NQ):
                    if between is not None and q == 5:
                        between()
                    r = b * NQ + q
                    act.wait_ge(d_done, c * NR + r + 1)
                    if later(c) or r - NER + 1 > 0:
                        act.wait_ge(m_ready, c * NR + r - NER + 1)
                    if later(c) or r - NER + 1 > 0:
                        act.wait_ge(xw_ready, c * NR + r - NER + 1)
                    act.activation(er[:, r % NER], p_d[r % 2][:].rearrange("p (h i) -> p h i", h=HG), ACT.Exp)\
                        .then_inc(e_ready, 1)

            def mixed(c):
                act.wait_ge(m_out, c + 1)
                if later(c):
                    act.wait_ge(rm_ready, c)
                for b in range(NB):
                    if later(c):
                        act.wait_ge(back_a, c * 2)
                    act.activation(junk[:, b, :], p_out[0][:, b * D:(b + 1) * D], ACT.Square, accum_out=ss[:, b:b + 1])\
                        .then_inc(back_a, 1)

            def swiglu(c, p):
                for f in range(NF):
                    act.wait_ge(gu_done, c * NF + f + 1)
                    if f >= 2:
                        act.wait_ge(gt_ready, c * NF + f - 1)
                    else:
                        if later(c):
                            act.wait_ge(hh_ready, c * NX)
                    act.activation(sg[:, f % 2, :], p_pair[f % 2][:, 0:NB * Q], ACT.Silu).then_inc(sg_ready, 1)
                    if f == 4 and p is not None:
                        pre_split(p)

            def route(c):
                act.wait_ge(router_done, c + 1)
                if later(c):
                    act.wait_ge(cw_ready, c)
                act.activation(th[:], p_out[0][:, 0:NB * NE].rearrange("p (b e) -> p b e", b=NB), ACT.Tanh, scale=0.5)\
                    .then_inc(th_ready, 1)

            def pre_split(c):
                split(c, ut_done, p_misc, u_h, (z_done[1], 1), u_hi_ready, u_hi_tail)

            def experts(c, p):
                for e in range(NX):
                    act.wait_ge(h13_done, c * NX + e + 1)
                    if e >= 2:
                        act.wait_ge(hh_ready, c * NX + e - 1)
                    else:
                        act.wait_ge(gt_ready, c * NF + NF - 1 + e)
                    act.activation(sg[:, e % 2, :], p_pair[e % 2][:, 0:NB * Q], ACT.Silu).then_inc(sx_ready, 1)
                    if e == 1:
                        route(c)
                    if p is not None:
                        if e == 2:
                            gates(p)
                            convolved_in(p)
                        if e == 4:
                            softplus(p)
                        if e == 6:
                            convolved_out(p)
                            b_on_tokens(p)

            def split_v(b):
                split(b, vt_done, p_out[1], v_h, (gu_done, NF), v_hi_ready, v_hi_tail)

            def split_x(b):
                split(b, xnt_done, p_out[1], x_h, (h13_done, NX), x_hi_ready, x_hi_tail)

            def body(p, f, b):
                if b is not None:
                    mixed(b)
                if f is not None:
                    scan(f, 0, None if b is None else lambda: split_v(b))
                elif b is not None:
                    split_v(b)
                if b is not None:
                    swiglu(b, p)
                elif p is not None:
                    pre_split(p)
                if f is not None and not later(f):
                    setup_rest()
                if f is not None:
                    scan(f, 1, None if b is None else lambda: split_x(b))
                elif b is not None:
                    split_x(b)
                if b is not None:
                    experts(b, p)
                elif p is not None:
                    gates(p)
                    convolved_in(p)
                    softplus(p)
                    convolved_out(p)
                    b_on_tokens(p)
                if p is not None:
                    decays(p)

            run(act, body)

        @block.vector
        def _(ve):
            pre_steps, front_steps, back_steps = Steps(PRE_V), Steps(FRONT_V), Steps(BACK_V)

            def setup():
                ve.wait_ge(in_small, 16 * N_SMALL)
                setup_steps = Steps(0)
                ve.tensor_scalar(tab_rest[:, 0, :], tab[:], EMB_SCALE, None, ALU.mult).then_inc(setup_v, 1)
                ve.wait_ge(setup_v, setup_steps.next(0))
                ve.tensor_copy(tab3[:, 0, :], tab_rest[:, 0, :]).then_inc(setup_v, 1)
                ve.wait_ge(setup_v, setup_steps.next(0))
                ve.tensor_tensor(tab_rest[:, 1, :], tab_rest[:, 0, :], tab3[:, 0, :], ALU.subtract).then_inc(setup_v, 1)
                ve.wait_ge(setup_v, setup_steps.next(0))
                ve.tensor_copy(tab3[:, 1, :], tab_rest[:, 1, :]).then_inc(setup_v, 1)
                ve.wait_ge(setup_v, setup_steps.next(0))
                ve.tensor_tensor(tab3[:, 2, :], tab_rest[:, 1, :], tab3[:, 1, :], ALU.subtract).then_inc(setup_v, 1)
                ve.wait_ge(setup_v, setup_steps.next(0))
                ve.tensor_copy(spread16[:], spread[:]).then_inc(setup_v, 1)
                ve.wait_ge(setup_v, setup_steps.next(0))
                ve.tensor_copy(upper16[:], upper[:]).then_inc(setup_v, 1)
                ve.wait_ge(setup_v, setup_steps.next(0))
                ve.memset(pa[:], 0.0).then_inc(setup_v, 1)
                ve.wait_ge(setup_v, setup_steps.next(0))
                ve.memset(pb[:], 0.0).then_inc(setup_v, 1)
                ve.wait_ge(setup_v, setup_steps.next(0))
                ve.memset(pa[0:1, :, :, HF:HF + 4], -1.0).then_inc(setup_v, 1)
                ve.wait_ge(setup_v, setup_steps.next(0))
                for b in range(NB):
                    for f in range(2):
                        ve.tensor_copy(ri[0:64, b, f], hrows[:].unsqueeze(2).to_broadcast([64, HF, Q])).then_inc(setup_v, 1)
                        ve.wait_ge(setup_v, setup_steps.next(0))
                        ve.tensor_copy(ri[64:128, b, f],
                                       mrows[64:128, :].unsqueeze(1).to_broadcast([64, HF, Q])).then_inc(setup_v, 1)
                        ve.wait_ge(setup_v, setup_steps.next(0))
                        ve.tensor_copy(lj[64:128, b, f], prows[64:128, :]).then_inc(setup_v, 1)
                        ve.wait_ge(setup_v, setup_steps.next(0))
                ve.wait_ge(in_w, 48)
                ve.wait_ge(w_in_hi, 2)
                ve.scalar_tensor_tensor(w_lo[:, 0:COL_G], w_raw[:, 0:COL_G], nrm[:, 0:1], w_hi[:, 0:COL_G],
                                        ALU.mult, ALU.subtract).then_inc(w_in_lo, 1)
                ve.scalar_tensor_tensor(wt_lo[:, 0:COL_G], wt_raw[0:DT, 0:COL_G], nrm[0:DT, 1:2], wt_hi[0:DT, 0:COL_G],
                                        ALU.mult, ALU.subtract).then_inc(w_in_lo, 1)

            def setup_rest():
                ve.wait_ge(in_late, 96)
                ve.wait_ge(w_rest_hi, 4)
                m, x = slice(COL_G, COL_E), slice(COL_E, COLS)
                ve.scalar_tensor_tensor(w_lo[:, m], w_raw[:, m], nrm[:, 2:3], w_hi[:, m],
                                        ALU.mult, ALU.subtract).then_inc(w_rest_lo, 1)
                ve.scalar_tensor_tensor(wt_lo[:, m], wt_raw[0:DT, m], nrm[0:DT, 3:4], wt_hi[0:DT, m],
                                        ALU.mult, ALU.subtract).then_inc(w_rest_lo, 1)
                ve.tensor_tensor(w_lo[:, x], w_raw[:, x], w_hi[:, x], ALU.subtract).then_inc(w_rest_lo, 1)
                ve.tensor_tensor(wt_lo[:, x], wt_raw[0:DT, x], wt_hi[0:DT, x], ALU.subtract).then_inc(w_rest_lo, 1)

            def split(c, head, tail, src, hi, lo, lo_ready, lo_tail):
                ve.wait_ge(head, c + 1)
                ve.wait_ge(tail, c + 1)
                ve.tensor_tensor(lo[:], src[:, 0:NB * Q], hi[:, 0, :], ALU.subtract).then_inc(lo_ready, 1)
                ve.tensor_tensor(hi[DT:128, 1, :], src[0:DT, NB * Q:2 * NB * Q], hi[0:DT, 1, :], ALU.subtract)\
                    .then_inc(lo_tail, 1)

            def pre_onehot(c):
                ve.wait_ge(tokens_in, c * 16 + 16)
                if later(c):
                    ve.wait_ge(emb_done, c)
                ve.tensor_scalar(onehot[:], tok[:], float(V - 1), ids[:, 0:1], ALU.min, ALU.is_equal)\
                    .then_inc(onehot_ready, 1)

            def pre_norm(c):
                ve.wait_ge(emb_done, c + 1)
                ve.wait_ge(position_in, c * 16 + 16)
                if later(c):
                    ve.wait_ge(h0_copied, c)
                ve.tensor_tensor(h0_next[:], p_misc[:, 0:NB * D].rearrange("p (b d) -> p b d", b=NB),
                                 pos[:].unsqueeze(1).to_broadcast([128, NB, D]), ALU.add).then_inc(h0_ready, 1)
                ve.wait_ge(h0_ready, c + 1)
                pre_steps.start()
                ve.bn_stats(stat[:, 0, :], h0_next[:, 0, :]).then_inc(pre_v, 1)
                ve.wait_ge(pre_v, pre_steps.next(c))
                ve.bn_stats(stat[:, 1, :], h0_next[:, 1, :]).then_inc(pre_v, 1)
                ve.wait_ge(pre_v, pre_steps.next(c))
                settle(ve)
                ve.bn_aggr(mv[:, 0, :], stat[:, 0, :]).then_inc(pre_v, 1)
                ve.wait_ge(pre_v, pre_steps.next(c))
                assert pre_steps.n == PRE_V
                settle(ve)
                ve.bn_aggr(mv[:, 1, :], stat[:, 1, :]).then_inc(stat_ready, 1)

            def pre_apply(c):
                ve.wait_ge(r0_ready, c + 1)
                if later(c):
                    ve.wait_ge(ut_done, c)
                ve.tensor_scalar(un[:, 0, :], h0_next[:, 0, :], mv[:, 0, 0:1], r0[:, 0:1], ALU.subtract, ALU.mult)
                ve.tensor_scalar(un[:, 1, :], h0_next[:, 1, :], mv[:, 1, 0:1], r0[:, 1:2], ALU.subtract, ALU.mult)\
                    .then_inc(un_ready, 1)

            def pre_split(c):
                split(c, u_hi_ready, u_hi_tail, p_misc, u_h, u_l, u_lo_ready, u_lo_tail)

            def convolve(c, tiles, starts):
                if starts:
                    front_steps.start()
                    if later(c):
                        ve.wait_ge(xs_ready, c)
                        ve.wait_ge(b_ready, c)
                        ve.wait_ge(c_ready, c)
                        ve.wait_ge(halo_kept, c)
                    ve.wait_ge(xr_ready[0], c + 1)
                    ve.wait_ge(xr_ready[1], c + 1)
                for m in tiles:
                    ve.tensor_scalar(xa[:, m], xr[:, m, :, 0:Q], cw_[:, m, 0:1], cb_[:, m:m + 1],
                                     ALU.mult, ALU.add).then_inc(front_v, 1)
                    front_steps.next(c)
                for k in range(1, KC):
                    for m in tiles:
                        ve.wait_ge(front_v, front_steps.back(c, len(tiles) - 1))
                        last = k == KC - 1 and m == NM - 1
                        ve.scalar_tensor_tensor(xa[:, m], xr[:, m, :, k:k + Q], cw_[:, m, k:k + 1], xa[:, m],
                                                ALU.mult, ALU.add).then_inc(xa_ready if last else front_v, 1)
                        if not last:
                            front_steps.next(c)

            def steps_dt(c):
                ve.wait_ge(z_ready[1], c + 1)
                ve.tensor_tensor(dx[:], p_misc[:, 256:256 + NB * NH].rearrange("p (b h) -> p b h", b=NB),
                                 dtb[:].unsqueeze(1).to_broadcast([128, NB, NH]), ALU.add).then_inc(dx_ready, 1)
                ve.wait_ge(dx_ready, c + 1)
                ve.scalar_tensor_tensor(dn[:], dx[:], -1.0, dx[:], ALU.mult, ALU.min).then_inc(dn_ready, 1)

            def halves(t):
                return t[:].rearrange("p b (f h) -> p b f h", f=2)

            def steps_decay(c):
                ve.wait_ge(dl_ready, c + 1)
                if later(c):
                    ve.wait_ge(cum_done, c)
                ve.scalar_tensor_tensor(dt_[:], dx[:], 0.0, dl[:], ALU.max, ALU.add).then_inc(front_v, 1)
                ve.wait_ge(front_v, front_steps.next(c))
                ve.tensor_tensor(ap_[:], dt_[:], aexp[:].unsqueeze(1).to_broadcast([128, NB, NH]), ALU.mult).then_inc(front_v, 1)
                ve.wait_ge(front_v, front_steps.next(c))
                ve.tensor_scalar(ag_[:], ap_[:], DEAD, ROUND, ALU.min, ALU.add).then_inc(front_v, 1)
                ve.wait_ge(front_v, front_steps.next(c))
                ve.tensor_scalar(pa[:, :, :, 0:HF], halves(ag_), ROUND, None, ALU.subtract).then_inc(front_v, 1)
                ve.wait_ge(front_v, front_steps.next(c))
                ve.tensor_scalar(ag_[:], ap_[:], DEAD, None, ALU.min).then_inc(front_v, 1)
                ve.wait_ge(front_v, front_steps.next(c))
                ve.tensor_tensor(halves(ar_), halves(ag_), pa[:, :, :, 0:HF], ALU.subtract).then_inc(front_v, 1)
                ve.wait_ge(front_v, front_steps.next(c))
                ve.tensor_copy(pa[:, :, :, 16:16 + HF], halves(ar_)).then_inc(front_v, 1)
                ve.wait_ge(front_v, front_steps.next(c))
                ve.tensor_tensor(pb[:, :, :, 16:16 + HF], halves(ar_), pa[:, :, :, 16:16 + HF], ALU.subtract).then_inc(pab_ready, 1)
                assert front_steps.n == FRONT_V, front_steps.n

            def masked_g(c):
                ve.wait_ge(bt_ready, c + 1)
                ve.tensor_tensor(gm[:], p_y[:, 0:NB * Q].rearrange("p (b i) -> p b i", b=NB),
                                 upper[:].unsqueeze(1).to_broadcast([128, NB, Q]), ALU.mult).then_inc(gm_ready, 1)

            def operands(c):
                ve.wait_ge(cum_done, c + 1)
                if later(c):
                    ve.wait_ge(d_done, c * NR)
                if later(c):
                    ve.wait_ge(sums_out, c * 16)
                part = [p_misc[32 * f:32 * (f + 1), 0:NB * Q].rearrange("p (b i) -> p b i", b=NB) for f in range(2)]
                ve.tensor_copy(lj[0:32, :, 0, :], part[0])
                ve.tensor_copy(lj[0:32, :, 1, :], part[1]).then_inc(lj_high, 1)
                ve.wait_ge(lj_high, c + 1)
                ve.tensor_tensor(lj[32:64, :, 0, :], part[0], lj[0:32, :, 0, :], ALU.subtract)
                ve.tensor_tensor(lj[32:64, :, 1, :], part[1], lj[0:32, :, 1, :], ALU.subtract).then_inc(lj_ready, 1)

            def scaled_x(c, b):
                ve.wait_ge(xt_done[b], c + 1)
                if later(c):
                    ve.wait_ge(xw_ready, c * NR)
                    ve.wait_ge(yq_done, c * NR)
                blocks = xd[:, b].rearrange("p (g o) (s d) -> p g (o s) d", o=2, s=2)[:, :, 0:4:3, :]
                ve.tensor_tensor(blocks, p_d[b][:, 0:DI].rearrange("p (g o d) -> p g o d", o=2, d=HD),
                                 dt_[:, b, :].rearrange("p (g o) -> p g o", o=2).unsqueeze(3)
                                 .to_broadcast([128, NH // 2, 2, HD]), ALU.mult).then_inc(xd_ready[b], 1)

            def skipped_x(c):
                ve.wait_ge(xs_ready, c + 1)
                if later(c):
                    ve.wait_ge(t1_sum[1], c)
                for k in range(KT):
                    ins = ve.tensor_scalar(xk[:, k], xs[:, k], dsk[:, k:k + 1], None, ALU.mult)
                ins.then_inc(xk_ready, 1)

            def scan(c, b, between):
                ve.wait_ge(yi_done[b], c + 1)
                ve.wait_ge(ecx_ready[0], c + 1)
                ve.wait_ge(ecx_ready[1], c + 1)
                if later(c):
                    ve.wait_ge(y_sum[b], c)
                ve.tensor_tensor(t1[:, b], p_misc[:, 0:DI].rearrange("p (k i) -> p k i", k=KT), ecx[:, :, b, :],
                                 ALU.mult).then_inc(t1_ready[b], 1)
                for q in range(NQ):
                    r = b * NQ + q
                    ve.wait_ge(e_ready, c * NR + r + 1)
                    if q == 0:
                        ve.wait_ge(gm_ready, c + 1)
                    if later(c) or r - NER + 1 > 0:
                        ve.wait_ge(yq_done, c * NR + r - NER + 1)
                    ve.scalar_tensor_tensor(mr[:, r % NER], er[:, r % NER], 1.0,
                                            gm[:, b, :].unsqueeze(1).to_broadcast([128, HG, Q]), ALU.min, ALU.mult)\
                        .then_inc(m_ready, 1)
                    if q in between:
                        between[q]()
                ve.wait_ge(sn_done[b], c + 1)
                ve.wait_ge(s_decayed[b], c + 1)
                ve.tensor_tensor(state[:, b, :], state[:, b, :], p_misc[0:NS, 0:DI], ALU.add).then_inc(s_ready[b], 1)
                ve.wait_ge(t1_sum[b], c + 1)
                ve.wait_ge(yq_done, c * NR + (b + 1) * NQ)
                if later(c):
                    ve.wait_ge(m_out, c)
                ve.tensor_tensor(y[:, b], p_y[:, 0:DI].rearrange("p (k i) -> p k i", k=KT), t1[:, b], ALU.add)\
                    .then_inc(y_sum[b], 1)

            def mixed(c):
                ve.wait_ge(rm_ready, c + 1)
                if later(c):
                    ve.wait_ge(vt_done, c)
                for b in range(NB):
                    ins = ve.tensor_scalar(vn[:, b, :], p_out[0][:, b * D:(b + 1) * D], rm[:, b:b + 1], None, ALU.mult)
                ins.then_inc(vn_ready, 1)
                ve.wait_ge(h0_copied, c + 1)
                if later(c):
                    ve.wait_ge(h1_ready, c)
                ve.tensor_tensor(hm[:], p_out[0][:, 0:NB * D].rearrange("p (b d) -> p b d", b=NB), h0[:], ALU.add)\
                    .then_inc(hm_ready, 1)

            def swiglu(c, p):
                for f in range(NF):
                    ve.wait_ge(sg_ready, c * NF + f + 1)
                    if f == 0:
                        if later(c):
                            ve.wait_ge(mlp_done, c)
                    ve.tensor_tensor(gt[:, f, :], sg[:, f % 2, :], p_pair[f % 2][:, NB * Q:2 * NB * Q], ALU.mult)\
                        .then_inc(gt_ready, 1)
                    if p is not None:
                        if f == 0:
                            pre_norm(p)
                        if f == 2:
                            pre_apply(p)
                        if f == 4:
                            pre_split(p)

            def norm2(c):
                back_steps.start()
                ve.wait_ge(mlp_done, c + 1)
                if later(c):
                    ve.wait_ge(acc_done, c * NX)
                ve.tensor_tensor(h1[:], p_out[0][:, 0:NB * D].rearrange("p (b d) -> p b d", b=NB), hm[:], ALU.add)\
                    .then_inc(h1_ready, 1)
                ve.wait_ge(h1_ready, c + 1)
                ve.bn_stats(stat2[:, 0, :], h1[:, 0, :]).then_inc(back_v, 1)
                ve.wait_ge(back_v, back_steps.next(c))
                ve.bn_stats(stat2[:, 1, :], h1[:, 1, :]).then_inc(back_v, 1)
                ve.wait_ge(back_v, back_steps.next(c))
                settle(ve)
                ve.bn_aggr(mv2[:, 0, :], stat2[:, 0, :]).then_inc(back_v, 1)
                ve.wait_ge(back_v, back_steps.next(c))
                settle(ve)
                ve.bn_aggr(mv2[:, 1, :], stat2[:, 1, :]).then_inc(stat2_ready, 1)

            def norm2_apply(c):
                ve.wait_ge(r2_ready, c + 1)
                if later(c):
                    ve.wait_ge(xnt_done, c)
                for b in range(NB):
                    ins = ve.tensor_scalar(xn[:, b, :], h1[:, b, :], mv2[:, b, 0:1], r2[:, b:b + 1], ALU.subtract, ALU.mult)
                ins.then_inc(xn_ready, 1)

            def ranks(c, s, n, before, gt_, ge_, rank):
                other = s.unsqueeze(2).to_broadcast([128, NB, n, n])
                own = s.unsqueeze(3).to_broadcast([128, NB, n, n])
                prior = before[:].unsqueeze(1).to_broadcast([128, NB, n, n])
                ve.tensor_tensor(gt_[:], other, own, ALU.is_gt).then_inc(back_v, 1)
                ve.wait_ge(back_v, back_steps.next(c))
                ve.tensor_tensor(ge_[:], other, own, ALU.is_ge).then_inc(back_v, 1)
                ve.wait_ge(back_v, back_steps.next(c))
                ve.tensor_tensor(ge_[:], ge_[:], prior, ALU.mult).then_inc(back_v, 1)
                ve.wait_ge(back_v, back_steps.next(c))
                ve.tensor_tensor(gt_[:], gt_[:], ge_[:], ALU.max).then_inc(back_v, 1)
                ve.wait_ge(back_v, back_steps.next(c))
                if rank is not None:
                    ve.reduce_sum(rank[:], gt_[:], AX_X).then_inc(back_v, 1)
                    ve.wait_ge(back_v, back_steps.next(c))

            def route_scores(c):
                ve.wait_ge(th_ready, c + 1)
                ve.tensor_scalar(sc[:], th[:], 0.5, 0.5, ALU.mult, ALU.add).then_inc(back_v, 1)
                ve.wait_ge(back_v, back_steps.next(c))
                ve.tensor_tensor(sv[:], sc[:], gbias[:].unsqueeze(1).to_broadcast([128, NB, NE]), ALU.add).then_inc(back_v, 1)
                ve.wait_ge(back_v, back_steps.next(c))
                pairs = sv[:].rearrange("p b (g j) -> p b g j", j=GE)
                ve.tensor_tensor(gs[:], pairs[:, :, :, 0], pairs[:, :, :, 1], ALU.add).then_inc(back_v, 1)
                ve.wait_ge(back_v, back_steps.next(c))

            def route_groups(c):
                ranks(c, gs[:], NG, before4, g_gt, g_ge, g_rank)
                ve.tensor_scalar(g_on[:], g_rank[:].unsqueeze(3).to_broadcast([128, NB, NG, GE]), 1.5, None,
                                 ALU.is_lt).then_inc(back_v, 1)
                ve.wait_ge(back_v, back_steps.next(c))

            def route_experts(c):
                on = g_on[:].rearrange("p b g j -> p b (g j)")
                ranks(c, sv[:], NE, before8, e_gt, e_ge, None)
                ve.tensor_tensor(e_gt[:], e_gt[:], on.unsqueeze(2).to_broadcast([128, NB, NE, NE]), ALU.mult).then_inc(back_v, 1)
                ve.wait_ge(back_v, back_steps.next(c))
                ve.reduce_sum(e_rank[:], e_gt[:], AX_X).then_inc(back_v, 1)
                ve.wait_ge(back_v, back_steps.next(c))
                ve.scalar_tensor_tensor(e_on[:].rearrange("p b e -> p (b e)"),
                                        e_rank[:].rearrange("p b e -> p (b e)"), 1.5,
                                        g_on[:].rearrange("p b g j -> p (b g j)"), ALU.is_lt, ALU.mult).then_inc(back_v, 1)
                ve.wait_ge(back_v, back_steps.next(c))
                ve.tensor_tensor(e_w[:], e_on[:], sc[:], ALU.mult).then_inc(back_v, 1)
                ve.wait_ge(back_v, back_steps.next(c))
                ve.reduce_sum(e_sum[:], e_w[:], AX_X).then_inc(back_v, 1)
                ve.wait_ge(back_v, back_steps.next(c))
                ve.tensor_scalar(e_sum1[:], e_sum[:], 1e-6, None, ALU.add).then_inc(back_v, 1)
                ve.wait_ge(back_v, back_steps.next(c))
                ve.reciprocal(e_inv[:], e_sum1[:]).then_inc(back_v, 1)
                ve.wait_ge(back_v, back_steps.next(c))
                ve.tensor_tensor(cw[:], e_w[:], e_inv[:].unsqueeze(2).to_broadcast([128, NB, NE]), ALU.mult)\
                    .then_inc(cw_ready, 1)
                assert back_steps.n == BACK_V, back_steps.n

            def weigh(c, e):
                ve.wait_ge(ex_done, c * NX + e + 1)
                p = p_out[(e + 1) % 2]
                if e == 0:
                    if later(c):
                        ve.wait_ge(out_written, c * 16)
                    ve.tensor_tensor(acc[:], p[:, 0:NB * D].rearrange("p (b d) -> p b d", b=NB), h1[:], ALU.add)\
                        .then_inc(acc_done, 1)
                    return
                if e == 1:
                    ve.wait_ge(cw_ready, c + 1)
                ve.wait_ge(acc_done, c * NX + e)
                for b in range(NB):
                    ins = ve.scalar_tensor_tensor(acc[:, b, :], p[:, b * D:(b + 1) * D], cw[:, b, e - 1:e], acc[:, b, :],
                                                  ALU.mult, ALU.add)
                ins.then_inc(acc_done, 1)

            def experts(c, p):
                for e in range(NX):
                    ve.wait_ge(sx_ready, c * NX + e + 1)
                    if e >= NHH:
                        ve.wait_ge(ex_done, c * NX + e - NHH + 1)
                    else:
                        if later(c):
                            ve.wait_ge(ex_done, c * NX)
                    ve.tensor_tensor(hh[:, e % NHH, :], sg[:, e % 2, :], p_pair[e % 2][:, NB * Q:2 * NB * Q], ALU.mult)\
                        .then_inc(hh_ready, 1)
                    if e == 0:
                        route_scores(c)
                    if e == 1:
                        route_groups(c)
                    if e >= 2:
                        weigh(c, e - 2)
                    if e == 2:
                        route_experts(c)
                    if p is not None:
                        if e == 3:
                            steps_dt(p)
                            convolve(p, (0, 1), True)
                        if e == 4:
                            convolve(p, (2, 3), False)
                        if e == 5:
                            steps_decay(p)
                        if e == 7:
                            scaled_x(p, 0)
                            scaled_x(p, 1)
                            operands(p)
                weigh(c, NX - 2)
                weigh(c, NX - 1)

            def split_v(b):
                split(b, v_hi_ready, v_hi_tail, p_out[1], v_h, v_l, v_lo_ready, v_lo_tail)

            def split_x(b):
                split(b, x_hi_ready, x_hi_tail, p_out[1], x_h, x_l, x_lo_ready, x_lo_tail)

            def body(p, f, b):
                if p is not None:
                    pre_onehot(p)
                if f is not None:
                    scan(f, 0, {} if b is None else {1: lambda: mixed(b), 4: lambda: split_v(b)})
                elif b is not None:
                    mixed(b)
                    split_v(b)
                if b is not None:
                    swiglu(b, p)
                    norm2(b)
                elif p is not None:
                    pre_norm(p)
                    pre_apply(p)
                    pre_split(p)
                if f is not None and not later(f):
                    setup_rest()
                if f is not None:
                    scan(f, 1, {} if b is None else {1: lambda: norm2_apply(b), 4: lambda: split_x(b)})
                elif b is not None:
                    norm2_apply(b)
                    split_x(b)
                if b is not None:
                    experts(b, p)
                elif p is not None:
                    steps_dt(p)
                    convolve(p, (0, 1), True)
                    convolve(p, (2, 3), False)
                    steps_decay(p)
                    scaled_x(p, 0)
                    scaled_x(p, 1)
                    operands(p)
                if p is not None:
                    masked_g(p)
                    skipped_x(p)

            setup()
            run(ve, body)

        @block.tensor
        def _(pe):
            def split_products(out_, cols, hi, lo, toks, weights_first):
                parts = ((w_hi[:, cols], hi[:, 0, toks]), (wt_hi[:, cols], hi[:, 1, toks]), (w_hi[:, cols], lo[:, toks]),
                         (w_lo[:, cols], hi[:, 0, toks]), (wt_lo[:, cols], hi[0:DT, 1, toks]))
                for i, (w, x) in enumerate(parts):
                    a, b = (w, x) if weights_first else (x, w)
                    ins = pe.matmul(out_, a, b, start=(i == 0), stop=(i == len(parts) - 1))
                return ins

            def transpose_channels(dst, src, done):
                for b in range(NB):
                    pe.transpose(dst[:, b * Q:(b + 1) * Q], src[:, b, 0:DH], idf[:])
                for b in range(NB):
                    ins = pe.transpose(dst[0:DT, (NB + b) * Q:(NB + b + 1) * Q], src[:, b, DH:D], idf[:])
                ins.then_inc(done, 1)

            def pre_embed(c):
                if not later(c):
                    pe.wait_ge(setup_v, 10 + 6 * NB)
                pe.wait_ge(onehot_ready, c + 1)
                if later(c):
                    pe.wait_ge(s_ready[0], c)
                settle(pe)
                for b in range(NB):
                    for k in range(3):
                        ins = pe.matmul(p_misc[:, b * D:(b + 1) * D], onehot[:, b, :], tab3[:, k, :],
                                        start=(k == 0), stop=(k == 2))
                ins.then_inc(emb_done, 1)

            def pre_turn(c):
                pe.wait_ge(un_ready, c + 1)
                transpose_channels(p_misc, un, ut_done)

            def project_in(c):
                if not later(c):
                    pe.wait_ge(w_in_hi, 2)
                    pe.wait_ge(w_in_lo, 2)
                pe.wait_ge(u_hi_ready, c + 1)
                pe.wait_ge(u_hi_tail, c + 1)
                pe.wait_ge(u_lo_ready, c + 1)
                pe.wait_ge(u_lo_tail, c + 1)
                if later(c):
                    pe.wait_ge(e_ready, c * NR)
                if later(c):
                    pe.wait_ge(y_sum[1], c)
                settle(pe)
                for i in range(2):
                    for j in range(2):
                        col = COL_X + (2 * i + j) * 128
                        ins = split_products(p_d[i][:, j * NB * Q:(j + 1) * NB * Q], slice(col, col + 128),
                                             u_h, u_l, slice(0, NB * Q), True)
                    ins.then_inc(x_done[i], 1)
                for k in range(KT):
                    ins = split_products((p_y, p_misc)[k // 2][:, k % 2 * NB * Q:(k % 2 + 1) * NB * Q],
                                         slice(k * 128, (k + 1) * 128), u_h, u_l, slice(0, NB * Q), True)
                    if k == 1:
                        ins.then_inc(z_done[0], 1)
                for b in range(NB):
                    ins = split_products(p_misc[:, 256 + b * NH:256 + (b + 1) * NH], slice(DI, ZD), u_h, u_l,
                                         slice(b * Q, (b + 1) * Q), False)
                ins.then_inc(z_done[1], 1)

            def scan_operands(c):
                pe.wait_ge(xs_ready, c + 1)
                pe.wait_ge(b_ready, c + 1)
                pe.wait_ge(c_ready, c + 1)
                pe.wait_ge(z_ready[0], c + 1)
                settle(pe)
                for b in range(NB):
                    for m in range(KT):
                        ins = pe.transpose(p_d[b][:, m * 128:(m + 1) * 128], xs[:, m, b, :], idf[:])
                    ins.then_inc(xt_done[b], 1)
                for b in range(NB):
                    pe.matmul(p_y[:, b * Q:(b + 1) * Q], bc[:, b, :], cc[:, b, :], start=True, stop=True)
                for b in range(NB):
                    ins = pe.transpose(p_y[:, 256 + b * NS:256 + (b + 1) * NS], bc[:, b, :], idf[0:NS, 0:NS])
                ins.then_inc(g_done, 1)

            def running_sums(c):
                pe.wait_ge(pab_ready, c + 1)
                settle(pe)
                for b in range(NB):
                    for i, part in enumerate((pa, pb)):
                        pe.matmul(p_misc[0:64, b * Q:(b + 1) * Q], part[:, b].rearrange("p f r -> p (f r)"), upper16[:],
                                  start=(i == 0), stop=(i == 1))
                o = p_misc[0:NS, 256:256 + NB * NH]
                pe.matmul(o, ones16[:], pa[:, :, :, 0:HF], start=True, stop=False)
                pe.matmul(o, ones16[:], pa[:, :, :, 16:16 + HF], start=False, stop=False)
                pe.matmul(o, ones16[:], pb[:, :, :, 16:16 + HF], start=False, stop=True).then_inc(cum_done, 1)

            def sums_on_channels(c):
                pe.wait_ge(lj_ready, c + 1)
                pe.wait_ge(xd_ready[0], c + 1)
                pe.wait_ge(xd_ready[1], c + 1)
                settle(pe)
                for k, halves in enumerate(((0,), (0, 1), (1,))):
                    for f in halves:
                        ins = pe.matmul(p_d[k // 2][:, k % 2 * NB * Q:(k % 2 + 1) * NB * Q], spread16[:, k, f, :],
                                        lj[0:64, :, f, :], start=(f == halves[0]), stop=(f == halves[-1]))
                    if k >= 1:
                        ins.then_inc(cumx_done[k - 1], 1)

            def exponents(c, r):
                b, q = divmod(r, NQ)
                f, g = divmod(q, NQ // 2)
                if r == 0:
                    pe.wait_ge(ri_in, c * 64 + 64)
                if r < 2:
                    pe.wait_ge(ecx_ready[r], c + 1)
                else:
                    pe.wait_ge(e_ready, c * NR + r - 1)
                pe.matmul(p_d[r % 2][:], lj[:, b, f, :], ri[:, b, f, g * HG:(g + 1) * HG, :].rearrange("p h i -> p (h i)"),
                          start=True, stop=True).then_inc(d_done, 1)

            def scan(c, b, between, p=None):
                if p is not None:
                    pe.wait_ge(u_lo_ready, p + 1)
                    pe.wait_ge(u_lo_tail, p + 1)
                if b == 0:
                    pe.wait_ge(eend_ready, c + 1)
                    pe.wait_ge(gm_ready, c + 1)
                    pe.wait_ge(bt_ready, c + 1)
                else:
                    pe.wait_ge(s_ready[0], c + 1)
                    pe.wait_ge(y_sum[0], c + 1)
                if later(c):
                    pe.wait_ge(s_ready[b], c)
                settle(pe)
                if b == 0:
                    exponents(c, 0)
                    exponents(c, 1)
                for k in range(KT):
                    ins = pe.matmul(p_misc[:, k * Q:(k + 1) * Q], state[:, b, k * 128:(k + 1) * 128], cc[:, b, :],
                                    start=True, stop=True)
                ins.then_inc(yi_done[b], 1)
                for q in range(NQ):
                    r = b * NQ + q
                    pe.wait_ge(m_ready, c * NR + r + 1)
                    for h in range(q * HG, (q + 1) * HG):
                        row = h * HD % 128 // 32 * 32
                        k = h * HD // 128
                        ins = pe.matmul(p_y[row:row + 32, k * Q:(k + 1) * Q], xd[:, b, h, :], mr[:, r % NER, h % HG, :],
                                        start=(h % 2 == 0), stop=(h % 2 == 1))
                    ins.then_inc(yq_done, 1)
                    if r + 2 < NR:
                        exponents(c, r + 2)
                    if q in between:
                        between[q]()
                pe.wait_ge(xw_ready, c * NR + (b + 1) * NQ)
                pe.wait_ge(t1_ready[b], c + 1)
                settle(pe)
                pe.matmul(p_misc[0:NS, 0:DI], bt[:, b, :], xw[:, b, :], start=True, stop=True).then_inc(sn_done[b], 1)

            def project_out(c):
                if not later(c):
                    pe.wait_ge(in_late, 96)
                pe.wait_ge(y_ready[0], c + 1)
                pe.wait_ge(y_ready[1], c + 1)
                if later(c):
                    pe.wait_ge(acc_done, c * NX)
                for b in range(NB):
                    for k in range(DI // 128):
                        ins = pe.matmul(p_out[0][:, b * D:(b + 1) * D], y[:, b, k, :], wo[:, k, :],
                                        start=(k == 0), stop=(k == DI // 128 - 1))
                ins.then_inc(m_out, 1)

            def turn_v(c):
                pe.wait_ge(vn_ready, c + 1)
                transpose_channels(p_out[1], vn, vt_done)

            def swiglu(c, p):
                if not later(c):
                    pe.wait_ge(w_rest_hi, 4)
                    pe.wait_ge(w_rest_lo, 4)
                pe.wait_ge(v_hi_ready, c + 1)
                pe.wait_ge(v_hi_tail, c + 1)
                pe.wait_ge(v_lo_ready, c + 1)
                pe.wait_ge(v_lo_tail, c + 1)
                pe.wait_ge(hm_ready, c + 1)

                def down(f):
                    pe.wait_ge(gt_ready, c * NF + f + 1)
                    for b in range(NB):
                        ins = pe.matmul(p_out[0][:, b * D:(b + 1) * D], gt[:, f, b * Q:(b + 1) * Q], wd[:, f, :],
                                        start=(f == 0 and b == 0), stop=(f == NF - 1), skip_group_check=True)
                    if f == NF - 1:
                        ins.then_inc(mlp_done, 1)

                for f in range(NF):
                    if f >= 2:
                        pe.wait_ge(gt_ready, c * NF + f - 1)
                    else:
                        if later(c):
                            pe.wait_ge(hh_ready, c * NX)
                    o = p_pair[f % 2]
                    split_products(o[:, 0:NB * Q], slice(COL_G + f * 128, COL_G + (f + 1) * 128), v_h, v_l,
                                   slice(0, NB * Q), True)
                    split_products(o[:, NB * Q:2 * NB * Q], slice(COL_U + f * 128, COL_U + (f + 1) * 128), v_h, v_l,
                                   slice(0, NB * Q), True).then_inc(gu_done, 1)
                    if f == 2 and p is not None:
                        pre_turn(p)
                    if f >= 2:
                        down(f - 2)
                down(NF - 2)
                down(NF - 1)

            def turn_x(c):
                pe.wait_ge(xn_ready, c + 1)
                transpose_channels(p_out[1], xn, xnt_done)

            def experts(c, p):
                pe.wait_ge(x_hi_ready, c + 1)
                pe.wait_ge(x_hi_tail, c + 1)
                pe.wait_ge(x_lo_ready, c + 1)
                pe.wait_ge(x_lo_tail, c + 1)
                pe.wait_ge(h1_ready, c + 1)
                settle(pe)
                for b in range(NB):
                    ins = split_products(p_out[0][:, b * NE:(b + 1) * NE], slice(COL_R, COLS), x_h, x_l,
                                         slice(b * Q, (b + 1) * Q), False)
                ins.then_inc(router_done, 1)

                def down(e):
                    pe.wait_ge(hh_ready, c * NX + e + 1)
                    if e == 1:
                        pe.wait_ge(th_ready, c + 1)
                    if e >= 2:
                        pe.wait_ge(acc_done, c * NX + e - 1)
                    for b in range(NB):
                        ins = pe.matmul(p_out[(e + 1) % 2][:, b * D:(b + 1) * D], hh[:, e % NHH, b * Q:(b + 1) * Q],
                                        w2t[:, e, :], start=True, stop=True)
                    ins.then_inc(ex_done, 1)

                for e in range(NX):
                    if e >= 2:
                        pe.wait_ge(hh_ready, c * NX + e - 1)
                    else:
                        pe.wait_ge(gt_ready, c * NF + NF - 1 + e)
                    o, col = p_pair[e % 2], COL_E + e * 2 * NI
                    split_products(o[:, 0:NB * Q], slice(col, col + NI), x_h, x_l, slice(0, NB * Q), True)
                    split_products(o[:, NB * Q:2 * NB * Q], slice(col + NI, col + 2 * NI), x_h, x_l,
                                   slice(0, NB * Q), True).then_inc(h13_done, 1)
                    if p is not None:
                        if e == 1:
                            project_in(p)
                        if e == 6:
                            running_sums(p)
                        if e == 7:
                            scan_operands(p)
                    if e >= 2:
                        down(e - 2)
                down(NX - 2)
                down(NX - 1)

            def body(p, f, b):
                if b is not None:
                    project_out(b)
                if f is not None:
                    scan(f, 0, {} if b is None else {3: lambda: turn_v(b)})
                elif b is not None:
                    turn_v(b)
                if p is not None:
                    pre_embed(p)
                if b is not None:
                    swiglu(b, p)
                elif p is not None:
                    pre_turn(p)
                if f is not None:
                    scan(f, 1, {} if b is None else {3: lambda: turn_x(b)}, p)
                elif b is not None:
                    turn_x(b)
                if b is not None:
                    experts(b, p)
                elif p is not None:
                    project_in(p)
                    running_sums(p)
                    scan_operands(p)
                if p is not None:
                    sums_on_channels(p)

            pe.wait_ge(in_small, 16 * N_SMALL)
            pe.wait_ge(setup_p, 5)
            run(pe, body)


N_SMALL = 22


def kernel(x, L0_tok_color_W, L0_tok_shape_W, L0_tok_quantity_W, L0_tok_special_W, L0_attn_norm1_w,
           L0_attn_in_proj_w, L0_attn_conv_w, L0_attn_conv_b, L0_attn_dt_bias, L0_attn_A_log, L0_attn_D,
           L0_attn_out_proj_w, L0_attn_norm2_w, L0_attn_w_gate, L0_attn_w_up, L0_attn_w_down, L0_ffn_gate_weight,
           L0_ffn_gate_bias, L0_ffn_w1, L0_ffn_w2, L0_ffn_w3, L0_ffn_sw1, L0_ffn_sw2, L0_ffn_sw3):
    import numpy as np
    import concourse.bacc as bacc
    from concourse.bass_utils import run_bass_kernel_spmd

    f32 = np.float32
    rate = np.exp(-(np.arange(0, D, 2, dtype=f32) / f32(D)) * f32(np.log(10000.0)))
    angle = np.arange(L, dtype=f32)[:, None] * rate.astype(f32)
    position = np.stack([np.sin(angle), np.cos(angle)], axis=-1).reshape(L, D).astype(f32)
    head_rows = np.zeros((64, HF), f32)
    for g in range(4):
        for h in range(HF):
            head_rows[16 * g + h, h] = 1.0
    spread_rows = np.zeros((64, KT, 2, 128), f32)
    for channel in range(DI):
        half, head = divmod(channel // HD, HF)
        spread_rows[head::16, channel // 128, half, channel % 128] = 1.0
    token, pair = np.arange(Q)[None, :], np.arange(Q // 2)[:, None]
    mask_rows = np.where(token < 2 * pair, f32(FAR), f32(0)).astype(f32)
    pair_rows = (token // 2 == pair).astype(f32)
    ids = np.arange(64)
    features = np.concatenate([L0_tok_color_W[ids // 16], L0_tok_shape_W[ids % 16 // 4], L0_tok_quantity_W[ids % 4]],
                              axis=1)
    z, xbc, dt = np.split(np.asarray(L0_attn_in_proj_w), [DI, 2 * DI + 2 * NS], axis=1)
    columns = [z, dt, xbc, L0_attn_w_gate, L0_attn_w_up, np.transpose(L0_ffn_sw1), np.transpose(L0_ffn_sw3)]
    for e in range(NE):
        columns += [np.transpose(L0_ffn_w1[e]), np.transpose(L0_ffn_w3[e])]
    columns.append(np.transpose(L0_ffn_gate_weight))
    w2 = np.concatenate([np.transpose(L0_ffn_sw2)[:, None, :], np.transpose(L0_ffn_w2, (2, 0, 1))], axis=1)
    arrays = {
        "tokens": x, "position": position, "vocab_ids": np.arange(V, dtype=f32)[:, None],
        "table": np.concatenate([features, L0_tok_special_W], axis=0),
        "weights": np.concatenate(columns, axis=1),
        "norm1": np.reshape(L0_attn_norm1_w, (D, 1)), "norm2": np.reshape(L0_attn_norm2_w, (D, 1)),
        "conv_w": np.transpose(np.reshape(L0_attn_conv_w, (NM, 128, KC)), (1, 0, 2)),
        "conv_b": np.transpose(np.reshape(L0_attn_conv_b, (NM, 128))),
        "dt_bias": L0_attn_dt_bias, "a_log": L0_attn_A_log, "d_skip": np.transpose(np.reshape(np.repeat(np.asarray(L0_attn_D), HD), (KT, 128))),
        "w_out": np.transpose(np.reshape(L0_attn_out_proj_w, (DI // 128, 128, D)), (1, 0, 2)),
        "w_down": np.transpose(np.reshape(L0_attn_w_down, (NF, 128, D)), (1, 0, 2)),
        "w2": w2, "gate_bias": L0_ffn_gate_bias,
        "identity": np.eye(128, dtype=f32), "lower_ones": np.triu(np.ones((128, 128), f32)),
        "head_rows": head_rows, "mask_rows": mask_rows, "pair_rows": pair_rows,
        "spread_rows": spread_rows,
        "order8": np.tril(np.ones((NE, NE), f32), -1), "order4": np.tril(np.ones((NG, NG), f32), -1),
    }
    nc = bacc.Bacc("TRN2", target_bir_lowering=False, num_devices=1)
    args = []
    for name, a in arrays.items():
        arrays[name] = a = np.ascontiguousarray(a)
        args.append(nc.dram_tensor(name, a.shape, mybir.dt.from_np(a.dtype), kind="ExternalInput").ap())
    args.append(nc.dram_tensor("out", (NB, L, D), F32, kind="ExternalOutput").ap())
    program(nc, *args)
    r = run_bass_kernel_spmd(nc, [arrays], core_ids=[0])
    return r.results[0]["out"]
```

```python
from contextlib import ExitStack

import concourse.bass as bass
from concourse import mybir

ALU = mybir.AluOpType
ACT = mybir.ActivationFunctionType
AX_X = mybir.AxisListType.X
F32 = mybir.dt.float32
F16 = mybir.dt.float16
BF16 = mybir.dt.bfloat16
I32 = mybir.dt.int32

NB = 2
L = 2048
Q = 128
NC = L // Q
D = 192
DH, DT = 128, D - 128
V = 70
DI = 384
NH, HD = 24, 16
NS = 64
KC = 4
NM = (DI + 2 * NS) // 128
DM = 768
NF = DM // 128
NE, NI = 8, 128
NG, GE = 4, 2
HG = 4
NQ = NH // HG
KT = DI // 128
ZD = DI + NH
COL_X = ZD
COL_G = COL_X + NM * 128
COL_U = COL_G + DM
COL_E = COL_U + DM
COL_R = COL_E + (NE + 1) * 2 * NI
COLS = COL_R + NE
HF = NH // 2
STEP = 1.0 / 16
ROUND = 1.5 * 2.0 ** 23 * STEP
DEAD = 88.0
FAR = -12000.0
EMB_SCALE = float(D) ** 0.5

PRE_V, FRONT_V, BACK_V = 3, 8, 23
PRE_P, DECAY_P, CONV_P = 1, 7, 2


def later(c):
    return not (isinstance(c, int) and c == 0)


class Steps:

    def __init__(self, per):
        self.per, self.n = per, 0

    def start(self):
        self.n = 0

    def next(self, c):
        self.n += 1
        return c * self.per + self.n

    def reached(self, c):
        return c * self.per + self.n


def program(nc, tokens, position, vocab_ids, table, weights, norms, conv_w, conv_b, shared_rows, d_skip, w_out, w_down,
            w2, identity, lower_ones, head_rows, pair_rows, spread_rows, out):
    with ExitStack() as ctx:
        def sb(name, shape, dt=F32):
            return ctx.enter_context(nc.sbuf_tensor(name, shape, dt))

        def sem(name):
            return ctx.enter_context(nc.semaphore(name))

        ids = sb("ids", [V, 1])
        tab = sb("tab", [V, D])
        tab_rest = sb("tab_rest", [V, 2, D])
        tab3 = sb("tab3", [V, 3, D], BF16)
        w_raw = sb("w_raw", [128, COLS])
        wt_raw = sb("wt_raw", [128, COLS])
        w_hi = sb("w_hi", [128, COLS], F16)
        w_lo = sb("w_lo", [128, COLS], F16)
        wt_hi = sb("wt_hi", [128, COLS], F16)
        wt_lo = sb("wt_lo", [DT, COLS], F16)
        nrm = sb("nrm", [128, 4])
        cw_ = sb("cw_", [128, NM, KC])
        cb_ = sb("cb_", [128, NM])
        shared = sb("shared", [128, 2 * NH + NE + NE * NE + NG * NG])
        dtb, alog, gbias = shared[:, 0:NH], shared[:, NH:2 * NH], shared[:, 2 * NH:2 * NH + NE]
        at = 2 * NH + NE
        before8 = shared[:, at:at + NE * NE].rearrange("p (e f) -> p e f", e=NE)
        at += NE * NE
        before4 = shared[:, at:at + NG * NG].rearrange("p (e f) -> p e f", e=NG)
        aexp = sb("aexp", [128, NH])
        dsk = sb("dsk", [128, KT])
        spread16 = sb("spread16", [64, KT, 2, 128], F16)
        wo = sb("wo", [128, DI // 128, D])
        wd = sb("wd", [128, NF, D])
        w2t = sb("w2t", [128, NE + 1, D])
        idf = sb("idf", [128, 128])
        upper = sb("upper", [128, 128])
        upper16 = sb("upper16", [128, 128], F16)
        ones16 = sb("ones16", [128, 64], F16)
        hrows = sb("hrows", [NS, HF])
        pairs_of = sb("pairs_of", [128, 2, Q])
        mrows, prows = pairs_of[:, 0], pairs_of[:, 1]
        mhalf = sb("mhalf", [128, 2])

        tok = sb("tok", [V, NB, Q], I32)
        pos = sb("pos", [128, D])
        onehot = sb("onehot", [V, NB, Q], BF16)
        h0_next = sb("h0_next", [128, NB, D])
        stat = sb("stat", [128, NB, 6])
        mv = sb("mv", [128, NB, 2])
        var0 = sb("var0", [128, NB])
        r0 = sb("r0", [128, NB])
        un = sb("un", [128, NB, D])
        u_h = sb("u_h", [128, 2, NB * Q], F16)
        u_l = sb("u_l", [128, NB * Q], F16)

        h0 = sb("h0", [128, NB, D])
        xr = sb("xr", [128, NM, NB, KC - 1 + Q])
        taps = sb("taps", [128, KC - 1, NB, Q])
        xa = sb("xa", [128, NM, NB, Q])
        xs = sb("xs", [128, NM, NB, Q])
        bc = sb("bc", [NS, NB, Q])
        cc = sb("cc", [NS, NB, Q])
        zs = sb("zs", [128, KT, NB, Q])
        dx = sb("dx", [128, NB, NH])
        dn = sb("dn", [128, NB, NH])
        de = sb("de", [128, NB, NH])
        dl = sb("dl", [128, NB, NH])
        dt_ = sb("dt_", [128, NB, NH])
        ap_ = sb("ap_", [128, NB, NH])
        ag_ = sb("ag_", [128, NB, NH])
        ac_ = sb("ac_", [128, NB, NH])
        am_ = sb("am_", [128, NB, NH])
        ar_ = sb("ar_", [128, NB, NH])
        pa = sb("pa", [128, NB, 2, 32], F16)
        pb = sb("pb", [128, NB, 2, 32], F16)
        eend = sb("eend", [NS, NB, NH])
        ecx = sb("ecx", [128, KT, NB, Q])
        lj = sb("lj", [128, NB, 2, 128], F16)
        ri = sb("ri", [128, NB, 2, HF, Q], F16)
        gm = sb("gm", [128, NB, Q])
        bt = sb("bt", [128, NB, NS])
        xd = sb("xd", [128, NB, NH, 2 * HD])
        xk = sb("xk", [128, KT, NB, Q])
        xw = sb("xw", [128, NB, DI])
        NER = 4
        er = sb("er", [128, NER, HG, Q])
        mr = sb("mr", [128, NER, HG, Q])
        t1 = sb("t1", [128, NB, KT, Q])
        state = sb("state", [NS, NB, DI])
        y = sb("y", [128, NB, KT, Q])

        hm = sb("hm", [128, NB, D])
        junk = sb("junk", [128, NB, D], BF16)
        ss = sb("ss", [128, NB])
        vv = sb("vv", [128, NB])
        rm = sb("rm", [128, NB])
        vn = sb("vn", [128, NB, D])
        v_h = sb("v_h", [128, 2, NB * Q], F16)
        v_l = sb("v_l", [128, NB * Q], F16)
        sg = sb("sg", [128, 2, NB * Q])
        gt = sb("gt", [128, NF, NB * Q])
        spread = gt[0:64, 0:KT]
        h1 = sb("h1", [128, NB, D])
        stat2 = sb("stat2", [128, NB, 6])
        mv2 = sb("mv2", [128, NB, 2])
        var2 = sb("var2", [128, NB])
        r2 = sb("r2", [128, NB])
        xn = sb("xn", [128, NB, D])
        x_h = sb("x_h", [128, 2, NB * Q], F16)
        x_l = sb("x_l", [128, NB * Q], F16)
        th = sb("th", [128, NB, NE])
        sc = sb("sc", [128, NB, NE])
        sv = sb("sv", [128, NB, NE])
        gs = sb("gs", [128, NB, NG])
        g_gt = sb("g_gt", [128, NB, NG, NG])
        g_ge = sb("g_ge", [128, NB, NG, NG])
        g_rank = sb("g_rank", [128, NB, NG])
        g_on = sb("g_on", [128, NB, NG, GE])
        e_gt = sb("e_gt", [128, NB, NE, NE])
        e_ge = sb("e_ge", [128, NB, NE, NE])
        e_rank = sb("e_rank", [128, NB, NE])
        g_sc = sb("g_sc", [128, NB, NE])
        e_w = sb("e_w", [128, NB, NE])
        e_sum = sb("e_sum", [128, NB])
        e_sum1 = sb("e_sum1", [128, NB])
        e_inv = sb("e_inv", [128, NB])
        cw = sb("cw", [128, NB, NE])
        NHH = 4
        hh = w_raw[:, 0:NHH * NB * Q].rearrange("p (s t) -> p s t", s=NHH)
        NWT = 3
        at = NHH * NB * Q
        wt_out = w_raw[:, at:at + NWT * NB * D].rearrange("p (s b d) -> p s b d", s=NWT, b=NB)
        at += NWT * NB * D
        acc = w_raw[:, at:at + NB * D].rearrange("p (b d) -> p b d", b=NB)
        assert at + NB * D <= COLS

        sums = nc.dram_tensor("sums", (NB, 2, 64, Q), F16, kind="Internal").ap()
        bank = [ctx.enter_context(nc.psum_tensor(f"bank{i}", [128, 512], F32)) for i in range(8)]
        p_pair = bank[0:2]
        p_out = bank[2:4]
        p_misc, p_d0, p_d1, p_y = bank[4:8]
        p_d = (p_d0, p_d1)

        in_first, in_small, in_w, in_late = sem("in_first"), sem("in_small"), sem("in_w"), sem("in_late")
        setup_v, setup_a, setup_p = sem("setup_v"), sem("setup_a"), sem("setup_p")
        w_in_hi, w_in_lo, w_rest_hi, w_rest_lo = sem("w_in_hi"), sem("w_in_lo"), sem("w_rest_hi"), sem("w_rest_lo")
        passed = sem("passed")
        tokens_in, position_in = sem("tokens_in"), sem("position_in")
        onehot_ready, emb_done, h0_ready, stat_ready, r0_ready = (sem(n) for n in (
            "onehot_ready", "emb_done", "h0_ready", "stat_ready", "r0_ready"))
        un_ready, ut_done, u_hi_ready, u_hi_tail, u_lo_ready, u_lo_tail = (sem(n) for n in (
            "un_ready", "ut_done", "u_hi_ready", "u_hi_tail", "u_lo_ready", "u_lo_tail"))
        pre_v, front_v, back_v, pre_p, front_p, back_p, back_a = (sem(n) for n in (
            "pre_v", "front_v", "back_v", "pre_p", "front_p", "back_p", "back_a"))
        h0_copied = sem("h0_copied")
        x_done = [sem(f"x_done{i}") for i in range(2)]
        z_done = [sem(f"z_done{i}") for i in range(2)]
        xr_ready = [sem(f"xr_ready{i}") for i in range(2)]
        z_ready = [sem(f"z_ready{i}") for i in range(2)]
        dx_ready, dn_ready, de_ready, dl_ready, pab_ready = (sem(n) for n in (
            "dx_ready", "dn_ready", "de_ready", "dl_ready", "pab_ready"))
        am_ready = sem("am_ready")
        xa_ready, halo_kept, xs_ready, b_ready, c_ready = (sem(n) for n in (
            "xa_ready", "halo_kept", "xs_ready", "b_ready", "c_ready"))
        cum_done, eend_ready = sem("cum_done"), sem("eend_ready")
        cumx_done = [sem(f"cumx_done{i}") for i in range(2)]
        ecx_ready = [sem(f"ecx_ready{i}") for i in range(2)]
        g_done, gm_ready, bt_ready = sem("g_done"), sem("gm_ready"), sem("bt_ready")
        xt_done = [sem(f"xt_done{b}") for b in range(NB)]
        lj_high, lj_ready = sem("lj_high"), sem("lj_ready")
        xd_ready = [sem(f"xd_ready{b}") for b in range(NB)]
        xk_ready = sem("xk_ready")
        ri_in, sums_out = sem("ri_in"), sem("sums_out")
        NR = NB * NQ
        d_done = sem("d_done")
        e_ready = sem("e_ready")
        m_ready = sem("m_ready")
        yq_done = sem("yq_done")
        xw_ready = sem("xw_ready")
        yi_done = [sem(f"yi_done{b}") for b in range(NB)]
        t1_ready = [sem(f"t1_ready{b}") for b in range(NB)]
        t1_sum = [sem(f"t1_sum{b}") for b in range(NB)]
        sn_done = [sem(f"sn_done{b}") for b in range(NB)]
        s_decayed = [sem(f"s_decayed{b}") for b in range(NB)]
        s_ready = [sem(f"s_ready{b}") for b in range(NB)]
        y_sum = [sem(f"y_sum{b}") for b in range(NB)]
        y_ready = [sem(f"y_ready{b}") for b in range(NB)]
        m_out, hm_ready, rm_ready, vn_ready, vt_done = (sem(n) for n in (
            "m_out", "hm_ready", "rm_ready", "vn_ready", "vt_done"))
        v_hi_ready, v_hi_tail, v_lo_ready, v_lo_tail = (sem(n) for n in (
            "v_hi_ready", "v_hi_tail", "v_lo_ready", "v_lo_tail"))
        gu_done, sg_ready, gt_ready = sem("gu_done"), sem("sg_ready"), sem("gt_ready")
        mlp_done, h1_ready, stat2_ready, r2_ready, xn_ready, xnt_done = (sem(n) for n in (
            "mlp_done", "h1_ready", "stat2_ready", "r2_ready", "xn_ready", "xnt_done"))
        x_hi_ready, x_hi_tail, x_lo_ready, x_lo_tail = (sem(n) for n in (
            "x_hi_ready", "x_hi_tail", "x_lo_ready", "x_lo_tail"))
        router_done, th_ready, cw_ready = sem("router_done"), sem("th_ready"), sem("cw_ready")
        NX = NE + 1
        h13_done, sx_ready, hh_ready, ex_done, acc_done = (sem(n) for n in (
            "h13_done", "sx_ready", "hh_ready", "ex_done", "acc_done"))
        weighed, sx_half, gt_half = sem("weighed"), sem("sx_half"), sem("gt_half")
        halved, decay_p, conv_p, xa_rest_ready = sem("halved"), sem("decay_p"), sem("conv_p"), sem("xa_rest_ready")
        tap_ready = [sem(f"tap_ready{i}") for i in range(2)]
        xt_tanh, taps_ready = sem("xt_tanh"), sem("taps_ready")
        zs_ready = [sem(f"zs_ready{i}") for i in range(2)]
        out_written = sem("out_written")

        def settle(eng):
            eng.sem_inc(passed, 1)

        block = ctx.enter_context(nc.Block())

        def run(eng, body):
            body(0, None, None)
            body(1, 0, None)
            body(2, 1, 0)
            with eng.Fori(1, NC - 2) as i:
                body(i + 2, i + 1, i)
            body(None, NC - 1, NC - 2)
            body(None, None, NC - 1)

        @block.sync
        def _(sp):
            def load_weights():
                part = slice(0, COL_G)
                sp.dma_start(w_raw[:, part], weights[0:DH, part]).then_inc(in_w, 16)
                sp.dma_start(wt_raw[0:DT, part], weights[DH:D, part]).then_inc(in_w, 16)
                sp.dma_start(wt_raw[DT:128, part], weights[DH:D, part]).then_inc(in_w, 16)
                sp.dma_start(nrm[:], norms).then_inc(in_w, 16)

            def load_small():
                small = [(cw_[:], conv_w), (cb_[:], conv_b), (shared[:], shared_rows.partition_broadcast(128)),
                         (dsk[:], d_skip), (spread, spread_rows.rearrange("r k f c -> r k (f c)")),
                         (hrows[:], head_rows), (pairs_of[64:128], pair_rows), (upper[:], lower_ones)]
                assert len(small) == N_SMALL
                for dst, src in small:
                    sp.dma_start(dst, src).then_inc(in_small, 16)

            def load(c):
                if later(c):
                    sp.wait_ge(onehot_ready, c)
                settle(sp)
                sp.dma_start(tok[:], tokens[:, bass.ds(c * Q, Q)].partition_broadcast(V)).then_inc(tokens_in, 16)
                if later(c):
                    sp.wait_ge(h0_ready, c)
                settle(sp)
                sp.dma_start(pos[:], position[bass.ds(c * Q, Q), :]).then_inc(position_in, 16)

            def sums_in_rows(c):
                if not later(c):
                    sp.wait_ge(setup_v, SETUP_V)
                sp.wait_ge(lj_ready, c + 1)
                settle(sp)
                sp.dma_start(sums.rearrange("b f r i -> r b f i"), lj[0:64]).then_inc(sums_out, 16)
                sp.wait_ge(sums_out, c * 16 + 16)
                settle(sp)
                if later(c):
                    sp.wait_ge(d_done, c * NR)
                settle(sp)
                for b in range(NB):
                    for f in range(2):
                        sp.dma_start(ri[HF:HF + 4, b, f, :, :],
                                     sums[b, f].rearrange("(g r) i -> g r i", g=4)[:, 0:HF, :]).then_inc(ri_in, 16)

            def store(c):
                sp.wait_ge(acc_done, c * NX + NX)
                settle(sp)
                sp.dma_start(out[:, bass.ds(c * Q, Q), :].rearrange("b t d -> t b d"), acc[:]).then_inc(out_written, 16)

            def body(p, f, b):
                if later_chunk(p):
                    load(p)
                if p is not None:
                    sums_in_rows(p)
                if b is not None:
                    store(b)

            def later_chunk(p):
                return p is not None and later(p)

            sp.dma_start(ids[:], vocab_ids).then_inc(in_first, 16)
            sp.dma_start(tab[:], table).then_inc(in_first, 16)
            load(0)
            sp.dma_start(idf[:], identity).then_inc(in_first, 16)
            load_weights()
            load_small()
            rest = slice(COL_G, COLS)
            sp.dma_start(w_raw[:, rest], weights[0:DH, rest]).then_inc(in_late, 16)
            sp.dma_start(wt_raw[0:DT, rest], weights[DH:D, rest]).then_inc(in_late, 16)
            sp.dma_start(wt_raw[DT:128, rest], weights[DH:D, rest]).then_inc(in_late, 16)
            sp.dma_start(wo[:], w_out).then_inc(in_late, 16)
            sp.dma_start(wd[:], w_down).then_inc(in_late, 16)
            sp.dma_start(w2t[:], w2).then_inc(in_late, 16)
            run(sp, body)
            sp.wait_ge(out_written, 16 * NC)

        @block.gpsimd
        def _(pool):
            pool.memset(mhalf[:], -0.5).then_inc(setup_p, 1)
            pool.memset(state[:], 0.0).then_inc(setup_p, 1)
            pool.memset(xr[:, :, :, 0:KC - 1], 0.0).then_inc(setup_p, 1)
            pool.memset(ones16[:], 1.0).then_inc(setup_p, 1)
            pool.memset(xd[:], 0.0).then_inc(setup_p, 1)
            pool.wait_ge(setup_p, 5)

            def rsqrt(c, ready, src, scale, bias, mid, dst, chain, steps, k, done):
                pool.wait_ge(ready, c + 1)
                settle(pool)
                pool.tensor_scalar(mid, src, scale, bias, ALU.mult, ALU.add).then_inc(chain, 1)
                pool.wait_ge(chain, c * steps + k)
                pool.tensor_tensor(dst, mid, mhalf[:], ALU.pow).then_inc(done, 1)

            def pre(c):
                rsqrt(c, stat_ready, mv[:, :, 1], 1.0 + 1e-6, 1e-11, var0[:], r0[:], pre_p, PRE_P, 1, r0_ready)

            def keep(c):
                if later(c):
                    pool.wait_ge(hm_ready, c)
                pool.wait_ge(h0_ready, c + 1)
                settle(pool)
                pool.tensor_copy(h0[:], h0_next[:]).then_inc(h0_copied, 1)

            def halo(c):
                pool.wait_ge(xa_ready, c + 1)
                pool.wait_ge(xa_rest_ready, c + 1)
                settle(pool)
                pool.tensor_copy(xr[:, :, :, 0:KC - 1], xr[:, :, :, Q:Q + KC - 1]).then_inc(halo_kept, 1)

            def scan(c, b, after):
                if later(c):
                    pool.wait_ge(sn_done[b], c)
                for q in range(NQ):
                    r = b * NQ + q
                    pool.wait_ge(e_ready, c * NR + r + 1)
                    if q == 0:
                        pool.wait_ge(xd_ready[b], c + 1)
                    for odd in range(2):
                        h = slice(q * HG + odd, (q + 1) * HG, 2)
                        o = slice(q * HG * HD, (q + 1) * HG * HD)
                        ins = pool.tensor_tensor(
                            xw[:, b, o].rearrange("p (g o d) -> p g o d", o=2, d=HD)[:, :, odd, :],
                            xd[:, b, h, odd * HD:(odd + 1) * HD],
                            er[:, r % NER, odd:HG:2, Q - 1:Q].to_broadcast([128, HG // 2, HD]), ALU.mult)
                    ins.then_inc(xw_ready, 1)
                    if q in after:
                        after[q]()
                pool.wait_ge(eend_ready, c + 1)
                pool.wait_ge(yi_done[b], c + 1)
                if later(c):
                    pool.wait_ge(s_ready[b], c)
                sv_ = state[:, b, :].rearrange("n (h p) -> n h p", h=NH)
                pool.tensor_tensor(sv_, sv_, eend[:, b, :].unsqueeze(2).to_broadcast([NS, NH, HD]), ALU.mult)\
                    .then_inc(s_decayed[b], 1)
                pool.wait_ge(t1_ready[b], c + 1)
                pool.wait_ge(xk_ready, c + 1)
                pool.tensor_tensor(t1[:, b], t1[:, b], xk[:, :, b, :], ALU.add).then_inc(t1_sum[b], 1)

            def gate(c, b):
                pool.wait_ge(y_sum[b], c + 1)
                pool.wait_ge(zs_ready[0], c + 1)
                pool.wait_ge(zs_ready[1], c + 1)
                pool.tensor_tensor(y[:, b], y[:, b], zs[:, :, b, :], ALU.mult).then_inc(y_ready[b], 1)

            def mixed(c):
                pool.wait_ge(back_a, c * 2 + 2)
                settle(pool)
                pool.tensor_scalar(vv[:], ss[:], 1.0 / D, 1e-6, ALU.mult, ALU.add).then_inc(back_p, 1)
                pool.wait_ge(back_p, c + 1)
                pool.tensor_tensor(rm[:], vv[:], mhalf[:], ALU.pow).then_inc(rm_ready, 1)

            def halves(t):
                return t[:].rearrange("p b (f h) -> p b f h", f=2)

            decay_steps = Steps(DECAY_P)

            def steps_decay(c):
                decay_steps.start()
                pool.wait_ge(dl_ready, c + 1)
                if later(c):
                    pool.wait_ge(xd_ready[1], c)
                    pool.wait_ge(cum_done, c)
                pool.wait_ge(am_ready, c + 1)
                pool.tensor_tensor(dt_[:], am_[:], dl[:], ALU.add).then_inc(decay_p, 1)
                pool.wait_ge(decay_p, decay_steps.next(c))
                pool.tensor_tensor(ap_[:], dt_[:], aexp[:].unsqueeze(1).to_broadcast([128, NB, NH]), ALU.mult).then_inc(decay_p, 1)
                pool.wait_ge(decay_p, decay_steps.next(c))
                settle(pool)
                pool.tensor_scalar(ag_[:], ap_[:], DEAD, ROUND, ALU.min, ALU.add).then_inc(decay_p, 1)
                pool.tensor_scalar(ac_[:], ap_[:], DEAD, None, ALU.min).then_inc(decay_p, 1)
                decay_steps.next(c)
                pool.wait_ge(decay_p, decay_steps.next(c))
                settle(pool)
                pool.tensor_scalar(pa[:, :, :, 0:HF], halves(ag_), ROUND, None, ALU.subtract).then_inc(decay_p, 1)
                pool.wait_ge(decay_p, decay_steps.next(c))
                pool.tensor_tensor(halves(ar_), halves(ac_), pa[:, :, :, 0:HF], ALU.subtract).then_inc(decay_p, 1)
                pool.wait_ge(decay_p, decay_steps.next(c))
                settle(pool)
                pool.tensor_copy(pa[:, :, :, 16:16 + HF], halves(ar_)).then_inc(decay_p, 1)
                pool.wait_ge(decay_p, decay_steps.next(c))
                assert decay_steps.n == DECAY_P, decay_steps.n
                pool.tensor_tensor(pb[:, :, :, 16:16 + HF], halves(ar_), pa[:, :, :, 16:16 + HF], ALU.subtract)\
                    .then_inc(pab_ready, 1)

            conv_steps = Steps(CONV_P)

            def convolve(c):
                conv_steps.start()
                m = NM - 1
                pool.wait_ge(taps_ready, c + 1)
                for k in range(1, KC):
                    if k > 1:
                        pool.wait_ge(conv_p, conv_steps.reached(c))
                    ins = pool.tensor_tensor(xa[:, m], xa[:, m], taps[:, k - 1], ALU.add)
                    if k < KC - 1:
                        ins.then_inc(conv_p, 1)
                        conv_steps.next(c)
                    else:
                        ins.then_inc(xa_rest_ready, 1)
                assert conv_steps.n == CONV_P, conv_steps.n

            def experts(c, p):
                for e in range(NX):
                    pool.wait_ge(weighed, c * NX + e + 1)
                    if e == 0:
                        if later(c):
                            pool.wait_ge(out_written, c * 16)
                        pool.wait_ge(h1_ready, c + 1)
                        settle(pool)
                        pool.tensor_tensor(acc[:], wt_out[:, 0], h1[:], ALU.add).then_inc(acc_done, 1)
                    else:
                        pool.wait_ge(acc_done, c * NX + e)
                        pool.tensor_tensor(acc[:], acc[:], wt_out[:, e % NWT], ALU.add).then_inc(acc_done, 1)
                    if p is not None:
                        if e == 0:
                            steps_decay(p)
                        if e == 4:
                            halo(p)

            def norm2(b):
                rsqrt(b, stat2_ready, mv2[:, :, 1], 1.0, 1e-5, var2[:], r2[:], front_p, 1, 1, r2_ready)

            def body(p, f, b):
                if f is not None:
                    scan(f, 0, {} if b is None else {1: lambda: mixed(b)})
                    keep(f)
                    gate(f, 0)
                elif b is not None:
                    mixed(b)
                if p is not None:
                    pre(p)
                if f is not None:
                    scan(f, 1, {} if b is None else {1: lambda: norm2(b)})
                    gate(f, 1)
                elif b is not None:
                    norm2(b)
                if p is not None:
                    convolve(p)
                if b is not None:
                    experts(b, p)
                elif p is not None:
                    steps_decay(p)
                    halo(p)

            run(pool, body)

        @block.scalar
        def _(act):
            act.wait_ge(in_w, 64)
            act.activation(w_hi[:, 0:COL_G], w_raw[:, 0:COL_G], ACT.Copy, scale=nrm[:, 0:1]).then_inc(w_in_hi, 1)
            act.activation(wt_hi[:, 0:COL_G], wt_raw[:, 0:COL_G], ACT.Copy, scale=nrm[:, 1:2]).then_inc(w_in_hi, 1)

            act.wait_ge(in_small, 16 * N_SMALL)
            act.activation(aexp[:], alog, ACT.Exp).then_inc(setup_a, 1)

            def setup_rest():
                act.wait_ge(in_late, 96)
                act.activation(w_hi[:, COL_G:COL_E], w_raw[:, COL_G:COL_E], ACT.Copy, scale=nrm[:, 2:3])\
                    .then_inc(w_rest_hi, 1)
                act.activation(wt_hi[:, COL_G:COL_E], wt_raw[:, COL_G:COL_E], ACT.Copy, scale=nrm[:, 3:4])\
                    .then_inc(w_rest_hi, 1)
                act.copy(w_hi[:, COL_E:COLS], w_raw[:, COL_E:COLS]).then_inc(w_rest_hi, 1)
                act.copy(wt_hi[:, COL_E:COLS], wt_raw[:, COL_E:COLS]).then_inc(w_rest_hi, 1)

            def scale_outputs():
                act.activation(wo[:], wo[:], ACT.Copy, scale=1.0 / 16).then_inc(halved, 1)
                act.activation(wd[:], wd[:], ACT.Copy, scale=0.5).then_inc(halved, 1)
                act.activation(w2t[:], w2t[:], ACT.Copy, scale=0.5).then_inc(halved, 1)

            def split(c, done, src, hi, taken, head, tail):
                act.wait_ge(done, c + 1)
                if later(c):
                    act.wait_ge(taken[0], c * taken[1])
                act.copy(hi[:, 0, :], src[:, 0:NB * Q]).then_inc(head, 1)
                act.copy(hi[0:DT, 1, :], src[0:DT, NB * Q:2 * NB * Q]).then_inc(tail, 1)

            def convolved_in(c):
                for i in range(2):
                    act.wait_ge(x_done[i], c + 1)
                    if later(c):
                        act.wait_ge(xa_ready, c)
                        act.wait_ge(xa_rest_ready, c)
                        act.wait_ge(halo_kept, c)
                    act.copy(xr[:, 2 * i:2 * i + 2, :, KC - 1:KC - 1 + Q],
                             p_d[i][:].rearrange("p (m b t) -> p m b t", m=2, b=NB)).then_inc(xr_ready[i], 1)
                    act.wait_ge(xr_ready[i], c + 1)
                    if later(c):
                        act.wait_ge(c_ready, c)
                    for m in (2 * i, 2 * i + 1):
                        ins = act.activation(xa[:, m], xr[:, m, :, 0:Q], ACT.Identity, bias=cb_[:, m:m + 1],
                                             scale=cw_[:, m, 0:1])
                    ins.then_inc(tap_ready[i], 1)

            def convolved_taps(c):
                if later(c):
                    act.wait_ge(xa_rest_ready, c)
                for k in range(1, KC):
                    ins = act.activation(taps[:, k - 1], xr[:, NM - 1, :, k:k + Q], ACT.Copy, scale=cw_[:, NM - 1, k:k + 1])
                ins.then_inc(taps_ready, 1)

            def gates(c, i):
                t = (slice(0, 2), slice(2, KT))[i]
                act.wait_ge(z_done[i], c + 1)
                if later(c):
                    act.wait_ge(y_ready[1], c)
                act.activation(zs[:, t], (p_y, p_misc)[i][:, 0:(t.stop - t.start) * NB * Q]
                               .rearrange("p (k b t) -> p k b t", b=NB, t=Q), ACT.Tanh, scale=0.5).then_inc(z_ready[i], 1)

            def convolved_out(c):
                act.wait_ge(xa_ready, c + 1)
                act.wait_ge(xa_rest_ready, c + 1)
                if later(c):
                    act.wait_ge(xt_done[1], c)
                    act.wait_ge(xk_ready, c)
                act.activation(xs[:], xa[:], ACT.Tanh, scale=0.5).then_inc(xt_tanh, 1)

            def skipped_x(c):
                act.wait_ge(xs_ready, c + 1)
                if later(c):
                    act.wait_ge(t1_sum[1], c)
                for k in range(KT):
                    ins = act.activation(xk[:, k], xs[:, k], ACT.Copy, scale=dsk[:, k:k + 1])
                ins.then_inc(xk_ready, 1)

            def softplus(c):
                act.wait_ge(dn_ready, c + 1)
                if later(c):
                    act.wait_ge(dl_ready, c)
                act.activation(de[:], dn[:], ACT.Exp).then_inc(de_ready, 1)
                act.wait_ge(de_ready, c + 1)
                if later(c):
                    act.wait_ge(pab_ready, c)
                act.activation(dl[:], de[:], ACT.Ln, bias=1.0).then_inc(dl_ready, 1)

            def b_on_tokens(c):
                act.wait_ge(g_done, c + 1)
                if later(c):
                    act.wait_ge(sn_done[1], c)
                act.copy(bt[:], p_y[:, 256:256 + NB * NS].rearrange("p (b n) -> p b n", b=NB)).then_inc(bt_ready, 1)

            def operands(c):
                act.wait_ge(cum_done, c + 1)
                if later(c):
                    act.wait_ge(d_done, c * NR)
                    act.wait_ge(sums_out, c * 16)
                for f in range(2):
                    ins = act.copy(lj[0:32, :, f, :], p_misc[32 * f:32 * (f + 1), 0:NB * Q].rearrange("p (b i) -> p b i", b=NB))
                ins.then_inc(lj_high, 1)

            def decays(c):
                act.wait_ge(lj_ready, c + 1)
                if later(c):
                    act.wait_ge(s_decayed[1], c)
                act.activation(eend[:], p_misc[0:NS, 256:256 + NB * NH].rearrange("p (b h) -> p b h", b=NB),
                               ACT.Exp, scale=-1.0).then_inc(eend_ready, 1)
                for i, t in ((0, slice(0, 2)), (1, slice(2, KT))):
                    act.wait_ge(cumx_done[i], c + 1)
                    if later(c):
                        act.wait_ge(t1_ready[1], c)
                    act.activation(ecx[:, t], p_d[i][:, 0:(t.stop - t.start) * NB * Q]
                                   .rearrange("p (k b t) -> p k b t", b=NB, t=Q), ACT.Exp, scale=-1.0)\
                        .then_inc(ecx_ready[i], 1)

            def scan(c, b, between):
                for q in range(NQ):
                    if q in between:
                        between[q]()
                    r = b * NQ + q
                    act.wait_ge(d_done, c * NR + r + 1)
                    if later(c) or r - NER + 1 > 0:
                        act.wait_ge(m_ready, c * NR + r - NER + 1)
                    if later(c) or r - NER + 1 > 0:
                        act.wait_ge(xw_ready, c * NR + r - NER + 1)
                    act.activation(er[:, r % NER], p_d[r % 2][:].rearrange("p (h i) -> p h i", h=HG), ACT.Exp)\
                        .then_inc(e_ready, 1)

            def mixed(c):
                act.wait_ge(m_out, c + 1)
                if later(c):
                    act.wait_ge(rm_ready, c)
                for b in range(NB):
                    if later(c):
                        act.wait_ge(back_a, c * 2)
                    act.activation(junk[:, b, :], p_out[0][:, b * D:(b + 1) * D], ACT.Square, accum_out=ss[:, b:b + 1])\
                        .then_inc(back_a, 1)

            def mixed_norm(c):
                act.wait_ge(rm_ready, c + 1)
                if later(c):
                    act.wait_ge(vt_done, c)
                for b in range(NB):
                    ins = act.activation(vn[:, b, :], p_out[0][:, b * D:(b + 1) * D], ACT.Copy, scale=rm[:, b:b + 1])
                ins.then_inc(vn_ready, 1)

            def swiglu(c, p):
                for f in range(NF):
                    act.wait_ge(gu_done, c * NF + f + 1)
                    if f >= 2:
                        act.wait_ge(gt_ready, c * NF + f - 1)
                    else:
                        if later(c):
                            act.wait_ge(hh_ready, c * NX)
                    act.activation(sg[:, f % 2, :], p_pair[f % 2][:, 0:NB * Q], ACT.Tanh, scale=0.5).then_inc(sg_ready, 1)
                    if f == 4 and p is not None:
                        pre_split(p)

            def route(c):
                act.wait_ge(router_done, c + 1)
                if later(c):
                    act.wait_ge(cw_ready, c)
                act.activation(th[:], p_out[0][:, 0:NB * NE].rearrange("p (b e) -> p b e", b=NB), ACT.Tanh, scale=0.5)\
                    .then_inc(th_ready, 1)

            def pre_split(c):
                split(c, ut_done, p_misc, u_h, (z_done[0], 1), u_hi_ready, u_hi_tail)

            def weigh(c, e):
                act.wait_ge(ex_done, c * NX + e + 1)
                if e >= NWT:
                    act.wait_ge(acc_done, c * NX + e - NWT + 1)
                elif later(c):
                    act.wait_ge(acc_done, c * NX)
                p = p_out[(e + 1) % 2]
                if e == 0:
                    act.copy(wt_out[:, 0], p[:, 0:NB * D].rearrange("p (b d) -> p b d", b=NB)).then_inc(weighed, 1)
                    return
                if e == 1:
                    act.wait_ge(cw_ready, c + 1)
                for b in range(NB):
                    ins = act.activation(wt_out[:, e % NWT, b], p[:, b * D:(b + 1) * D], ACT.Copy,
                                         scale=cw[:, b, e - 1:e])
                ins.then_inc(weighed, 1)

            def experts(c, p):
                for e in range(NX):
                    act.wait_ge(h13_done, c * NX + e + 1)
                    if e >= 2:
                        act.wait_ge(hh_ready, c * NX + e - 1)
                    else:
                        act.wait_ge(gt_ready, c * NF + NF - 1 + e)
                    act.activation(sg[:, e % 2, :], p_pair[e % 2][:, 0:NB * Q], ACT.Tanh, scale=0.5).then_inc(sx_ready, 1)
                    if e == 0:
                        route(c)
                        if p is not None:
                            convolved_taps(p)
                    if e == 7 and p is not None:
                        b_on_tokens(p)
                    for out_ in {2: (0,), 3: (), 4: (1, 2)}.get(e, (e - 2,) if e > 4 else ()):
                        weigh(c, out_)
                    if p is not None:
                        if e == 1:
                            gates(p, 1)
                            gates(p, 0)
                        if e == 2:
                            softplus(p)
                        if e == 4:
                            operands(p)
                            convolved_out(p)
                        if e == 8:
                            decays(p)
                weigh(c, NX - 2)
                weigh(c, NX - 1)

            def split_v(b):
                split(b, vt_done, p_out[1], v_h, (gu_done, NF), v_hi_ready, v_hi_tail)

            def split_x(b):
                split(b, xnt_done, p_out[1], x_h, (h13_done, NX), x_hi_ready, x_hi_tail)

            def body(p, f, b):
                if f is not None:
                    scan(f, 0, {} if b is None else {2: lambda: mixed(b), 4: lambda: mixed_norm(b)})
                elif b is not None:
                    mixed(b)
                    mixed_norm(b)
                if b is not None:
                    split_v(b)
                if f is not None:
                    skipped_x(f)
                if b is not None:
                    swiglu(b, p)
                elif p is not None:
                    if f is not None:
                        setup_rest()
                    pre_split(p)
                if f is not None:
                    scan(f, 1, {})
                if b is not None:
                    split_x(b)
                if p is not None:
                    convolved_in(p)
                if b is not None:
                    experts(b, p)
                elif p is not None:
                    convolved_taps(p)
                    gates(p, 1)
                    gates(p, 0)
                    softplus(p)
                    if f is not None:
                        scale_outputs()
                    operands(p)
                    convolved_out(p)
                    b_on_tokens(p)
                    decays(p)

            run(act, body)

        @block.vector
        def _(ve):
            pre_steps, front_steps, back_steps = Steps(PRE_V), Steps(FRONT_V), Steps(BACK_V)

            setup_steps = Steps(0)

            def setup_table():
                ve.wait_ge(in_first, 48)
                ve.tensor_scalar(tab_rest[:, 0, :], tab[:], EMB_SCALE, None, ALU.mult).then_inc(setup_v, 1)
                ve.wait_ge(setup_v, setup_steps.next(0))
                ve.tensor_copy(tab3[:, 0, :], tab_rest[:, 0, :]).then_inc(setup_v, 1)
                ve.wait_ge(setup_v, setup_steps.next(0))
                ve.tensor_tensor(tab_rest[:, 1, :], tab_rest[:, 0, :], tab3[:, 0, :], ALU.subtract).then_inc(setup_v, 1)
                ve.wait_ge(setup_v, setup_steps.next(0))
                ve.tensor_copy(tab3[:, 1, :], tab_rest[:, 1, :]).then_inc(setup_v, 1)
                ve.wait_ge(setup_v, setup_steps.next(0))
                ve.tensor_tensor(tab3[:, 2, :], tab_rest[:, 1, :], tab3[:, 1, :], ALU.subtract).then_inc(setup_v, 1)
                ve.wait_ge(setup_v, setup_steps.next(0))

            def setup_first():
                ve.wait_ge(in_small, 16 * N_SMALL)
                ve.tensor_scalar(dsk[:], dsk[:], 4.0, None, ALU.mult).then_inc(setup_v, 1)
                ve.wait_ge(setup_v, setup_steps.next(0))
                ve.tensor_copy(spread16[:].rearrange('r k f c -> r k (f c)'), spread).then_inc(setup_v, 1)
                ve.wait_ge(setup_v, setup_steps.next(0))
                ve.tensor_copy(upper16[:], upper[:]).then_inc(setup_v, 1)
                ve.wait_ge(setup_v, setup_steps.next(0))
                ve.memset(pa[:], 0.0).then_inc(setup_v, 1)
                ve.wait_ge(setup_v, setup_steps.next(0))
                ve.memset(pb[:], 0.0).then_inc(setup_v, 1)
                ve.wait_ge(setup_v, setup_steps.next(0))
                ve.memset(pa[0:1, :, :, HF:HF + 4], -1.0).then_inc(setup_v, 1)
                ve.wait_ge(setup_v, setup_steps.next(0))
                ve.wait_ge(in_w, 64)
                ve.wait_ge(w_in_hi, 2)
                ve.scalar_tensor_tensor(w_lo[:, 0:COL_G], w_raw[:, 0:COL_G], nrm[:, 0:1], w_hi[:, 0:COL_G],
                                        ALU.mult, ALU.subtract).then_inc(w_in_lo, 1)
                ve.scalar_tensor_tensor(wt_lo[:, 0:COL_G], wt_raw[0:DT, 0:COL_G], nrm[0:DT, 1:2], wt_hi[0:DT, 0:COL_G],
                                        ALU.mult, ALU.subtract).then_inc(w_in_lo, 1)

            def setup_exponents(b):
                for f in range(2):
                    ve.tensor_copy(ri[0:64, b, f], hrows[:].unsqueeze(2).to_broadcast([64, HF, Q])).then_inc(setup_v, 1)
                    ve.tensor_copy(ri[64:128, b, f], mrows[64:128, :].unsqueeze(1).to_broadcast([64, HF, Q])).then_inc(setup_v, 1)
                    ve.tensor_copy(lj[64:128, b, f], prows[64:128, :]).then_inc(setup_v, 1)

            def setup_rest(part):
                ve.wait_ge(in_late, 96)
                ve.wait_ge(w_rest_hi, part + 1)
                m, x = slice(COL_G, COL_E), slice(COL_E, COLS)
                if part == 0:
                    ve.scalar_tensor_tensor(w_lo[:, m], w_raw[:, m], nrm[:, 2:3], w_hi[:, m],
                                            ALU.mult, ALU.subtract).then_inc(w_rest_lo, 1)
                elif part == 1:
                    ve.scalar_tensor_tensor(wt_lo[:, m], wt_raw[0:DT, m], nrm[0:DT, 3:4], wt_hi[0:DT, m],
                                            ALU.mult, ALU.subtract).then_inc(w_rest_lo, 1)
                elif part == 2:
                    ve.tensor_tensor(w_lo[:, x], w_raw[:, x], w_hi[:, x], ALU.subtract).then_inc(w_rest_lo, 1)
                else:
                    ve.tensor_tensor(wt_lo[:, x], wt_raw[0:DT, x], wt_hi[0:DT, x], ALU.subtract).then_inc(w_rest_lo, 1)

            def split(c, head, tail, src, hi, lo, lo_ready, lo_tail):
                ve.wait_ge(head, c + 1)
                ve.wait_ge(tail, c + 1)
                ve.tensor_tensor(lo[:], src[:, 0:NB * Q], hi[:, 0, :], ALU.subtract).then_inc(lo_ready, 1)
                ve.tensor_tensor(hi[DT:128, 1, :], src[0:DT, NB * Q:2 * NB * Q], hi[0:DT, 1, :], ALU.subtract)\
                    .then_inc(lo_tail, 1)

            def pre_onehot(c):
                ve.wait_ge(tokens_in, c * 16 + 16)
                if later(c):
                    ve.wait_ge(emb_done, c)
                ve.tensor_scalar(onehot[:], tok[:], float(V - 1), ids[:, 0:1], ALU.min, ALU.is_equal)\
                    .then_inc(onehot_ready, 1)

            def pre_norm(c):
                ve.wait_ge(emb_done, c + 1)
                ve.wait_ge(position_in, c * 16 + 16)
                if later(c):
                    ve.wait_ge(h0_copied, c)
                ve.tensor_tensor(h0_next[:], p_misc[:, 0:NB * D].rearrange("p (b d) -> p b d", b=NB),
                                 pos[:].unsqueeze(1).to_broadcast([128, NB, D]), ALU.add).then_inc(h0_ready, 1)
                ve.wait_ge(h0_ready, c + 1)
                pre_steps.start()
                ve.bn_stats(stat[:, 0, :], h0_next[:, 0, :]).then_inc(pre_v, 1)
                ve.bn_stats(stat[:, 1, :], h0_next[:, 1, :]).then_inc(pre_v, 1)
                pre_steps.next(c)
                ve.wait_ge(pre_v, pre_steps.next(c))
                settle(ve)
                ve.bn_aggr(mv[:, 0, :], stat[:, 0, :]).then_inc(pre_v, 1)
                pre_steps.next(c)
                assert pre_steps.n == PRE_V
                settle(ve)
                ve.bn_aggr(mv[:, 1, :], stat[:, 1, :]).then_inc(stat_ready, 1)

            def pre_apply(c):
                ve.wait_ge(r0_ready, c + 1)
                if later(c):
                    ve.wait_ge(ut_done, c)
                ve.tensor_scalar(un[:, 0, :], h0_next[:, 0, :], mv[:, 0, 0:1], r0[:, 0:1], ALU.subtract, ALU.mult)
                ve.tensor_scalar(un[:, 1, :], h0_next[:, 1, :], mv[:, 1, 0:1], r0[:, 1:2], ALU.subtract, ALU.mult)\
                    .then_inc(un_ready, 1)

            def pre_split(c):
                split(c, u_hi_ready, u_hi_tail, p_misc, u_h, u_l, u_lo_ready, u_lo_tail)

            def convolve_tap(c, m, k):
                if m == 0 and k == 1:
                    front_steps.start()
                if k == 1:
                    ve.wait_ge(tap_ready[m // 2], c + 1)
                else:
                    ve.wait_ge(front_v, front_steps.reached(c))
                last = m == 2 and k == KC - 1
                ve.scalar_tensor_tensor(xa[:, m], xr[:, m, :, k:k + Q], cw_[:, m, k:k + 1], xa[:, m], ALU.mult, ALU.add)\
                    .then_inc(xa_ready if last else front_v, 1)
                if not last:
                    front_steps.next(c)
                else:
                    assert front_steps.n == FRONT_V, front_steps.n

            def convolved(c):
                ve.wait_ge(xt_tanh, c + 1)
                ve.scalar_tensor_tensor(xs[:, 0:KT], xs[:, 0:KT], 1.0, xa[:, 0:KT], ALU.add, ALU.mult).then_inc(xs_ready, 1)
                if later(c):
                    ve.wait_ge(g_done, c)
                    ve.wait_ge(yi_done[1], c)
                ve.scalar_tensor_tensor(bc[:], xs[0:NS, KT], 1.0, xa[0:NS, KT], ALU.add, ALU.mult).then_inc(b_ready, 1)
                ve.scalar_tensor_tensor(cc[:], xs[NS:128, KT], 1.0, xa[NS:128, KT], ALU.add, ALU.mult).then_inc(c_ready, 1)

            def gates(c, i):
                t = (slice(0, 2), slice(2, KT))[i]
                ve.wait_ge(z_ready[i], c + 1)
                ve.scalar_tensor_tensor(zs[:, t], zs[:, t], 1.0, (p_y, p_misc)[i][:, 0:(t.stop - t.start) * NB * Q]
                                        .rearrange("p (k b t) -> p k b t", b=NB, t=Q), ALU.add, ALU.mult)\
                    .then_inc(zs_ready[i], 1)

            def steps_dt(c):
                ve.wait_ge(z_ready[1], c + 1)
                ve.tensor_tensor(dx[:], p_misc[:, 256:256 + NB * NH].rearrange("p (b h) -> p b h", b=NB),
                                 dtb.unsqueeze(1).to_broadcast([128, NB, NH]), ALU.add).then_inc(dx_ready, 1)
                ve.wait_ge(dx_ready, c + 1)
                ve.scalar_tensor_tensor(dn[:], dx[:], -1.0, dx[:], ALU.mult, ALU.min).then_inc(dn_ready, 1)
                if later(c):
                    ve.wait_ge(pab_ready, c)
                ve.tensor_scalar(am_[:], dx[:], 0.0, None, ALU.max).then_inc(am_ready, 1)

            def masked_g(c):
                ve.wait_ge(bt_ready, c + 1)
                ve.tensor_tensor(gm[:], p_y[:, 0:NB * Q].rearrange("p (b i) -> p b i", b=NB),
                                 upper[:].unsqueeze(1).to_broadcast([128, NB, Q]), ALU.mult).then_inc(gm_ready, 1)

            def operands(c):
                ve.wait_ge(lj_high, c + 1)
                if later(c):
                    ve.wait_ge(d_done, c * NR)
                    ve.wait_ge(sums_out, c * 16)
                for f in range(2):
                    ins = ve.tensor_tensor(lj[32:64, :, f, :], p_misc[32 * f:32 * (f + 1), 0:NB * Q]
                                           .rearrange("p (b i) -> p b i", b=NB), lj[0:32, :, f, :], ALU.subtract)
                ins.then_inc(lj_ready, 1)

            def scaled_x(c, b):
                ve.wait_ge(xt_done[b], c + 1)
                ve.wait_ge(pab_ready, c + 1)
                if later(c):
                    ve.wait_ge(xw_ready, c * NR)
                    ve.wait_ge(yq_done, c * NR)
                blocks = xd[:, b].rearrange("p (g o) (s d) -> p g (o s) d", o=2, s=2)[:, :, 0:4:3, :]
                ve.tensor_tensor(blocks, p_d[b][:, 0:DI].rearrange("p (g o d) -> p g o d", o=2, d=HD),
                                 dt_[:, b, :].rearrange("p (g o) -> p g o", o=2).unsqueeze(3)
                                 .to_broadcast([128, NH // 2, 2, HD]), ALU.mult).then_inc(xd_ready[b], 1)

            def scan(c, b, between):
                for q in range(NQ):
                    r = b * NQ + q
                    ve.wait_ge(e_ready, c * NR + r + 1)
                    if q == 0:
                        ve.wait_ge(gm_ready, c + 1)
                    if later(c) or r - NER + 1 > 0:
                        ve.wait_ge(yq_done, c * NR + r - NER + 1)
                    ve.scalar_tensor_tensor(mr[:, r % NER], er[:, r % NER], 1.0,
                                            gm[:, b, :].unsqueeze(1).to_broadcast([128, HG, Q]), ALU.min, ALU.mult)\
                        .then_inc(m_ready, 1)
                    if q in between:
                        between[q]()
                    if q == (2, 5)[b]:
                        ve.wait_ge(yi_done[b], c + 1)
                        ve.wait_ge(ecx_ready[0], c + 1)
                        ve.wait_ge(ecx_ready[1], c + 1)
                        if later(c):
                            ve.wait_ge(y_sum[b], c)
                        ve.tensor_tensor(t1[:, b], p_misc[:, 0:DI].rearrange("p (k i) -> p k i", k=KT), ecx[:, :, b, :],
                                         ALU.mult).then_inc(t1_ready[b], 1)

            def scanned(c, b):
                ve.wait_ge(t1_sum[b], c + 1)
                ve.wait_ge(yq_done, c * NR + (b + 1) * NQ)
                if later(c):
                    ve.wait_ge(m_out, c)
                ve.tensor_tensor(y[:, b], p_y[:, 0:DI].rearrange("p (k i) -> p k i", k=KT), t1[:, b], ALU.add)\
                    .then_inc(y_sum[b], 1)

            def new_state(c, b):
                ve.wait_ge(sn_done[b], c + 1)
                ve.wait_ge(s_decayed[b], c + 1)
                ve.tensor_tensor(state[:, b, :], state[:, b, :], p_misc[0:NS, 0:DI], ALU.add).then_inc(s_ready[b], 1)

            def mixed(c):
                ve.wait_ge(vn_ready, c + 1)
                ve.wait_ge(h0_copied, c + 1)
                if later(c):
                    ve.wait_ge(h1_ready, c)
                ve.tensor_tensor(hm[:], p_out[0][:, 0:NB * D].rearrange("p (b d) -> p b d", b=NB), h0[:], ALU.add)\
                    .then_inc(hm_ready, 1)

            def swiglu(c, p):
                for t in range(NF):
                    ve.wait_ge(sg_ready, c * NF + t + 1)
                    ve.scalar_tensor_tensor(sg[:, t % 2, :], sg[:, t % 2, :], 1.0, p_pair[t % 2][:, 0:NB * Q],
                                            ALU.add, ALU.mult).then_inc(gt_half, 1)
                    ve.wait_ge(gt_half, c * NF + t + 1)
                    if t == 0:
                        if later(c):
                            ve.wait_ge(mlp_done, c)
                    ve.tensor_tensor(gt[:, t, :], sg[:, t % 2, :], p_pair[t % 2][:, NB * Q:2 * NB * Q], ALU.mult)\
                        .then_inc(gt_ready, 1)
                    if p is not None:
                        if t == 1:
                            pre_norm(p)
                        if t == 2:
                            pre_apply(p)
                        if t == 4:
                            pre_split(p)

            def second_input(c):
                back_steps.start()
                ve.wait_ge(mlp_done, c + 1)
                if later(c):
                    ve.wait_ge(acc_done, c * NX)
                ve.tensor_tensor(h1[:], p_out[0][:, 0:NB * D].rearrange("p (b d) -> p b d", b=NB), hm[:], ALU.add)\
                    .then_inc(h1_ready, 1)

            def norm2_stats(c):
                ve.wait_ge(h1_ready, c + 1)
                ve.bn_stats(stat2[:, 0, :], h1[:, 0, :]).then_inc(back_v, 1)
                ve.bn_stats(stat2[:, 1, :], h1[:, 1, :]).then_inc(back_v, 1)
                back_steps.next(c)
                ve.wait_ge(back_v, back_steps.next(c))
                settle(ve)
                ve.bn_aggr(mv2[:, 0, :], stat2[:, 0, :]).then_inc(back_v, 1)
                back_steps.next(c)
                settle(ve)
                ve.bn_aggr(mv2[:, 1, :], stat2[:, 1, :]).then_inc(stat2_ready, 1)

            def norm2(c):
                second_input(c)
                norm2_stats(c)

            def norm2_apply(c):
                ve.wait_ge(r2_ready, c + 1)
                if later(c):
                    ve.wait_ge(xnt_done, c)
                for b in range(NB):
                    ins = ve.tensor_scalar(xn[:, b, :], h1[:, b, :], mv2[:, b, 0:1], r2[:, b:b + 1], ALU.subtract, ALU.mult)
                ins.then_inc(xn_ready, 1)

            def ranks(c, s, n, before, gt_, ge_, p, m):
                other = s.unsqueeze(2).to_broadcast([128, NB, n, n])
                own = s.unsqueeze(3).to_broadcast([128, NB, n, n])
                prior = before.unsqueeze(1).to_broadcast([128, NB, n, n])
                ve.tensor_tensor(ge_[:], other, own, ALU.is_ge).then_inc(back_v, 1)
                back_steps.next(c)
                if p is not None:
                    convolve_tap(p, m, 1)
                ve.wait_ge(back_v, back_steps.reached(c))
                ve.tensor_tensor(ge_[:], ge_[:], prior, ALU.mult).then_inc(back_v, 1)
                ve.tensor_tensor(gt_[:], other, own, ALU.is_gt).then_inc(back_v, 1)
                back_steps.next(c)
                back_steps.next(c)
                if p is not None:
                    convolve_tap(p, m, 2)
                ve.wait_ge(back_v, back_steps.reached(c))
                ve.tensor_tensor(gt_[:], gt_[:], ge_[:], ALU.max).then_inc(back_v, 1)
                back_steps.next(c)
                if p is not None:
                    convolve_tap(p, m, 3)
                ve.wait_ge(back_v, back_steps.reached(c))

            def route_scores(c):
                ve.wait_ge(th_ready, c + 1)
                ve.tensor_scalar(sc[:], th[:], 0.5, 0.5, ALU.mult, ALU.add).then_inc(back_v, 1)
                ve.wait_ge(back_v, back_steps.next(c))
                ve.tensor_tensor(sv[:], sc[:], gbias.unsqueeze(1).to_broadcast([128, NB, NE]), ALU.add).then_inc(back_v, 1)
                ve.wait_ge(back_v, back_steps.next(c))
                pairs = sv[:].rearrange("p b (g j) -> p b g j", j=GE)
                ve.tensor_tensor(gs[:], pairs[:, :, :, 0], pairs[:, :, :, 1], ALU.add).then_inc(back_v, 1)
                ve.wait_ge(back_v, back_steps.next(c))

            def route_groups(c, p):
                ranks(c, gs[:], NG, before4, g_gt, g_ge, p, 1)
                ve.reduce_sum(g_rank[:], g_gt[:], AX_X).then_inc(back_v, 1)
                ve.wait_ge(back_v, back_steps.next(c))
                ve.tensor_scalar(g_on[:], g_rank[:].unsqueeze(3).to_broadcast([128, NB, NG, GE]), 1.5, None,
                                 ALU.is_lt).then_inc(back_v, 1)
                back_steps.next(c)

            def route_experts(c, p):
                ranks(c, sv[:], NE, before8, e_gt, e_ge, p, 2)

            def route_weights(c):
                on = g_on[:].rearrange("p b g j -> p b (g j)")
                ve.tensor_tensor(e_gt[:], e_gt[:], on.unsqueeze(2).to_broadcast([128, NB, NE, NE]), ALU.mult).then_inc(back_v, 1)
                ve.tensor_tensor(g_sc[:], on, sc[:], ALU.mult).then_inc(back_v, 1)
                back_steps.next(c)
                back_steps.next(c)
                ve.wait_ge(back_v, back_steps.reached(c))
                ve.reduce_sum(e_rank[:], e_gt[:], AX_X).then_inc(back_v, 1)
                ve.wait_ge(back_v, back_steps.next(c))
                ve.scalar_tensor_tensor(e_w[:], e_rank[:], 1.5, g_sc[:], ALU.is_lt, ALU.mult).then_inc(back_v, 1)
                back_steps.next(c)
                ve.wait_ge(back_v, back_steps.reached(c))
                ve.reduce_sum(e_sum[:], e_w[:], AX_X).then_inc(back_v, 1)
                ve.wait_ge(back_v, back_steps.next(c))
                ve.tensor_scalar(e_sum1[:], e_sum[:], 1e-6, None, ALU.add).then_inc(back_v, 1)
                back_steps.next(c)
                ve.wait_ge(back_v, back_steps.reached(c))
                ve.reciprocal(e_inv[:], e_sum1[:]).then_inc(back_v, 1)
                ve.wait_ge(back_v, back_steps.next(c))
                ve.tensor_tensor(cw[:], e_w[:], e_inv[:].unsqueeze(2).to_broadcast([128, NB, NE]), ALU.mult)\
                    .then_inc(cw_ready, 1)
                assert back_steps.n == BACK_V, back_steps.n

            def experts(c, p):
                for e in range(NX):
                    if e == 1 and p is not None:
                        steps_dt(p)
                    ve.wait_ge(sx_ready, c * NX + e + 1)
                    ve.scalar_tensor_tensor(sg[:, e % 2, :], sg[:, e % 2, :], 1.0, p_pair[e % 2][:, 0:NB * Q],
                                            ALU.add, ALU.mult).then_inc(sx_half, 1)
                    ve.wait_ge(sx_half, c * NX + e + 1)
                    if e >= NHH:
                        ve.wait_ge(ex_done, c * NX + e - NHH + 1)
                    else:
                        if later(c):
                            ve.wait_ge(ex_done, c * NX)
                    ve.tensor_tensor(hh[:, e % NHH, :], sg[:, e % 2, :], p_pair[e % 2][:, NB * Q:2 * NB * Q], ALU.mult)\
                        .then_inc(hh_ready, 1)
                    if e == 0:
                        route_scores(c)
                        route_groups(c, p)
                    if e == 1:
                        route_experts(c, p)
                    if e == 2:
                        if p is not None:
                            gates(p, 1)
                        route_weights(c)
                    if p is not None:
                        if e == 3:
                            gates(p, 0)
                        if e == 5:
                            operands(p)
                            convolved(p)
                        if e == 7:
                            scaled_x(p, 0)
                            scaled_x(p, 1)
                        if e == 8:
                            masked_g(p)

            def split_v(b):
                split(b, v_hi_ready, v_hi_tail, p_out[1], v_h, v_l, v_lo_ready, v_lo_tail)

            def split_x(b):
                split(b, x_hi_ready, x_hi_tail, p_out[1], x_h, x_l, x_lo_ready, x_lo_tail)

            def body(p, f, b):
                def mixed_and_tokens():
                    if p is not None:
                        pre_onehot(p)
                    mixed(b)

                if f is not None:
                    scan(f, 0, {} if b is None else {3: mixed_and_tokens})
                elif b is not None:
                    mixed(b)
                if b is not None:
                    split_v(b)
                else:
                    pre_onehot(p)
                if f is not None:
                    new_state(f, 0)
                    scanned(f, 0)
                if b is not None:
                    swiglu(b, p)
                else:
                    pre_norm(p)
                    pre_apply(p)
                    if not later(p):
                        setup_first()
                    pre_split(p)
                if f is not None:
                    scan(f, 1, {} if b is None else {1: lambda: norm2(b), 3: lambda: norm2_apply(b)})
                elif b is not None:
                    second_input(b)
                    norm2_stats(b)
                    norm2_apply(b)
                if b is not None:
                    split_x(b)
                if f is not None:
                    scanned(f, 1)
                    new_state(f, 1)
                if not later(p):
                    setup_exponents(0)
                if f is not None and b is None:
                    setup_rest(0)
                if p is not None:
                    for k in range(1, KC):
                        convolve_tap(p, 0, k)
                if b is not None:
                    experts(b, p)
                elif p is not None:
                    steps_dt(p)
                    gates(p, 1)
                    gates(p, 0)
                    if f is not None:
                        setup_rest(1)
                    for m in range(1, 3):
                        for k in range(1, KC):
                            convolve_tap(p, m, k)
                    if not later(p):
                        setup_exponents(1)
                    else:
                        setup_rest(2)
                    operands(p)
                    if f is not None:
                        setup_rest(3)
                    convolved(p)
                    scaled_x(p, 0)
                    scaled_x(p, 1)
                    masked_g(p)

            setup_table()
            run(ve, body)

        @block.tensor
        def _(pe):
            def split_products(out_, cols, hi, lo, toks, weights_first):
                parts = ((w_hi[:, cols], hi[:, 0, toks]), (wt_hi[:, cols], hi[:, 1, toks]), (w_hi[:, cols], lo[:, toks]),
                         (w_lo[:, cols], hi[:, 0, toks]), (wt_lo[:, cols], hi[0:DT, 1, toks]))
                for i, (w, x) in enumerate(parts):
                    a, b = (w, x) if weights_first else (x, w)
                    ins = pe.matmul(out_, a, b, start=(i == 0), stop=(i == len(parts) - 1))
                return ins

            def transpose_channels(dst, src, done):
                for b in range(NB):
                    pe.transpose(dst[:, b * Q:(b + 1) * Q], src[:, b, 0:DH], idf[:])
                for b in range(NB):
                    ins = pe.transpose(dst[0:DT, (NB + b) * Q:(NB + b + 1) * Q], src[:, b, DH:D], idf[:])
                ins.then_inc(done, 1)

            def pre_embed(c):
                if not later(c):
                    pe.wait_ge(setup_v, 5)
                pe.wait_ge(onehot_ready, c + 1)
                if later(c):
                    pe.wait_ge(s_ready[0], c)
                settle(pe)
                for b in range(NB):
                    for k in range(3):
                        ins = pe.matmul(p_misc[:, b * D:(b + 1) * D], onehot[:, b, :], tab3[:, k, :],
                                        start=(k == 0), stop=(k == 2))
                ins.then_inc(emb_done, 1)

            def pre_turn(c):
                pe.wait_ge(un_ready, c + 1)
                transpose_channels(p_misc, un, ut_done)

            def project_in_x(c):
                if not later(c):
                    pe.wait_ge(w_in_hi, 2)
                    pe.wait_ge(w_in_lo, 2)
                pe.wait_ge(u_hi_ready, c + 1)
                pe.wait_ge(u_hi_tail, c + 1)
                pe.wait_ge(u_lo_ready, c + 1)
                pe.wait_ge(u_lo_tail, c + 1)
                if later(c):
                    pe.wait_ge(e_ready, c * NR)
                settle(pe)
                for i in range(2):
                    for j in range(2):
                        col = COL_X + (2 * i + j) * 128
                        ins = split_products(p_d[i][:, j * NB * Q:(j + 1) * NB * Q], slice(col, col + 128),
                                             u_h, u_l, slice(0, NB * Q), True)
                    ins.then_inc(x_done[i], 1)

            def project_in_z(c):
                if later(c):
                    pe.wait_ge(y_sum[1], c)
                    pe.wait_ge(s_ready[1], c)
                settle(pe)
                for k in (2, 0, 1):
                    ins = split_products((p_y, p_misc)[k // 2][:, k % 2 * NB * Q:(k % 2 + 1) * NB * Q],
                                         slice(k * 128, (k + 1) * 128), u_h, u_l, slice(0, NB * Q), True)
                    if k == 2:
                        for b in range(NB):
                            ins = split_products(p_misc[:, 256 + b * NH:256 + (b + 1) * NH], slice(DI, ZD), u_h, u_l,
                                                 slice(b * Q, (b + 1) * Q), False)
                        ins.then_inc(z_done[1], 1)
                ins.then_inc(z_done[0], 1)

            def scan_operands(c):
                pe.wait_ge(xs_ready, c + 1)
                pe.wait_ge(b_ready, c + 1)
                pe.wait_ge(c_ready, c + 1)
                pe.wait_ge(zs_ready[0], c + 1)
                pe.wait_ge(xr_ready[0], c + 1)
                pe.wait_ge(xr_ready[1], c + 1)
                settle(pe)
                for b in range(NB):
                    for m in range(KT):
                        ins = pe.transpose(p_d[b][:, m * 128:(m + 1) * 128], xs[:, m, b, :], idf[:])
                    ins.then_inc(xt_done[b], 1)
                for b in range(NB):
                    pe.matmul(p_y[:, b * Q:(b + 1) * Q], bc[:, b, :], cc[:, b, :], start=True, stop=True)
                for b in range(NB):
                    ins = pe.transpose(p_y[:, 256 + b * NS:256 + (b + 1) * NS], bc[:, b, :], idf[0:NS, 0:NS])
                ins.then_inc(g_done, 1)

            def running_sums(c):
                if not later(c):
                    pe.wait_ge(setup_v, 11)
                    pe.wait_ge(setup_p, 5)
                pe.wait_ge(pab_ready, c + 1)
                pe.wait_ge(zs_ready[1], c + 1)
                settle(pe)
                for b in range(NB):
                    for i, part in enumerate((pa, pb)):
                        pe.matmul(p_misc[0:64, b * Q:(b + 1) * Q], part[:, b].rearrange("p f r -> p (f r)"), upper16[:],
                                  start=(i == 0), stop=(i == 1))
                o = p_misc[0:NS, 256:256 + NB * NH]
                pe.matmul(o, ones16[:], pa[:, :, :, 0:HF], start=True, stop=False)
                pe.matmul(o, ones16[:], pa[:, :, :, 16:16 + HF], start=False, stop=False)
                pe.matmul(o, ones16[:], pb[:, :, :, 16:16 + HF], start=False, stop=True).then_inc(cum_done, 1)

            def sums_on_channels(c):
                pe.wait_ge(lj_ready, c + 1)
                pe.wait_ge(xd_ready[0], c + 1)
                pe.wait_ge(xd_ready[1], c + 1)
                settle(pe)
                for k, halves in enumerate(((0,), (0, 1), (1,))):
                    for f in halves:
                        ins = pe.matmul(p_d[k // 2][:, k % 2 * NB * Q:(k % 2 + 1) * NB * Q], spread16[:, k, f, :],
                                        lj[0:64, :, f, :], start=(f == halves[0]), stop=(f == halves[-1]))
                    if k >= 1:
                        ins.then_inc(cumx_done[k - 1], 1)

            def exponents(c, r):
                b, q = divmod(r, NQ)
                f, g = divmod(q, NQ // 2)
                if r == 0 and not later(c):
                    pe.wait_ge(setup_v, SETUP_V)
                if r == 0:
                    pe.wait_ge(ri_in, c * 64 + 64)
                if r < 2:
                    pe.wait_ge(ecx_ready[r], c + 1)
                else:
                    pe.wait_ge(e_ready, c * NR + r - 1)
                pe.matmul(p_d[r % 2][:], lj[:, b, f, :], ri[:, b, f, g * HG:(g + 1) * HG, :].rearrange("p h i -> p (h i)"),
                          start=True, stop=True).then_inc(d_done, 1)

            def scan(c, b, between, p=None):
                if b == 0:
                    pe.wait_ge(eend_ready, c + 1)
                    pe.wait_ge(gm_ready, c + 1)
                    pe.wait_ge(bt_ready, c + 1)
                else:
                    pe.wait_ge(y_sum[0], c + 1)
                for q in range(NQ):
                    r = b * NQ + q
                    if r + 2 < NR:
                        exponents(c, r + 2)
                    pe.wait_ge(m_ready, c * NR + r + 1)
                    for h in range(q * HG, (q + 1) * HG):
                        row = h * HD % 128 // 32 * 32
                        k = h * HD // 128
                        ins = pe.matmul(p_y[row:row + 32, k * Q:(k + 1) * Q], xd[:, b, h, :], mr[:, r % NER, h % HG, :],
                                        start=(h % 2 == 0), stop=(h % 2 == 1))
                    ins.then_inc(yq_done, 1)
                    if q == 1:
                        state_read(c, b, p)
                    if q in between:
                        between[q]()

            def state_read(c, b, p):
                if p is not None:
                    pe.wait_ge(u_lo_ready, p + 1)
                    pe.wait_ge(u_lo_tail, p + 1)
                if b == 1:
                    pe.wait_ge(s_ready[0], c + 1)
                if later(c):
                    pe.wait_ge(s_ready[b], c)
                settle(pe)
                for k in range(KT):
                    ins = pe.matmul(p_misc[:, k * Q:(k + 1) * Q], state[:, b, k * 128:(k + 1) * 128], cc[:, b, :],
                                    start=True, stop=True)
                ins.then_inc(yi_done[b], 1)

            def state_share(c, b):
                pe.wait_ge(xw_ready, c * NR + (b + 1) * NQ)
                pe.wait_ge(t1_ready[b], c + 1)
                settle(pe)
                pe.matmul(p_misc[0:NS, 0:DI], bt[:, b, :], xw[:, b, :], start=True, stop=True).then_inc(sn_done[b], 1)

            def project_out(c):
                if not later(c):
                    pe.wait_ge(halved, 3)
                pe.wait_ge(y_ready[0], c + 1)
                pe.wait_ge(y_ready[1], c + 1)
                if later(c):
                    pe.wait_ge(weighed, c * NX - 1)
                for b in range(NB):
                    for k in range(DI // 128):
                        ins = pe.matmul(p_out[0][:, b * D:(b + 1) * D], y[:, b, k, :], wo[:, k, :],
                                        start=(k == 0), stop=(k == DI // 128 - 1))
                ins.then_inc(m_out, 1)

            def turn_v(c):
                pe.wait_ge(vn_ready, c + 1)
                if later(c):
                    pe.wait_ge(weighed, c * NX)
                transpose_channels(p_out[1], vn, vt_done)

            def swiglu(c, p):
                if not later(c):
                    pe.wait_ge(w_rest_hi, 4)
                    pe.wait_ge(w_rest_lo, 4)
                pe.wait_ge(v_hi_ready, c + 1)
                pe.wait_ge(v_hi_tail, c + 1)
                pe.wait_ge(v_lo_ready, c + 1)
                pe.wait_ge(v_lo_tail, c + 1)
                pe.wait_ge(hm_ready, c + 1)

                def down(f):
                    pe.wait_ge(gt_ready, c * NF + f + 1)
                    for b in range(NB):
                        ins = pe.matmul(p_out[0][:, b * D:(b + 1) * D], gt[:, f, b * Q:(b + 1) * Q], wd[:, f, :],
                                        start=(f == 0 and b == 0), stop=(f == NF - 1), skip_group_check=True)
                    if f == NF - 1:
                        ins.then_inc(mlp_done, 1)

                for f in range(NF):
                    if f >= 2:
                        pe.wait_ge(gt_ready, c * NF + f - 1)
                    else:
                        if later(c):
                            pe.wait_ge(hh_ready, c * NX)
                    o = p_pair[f % 2]
                    split_products(o[:, 0:NB * Q], slice(COL_G + f * 128, COL_G + (f + 1) * 128), v_h, v_l,
                                   slice(0, NB * Q), True)
                    split_products(o[:, NB * Q:2 * NB * Q], slice(COL_U + f * 128, COL_U + (f + 1) * 128), v_h, v_l,
                                   slice(0, NB * Q), True).then_inc(gu_done, 1)
                    if f == 0 and p is not None:
                        pre_embed(p)
                    if f == 4 and p is not None:
                        pre_turn(p)
                    if f >= 2:
                        down(f - 2)
                down(NF - 2)
                down(NF - 1)

            def turn_x(c):
                pe.wait_ge(xn_ready, c + 1)
                transpose_channels(p_out[1], xn, xnt_done)

            def experts(c, p):
                pe.wait_ge(x_hi_ready, c + 1)
                pe.wait_ge(x_hi_tail, c + 1)
                pe.wait_ge(x_lo_ready, c + 1)
                pe.wait_ge(x_lo_tail, c + 1)
                pe.wait_ge(h1_ready, c + 1)
                settle(pe)
                for b in range(NB):
                    ins = split_products(p_out[0][:, b * NE:(b + 1) * NE], slice(COL_R, COLS), x_h, x_l,
                                         slice(b * Q, (b + 1) * Q), False)
                ins.then_inc(router_done, 1)

                def down(e):
                    pe.wait_ge(hh_ready, c * NX + e + 1)
                    if e == 1:
                        pe.wait_ge(th_ready, c + 1)
                    if e >= 2:
                        pe.wait_ge(weighed, c * NX + e - 1)
                    for b in range(NB):
                        ins = pe.matmul(p_out[(e + 1) % 2][:, b * D:(b + 1) * D], hh[:, e % NHH, b * Q:(b + 1) * Q],
                                        w2t[:, e, :], start=True, stop=True)
                    ins.then_inc(ex_done, 1)

                for e in range(NX):
                    if e >= 2:
                        pe.wait_ge(hh_ready, c * NX + e - 1)
                    else:
                        pe.wait_ge(gt_ready, c * NF + NF - 1 + e)
                    o, col = p_pair[e % 2], COL_E + e * 2 * NI
                    split_products(o[:, 0:NB * Q], slice(col, col + NI), x_h, x_l, slice(0, NB * Q), True)
                    split_products(o[:, NB * Q:2 * NB * Q], slice(col + NI, col + 2 * NI), x_h, x_l,
                                   slice(0, NB * Q), True).then_inc(h13_done, 1)
                    if e >= 2:
                        down(e - 2)
                    if p is not None:
                        if e == 0:
                            project_in_z(p)
                        if e == 4:
                            running_sums(p)
                        if e == 7:
                            scan_operands(p)
                        if e == 8:
                            sums_on_channels(p)
                down(NX - 2)
                down(NX - 1)

            def body(p, f, b):
                if f is not None:
                    exponents(f, 0)
                    exponents(f, 1)
                if b is not None:
                    project_out(b)
                if f is not None:
                    scan(f, 0, {} if b is None else {3: lambda: turn_v(b)})
                elif b is not None:
                    turn_v(b)
                if f is not None:
                    state_share(f, 0)
                if b is not None:
                    swiglu(b, p)
                else:
                    pre_embed(p)
                    pre_turn(p)
                if f is not None:
                    scan(f, 1, {} if b is None else {3: lambda: turn_x(b)}, p)
                elif b is not None:
                    turn_x(b)
                if p is not None:
                    project_in_x(p)
                if f is not None:
                    state_share(f, 1)
                if b is not None:
                    experts(b, p)
                elif p is not None:
                    project_in_z(p)
                    running_sums(p)
                    scan_operands(p)
                    sums_on_channels(p)

            pe.wait_ge(in_first, 48)
            run(pe, body)


N_SMALL = 8
SETUP_V = 11 + 6 * NB


def kernel(x, L0_tok_color_W, L0_tok_shape_W, L0_tok_quantity_W, L0_tok_special_W, L0_attn_norm1_w,
           L0_attn_in_proj_w, L0_attn_conv_w, L0_attn_conv_b, L0_attn_dt_bias, L0_attn_A_log, L0_attn_D,
           L0_attn_out_proj_w, L0_attn_norm2_w, L0_attn_w_gate, L0_attn_w_up, L0_attn_w_down, L0_ffn_gate_weight,
           L0_ffn_gate_bias, L0_ffn_w1, L0_ffn_w2, L0_ffn_w3, L0_ffn_sw1, L0_ffn_sw2, L0_ffn_sw3):
    import numpy as np
    import concourse.bacc as bacc
    from concourse.bass_utils import run_bass_kernel_spmd

    f32 = np.float32
    rate = np.exp(-(np.arange(0, D, 2, dtype=f32) / f32(D)) * f32(np.log(10000.0)))
    angle = np.arange(L, dtype=f32)[:, None] * rate.astype(f32)
    position = np.stack([np.sin(angle), np.cos(angle)], axis=-1).reshape(L, D).astype(f32)
    head_rows = np.zeros((64, HF), f32)
    for g in range(4):
        for h in range(HF):
            head_rows[16 * g + h, h] = 1.0
    spread_rows = np.zeros((64, KT, 2, 128), f32)
    for channel in range(DI):
        half, head = divmod(channel // HD, HF)
        spread_rows[head::16, channel // 128, half, channel % 128] = 1.0
    token, pair = np.arange(Q)[None, :], np.arange(Q // 2)[:, None]
    pair_rows = np.stack([np.where(token < 2 * pair, f32(FAR), f32(0)), token // 2 == pair], axis=1).astype(f32)
    shared_rows = np.concatenate([L0_attn_dt_bias, L0_attn_A_log, L0_ffn_gate_bias,
                                  np.tril(np.ones((NE, NE), f32), -1).ravel(), np.tril(np.ones((NG, NG), f32), -1).ravel()])
    norms = np.stack([part for n in (np.asarray(L0_attn_norm1_w), np.asarray(L0_attn_norm2_w))
                      for part in (n[0:DH], np.concatenate([n[DH:D], n[DH:D]]))], axis=1)
    ids = np.arange(64)
    features = np.concatenate([L0_tok_color_W[ids // 16], L0_tok_shape_W[ids % 16 // 4], L0_tok_quantity_W[ids % 4]],
                              axis=1)
    z, xbc, dt = np.split(np.asarray(L0_attn_in_proj_w), [DI, 2 * DI + 2 * NS], axis=1)
    columns = [z, dt, xbc, L0_attn_w_gate, L0_attn_w_up, np.transpose(L0_ffn_sw1), np.transpose(L0_ffn_sw3)]
    for e in range(NE):
        columns += [np.transpose(L0_ffn_w1[e]), np.transpose(L0_ffn_w3[e])]
    columns.append(np.transpose(L0_ffn_gate_weight))
    w2 = np.concatenate([np.transpose(L0_ffn_sw2)[:, None, :], np.transpose(L0_ffn_w2, (2, 0, 1))], axis=1)
    arrays = {
        "tokens": x, "position": position, "vocab_ids": np.arange(V, dtype=f32)[:, None],
        "table": np.concatenate([features, L0_tok_special_W], axis=0),
        "weights": np.concatenate(columns, axis=1),
        "norms": norms,
        "conv_w": np.transpose(np.reshape(L0_attn_conv_w, (NM, 128, KC)), (1, 0, 2)),
        "conv_b": np.transpose(np.reshape(L0_attn_conv_b, (NM, 128))),
        "shared_rows": shared_rows,
        "d_skip": np.transpose(np.reshape(np.repeat(np.asarray(L0_attn_D), HD), (KT, 128))),
        "w_out": np.transpose(np.reshape(L0_attn_out_proj_w, (DI // 128, 128, D)), (1, 0, 2)),
        "w_down": np.transpose(np.reshape(L0_attn_w_down, (NF, 128, D)), (1, 0, 2)),
        "w2": w2,
        "identity": np.eye(128, dtype=f32), "lower_ones": np.triu(np.ones((128, 128), f32)),
        "head_rows": head_rows, "pair_rows": pair_rows, "spread_rows": spread_rows,
    }
    nc = bacc.Bacc("TRN2", target_bir_lowering=False, num_devices=1)
    args = []
    for name, a in arrays.items():
        arrays[name] = a = np.ascontiguousarray(a)
        args.append(nc.dram_tensor(name, a.shape, mybir.dt.from_np(a.dtype), kind="ExternalInput").ap())
    args.append(nc.dram_tensor("out", (NB, L, D), F32, kind="ExternalOutput").ap())
    program(nc, *args)
    r = run_bass_kernel_spmd(nc, [arrays], core_ids=[0])
    return r.results[0]["out"]
```
